# Optimizing a Trainium2 kernel written in Bass

```python
import numpy as np
import jax
import jax.numpy as jnp

def _softmax(x, axis=-1):
    return jax.nn.softmax(x, axis=axis)

def _gelu(x):
    return jax.nn.gelu(x, approximate=True)

def _silu(x):
    return jax.nn.silu(x)

def _sigmoid(x):
    return jax.nn.sigmoid(x)

def _layernorm(x, axis=-1, eps=1e-05):
    m = jnp.mean(x, axis=axis, keepdims=True)
    v = jnp.var(x, axis=axis, keepdims=True)
    return (x - m) / jnp.sqrt(v + eps)

def _scatter_add(tgt, idx, src, axis=0):
    return tgt.at[idx].add(src)

def _segment_sum(src, seg, n):
    return jax.ops.segment_sum(src, seg, n)
kernel_name = 'mk_adaln_d1_jaxref_r4_916952'

def setup_inputs(seed: int=0):
    np.random.seed(seed)
    _w = jnp.asarray

    def _L0_attn_setup():
        import jax, jax.numpy as jnp
        import numpy as np
        B, N, D, F = (4, 1024, 256, 64)
        LN_EPS = 1e-05
        ATTN_EPS = 1e-06

        def _layer_norm(x, w, b):
            mu = jnp.mean(x, axis=-1, keepdims=True)
            var = jnp.var(x, axis=-1, keepdims=True)
            return (x - mu) * jax.lax.rsqrt(var + LN_EPS) * w + b

        def _linear(x, w, b):
            return jnp.einsum('bnd,fd->bnf', x, w) + b

        def _causal_linear_attn(Q, K, V, eps=ATTN_EPS):
            b, n, f = K.shape
            d = V.shape[-1]
            Qt = jnp.swapaxes(Q, 0, 1)
            Kt = jnp.swapaxes(K, 0, 1)
            Vt = jnp.swapaxes(V, 0, 1)

            def step(carry, qkv):
                KV, Ks = carry
                q, k, v = qkv
                KV = KV + k[:, :, None] * v[:, None, :]
                Ks = Ks + k
                num = jnp.einsum('bf,bfd->bd', q, KV)
                den = jnp.sum(q * Ks, axis=-1, keepdims=True) + eps
                return ((KV, Ks), num / den)
            init = (jnp.zeros((b, f, d), Q.dtype), jnp.zeros((b, f), Q.dtype))
            _, out = jax.lax.scan(step, init, (Qt, Kt, Vt))
            return jnp.swapaxes(out, 0, 1)
        key = jax.random.key(seed)
        ks = jax.random.split(key, 9)
        s = 0.02
        return {'x': jax.random.normal(ks[0], (B, N, D), dtype=jnp.float32), 'ln1_w': jnp.ones((D,), jnp.float32), 'ln1_b': jnp.zeros((D,), jnp.float32), 'q_w': jax.random.normal(ks[1], (F, D), jnp.float32) * s, 'q_b': jnp.zeros((F,), jnp.float32), 'k_w': jax.random.normal(ks[2], (F, D), jnp.float32) * s, 'k_b': jnp.zeros((F,), jnp.float32), 'v_w': jax.random.normal(ks[3], (D, D), jnp.float32) * s, 'v_b': jnp.zeros((D,), jnp.float32), 'o_w': jax.random.normal(ks[4], (D, D), jnp.float32) * s, 'o_b': jnp.zeros((D,), jnp.float32), 'ln2_w': jnp.ones((D,), jnp.float32), 'ln2_b': jnp.zeros((D,), jnp.float32), 'f1_w': jax.random.normal(ks[5], (4 * D, D), jnp.float32) * s, 'f1_b': jnp.zeros((4 * D,), jnp.float32), 'f2_w': jax.random.normal(ks[6], (D, 4 * D), jnp.float32) * s, 'f2_b': jnp.zeros((D,), jnp.float32)}
    _L0_attn_in = _L0_attn_setup()

    def _L0_ffn_setup():
        import jax, jax.numpy as jnp
        import numpy as np
        D_MODEL = 256
        NUM_EXPERTS = 8
        HIDDEN = 1024
        TOP_K = 2
        key = jax.random.key(seed)
        ks = jax.random.split(key, 6)
        x = jax.random.normal(ks[0], (2, 256, D_MODEL), dtype=jnp.float32)
        gate_w = jax.random.normal(ks[1], (NUM_EXPERTS, D_MODEL), dtype=jnp.float32) * (1.0 / np.sqrt(D_MODEL))
        w1 = jax.random.normal(ks[2], (NUM_EXPERTS, HIDDEN, D_MODEL), dtype=jnp.float32) * (1.0 / np.sqrt(D_MODEL))
        b1 = jax.random.normal(ks[3], (NUM_EXPERTS, HIDDEN), dtype=jnp.float32) * 0.01
        w2 = jax.random.normal(ks[4], (NUM_EXPERTS, D_MODEL, HIDDEN), dtype=jnp.float32) * (1.0 / np.sqrt(HIDDEN))
        b2 = jax.random.normal(ks[5], (NUM_EXPERTS, D_MODEL), dtype=jnp.float32) * 0.01
        return {'x': x, 'gate_w': gate_w, 'w1': w1, 'b1': b1, 'w2': w2, 'b2': b2}
    _L0_ffn_in = _L0_ffn_setup()
    _L0_c = _w((lambda *s: np.random.randn(*s).astype(np.float32) * 0.05)(2, 256))
    _L0_wmod = _w((lambda *s: np.random.randn(*s).astype(np.float32) * 0.05)(256, 6 * 256) * 256 ** (-0.5))
    _d = {'L0_attn_x': _L0_attn_in['x'], 'L0_attn_ln1_w': _L0_attn_in['ln1_w'], 'L0_attn_ln1_b': _L0_attn_in['ln1_b'], 'L0_attn_q_w': _L0_attn_in['q_w'], 'L0_attn_q_b': _L0_attn_in['q_b'], 'L0_attn_k_w': _L0_attn_in['k_w'], 'L0_attn_k_b': _L0_attn_in['k_b'], 'L0_attn_v_w': _L0_attn_in['v_w'], 'L0_attn_v_b': _L0_attn_in['v_b'], 'L0_attn_o_w': _L0_attn_in['o_w'], 'L0_attn_o_b': _L0_attn_in['o_b'], 'L0_attn_ln2_w': _L0_attn_in['ln2_w'], 'L0_attn_ln2_b': _L0_attn_in['ln2_b'], 'L0_attn_f1_w': _L0_attn_in['f1_w'], 'L0_attn_f1_b': _L0_attn_in['f1_b'], 'L0_attn_f2_w': _L0_attn_in['f2_w'], 'L0_attn_f2_b': _L0_attn_in['f2_b'], 'L0_ffn_gate_w': _L0_ffn_in['gate_w'], 'L0_ffn_w1': _L0_ffn_in['w1'], 'L0_ffn_b1': _L0_ffn_in['b1'], 'L0_ffn_w2': _L0_ffn_in['w2'], 'L0_ffn_b2': _L0_ffn_in['b2'], 'L0_c': _L0_c, 'L0_wmod': _L0_wmod}
    _x0 = _d['L0_attn_x']
    _d['L0_attn_x'] = jax.random.normal(jax.random.fold_in(jax.random.key(seed), 1), (2, 2048, 256), dtype=_x0.dtype)
    del _x0
    return _d

def reference(L0_attn_x, L0_attn_ln1_w, L0_attn_ln1_b, L0_attn_q_w, L0_attn_q_b, L0_attn_k_w, L0_attn_k_b, L0_attn_v_w, L0_attn_v_b, L0_attn_o_w, L0_attn_o_b, L0_attn_ln2_w, L0_attn_ln2_b, L0_attn_f1_w, L0_attn_f1_b, L0_attn_f2_w, L0_attn_f2_b, L0_ffn_gate_w, L0_ffn_w1, L0_ffn_b1, L0_ffn_w2, L0_ffn_b2, L0_c, L0_wmod):

    def _L0_attn_ref(x, ln1_w, ln1_b, q_w, q_b, k_w, k_b, v_w, v_b, o_w, o_b, ln2_w, ln2_b, f1_w, f1_b, f2_w, f2_b):
        import jax, jax.numpy as jnp
        import numpy as np
        B, N, D, F = (4, 1024, 256, 64)
        LN_EPS = 1e-05
        ATTN_EPS = 1e-06

        def _layer_norm(x, w, b):
            mu = jnp.mean(x, axis=-1, keepdims=True)
            var = jnp.var(x, axis=-1, keepdims=True)
            return (x - mu) * jax.lax.rsqrt(var + LN_EPS) * w + b

        def _linear(x, w, b):
            return jnp.einsum('bnd,fd->bnf', x, w) + b

        def _causal_linear_attn(Q, K, V, eps=ATTN_EPS):
            b, n, f = K.shape
            d = V.shape[-1]
            Qt = jnp.swapaxes(Q, 0, 1)
            Kt = jnp.swapaxes(K, 0, 1)
            Vt = jnp.swapaxes(V, 0, 1)

            def step(carry, qkv):
                KV, Ks = carry
                q, k, v = qkv
                KV = KV + k[:, :, None] * v[:, None, :]
                Ks = Ks + k
                num = jnp.einsum('bf,bfd->bd', q, KV)
                den = jnp.sum(q * Ks, axis=-1, keepdims=True) + eps
                return ((KV, Ks), num / den)
            init = (jnp.zeros((b, f, d), Q.dtype), jnp.zeros((b, f), Q.dtype))
            _, out = jax.lax.scan(step, init, (Qt, Kt, Vt))
            return jnp.swapaxes(out, 0, 1)
        x_norm = _layer_norm(x, ln1_w, ln1_b)
        Q = jax.nn.elu(_linear(x_norm, q_w, q_b)) + 1.0
        K = jax.nn.elu(_linear(x_norm, k_w, k_b)) + 1.0
        V = _linear(x_norm, v_w, v_b)
        attn = _causal_linear_attn(Q, K, V)
        attn = _linear(attn, o_w, o_b)
        x = x + attn
        h = _layer_norm(x, ln2_w, ln2_b)
        h = jax.nn.gelu(_linear(h, f1_w, f1_b), approximate=False)
        x = x + _linear(h, f2_w, f2_b)
        return x

    def _L0_ffn_ref(x, gate_w, w1, b1, w2, b2):
        import jax, jax.numpy as jnp
        import numpy as np
        D_MODEL = 256
        NUM_EXPERTS = 8
        HIDDEN = 1024
        TOP_K = 2
        B, S, D = x.shape
        xf = x.reshape(-1, D)
        T = xf.shape[0]
        gate_logits = xf @ gate_w.T
        gate_probs = jax.nn.softmax(gate_logits, axis=-1)
        topk_scores, topk_idx = jax.lax.top_k(gate_probs, TOP_K)
        topk_scores = topk_scores / jnp.sum(topk_scores, axis=-1, keepdims=True)
        combine = jnp.zeros((T, NUM_EXPERTS), dtype=x.dtype)
        combine = combine.at[jnp.arange(T)[:, None], topk_idx].set(topk_scores)
        h = jax.nn.relu(jnp.einsum('td,ehd->teh', xf, w1) + b1)
        expert_out = jnp.einsum('teh,edh->ted', h, w2) + b2
        out = jnp.einsum('ted,te->td', expert_out, combine)
        return out.reshape(B, S, D)
    x = L0_attn_x
    mod = (_silu(L0_c) @ L0_wmod).reshape(L0_c.shape[0], 6, 1, -1)
    sa, ca, ga, sb, cb, gb = (mod[:, 0], mod[:, 1], mod[:, 2], mod[:, 3], mod[:, 4], mod[:, 5])
    ga = (2 * (ga >= 0) - 1) * jnp.maximum(jnp.abs(ga), 0.25)
    gb = (2 * (gb >= 0) - 1) * jnp.maximum(jnp.abs(gb), 0.25)
    h = _layernorm(x, axis=-1) * (1 + ca) + sa
    x = x + ga * _L0_attn_ref(h, L0_attn_ln1_w, L0_attn_ln1_b, L0_attn_q_w, L0_attn_q_b, L0_attn_k_w, L0_attn_k_b, L0_attn_v_w, L0_attn_v_b, L0_attn_o_w, L0_attn_o_b, L0_attn_ln2_w, L0_attn_ln2_b, L0_attn_f1_w, L0_attn_f1_b, L0_attn_f2_w, L0_attn_f2_b)
    h = _layernorm(x, axis=-1) * (1 + cb) + sb
    x = x + gb * _L0_ffn_ref(h, L0_ffn_gate_w, L0_ffn_w1, L0_ffn_b1, L0_ffn_w2, L0_ffn_b2)
    return x

_drawn_inputs = setup_inputs


def setup_inputs(seed=0):
    import zlib

    import numpy as np

    out = dict(_drawn_inputs(seed))
    spreads = {'L0_attn_ln1_w': (1.0, 0.6),
     'L0_attn_ln1_b': (0.0, 0.8),
     'L0_attn_q_b': (0.0, 2.0),
     'L0_attn_k_b': (0.0, 2.0),
     'L0_attn_v_b': (0.0, 0.748),
     'L0_attn_o_b': (0.0, 0.275),
     'L0_attn_ln2_w': (1.0, 0.6),
     'L0_attn_ln2_b': (0.0, 2.0),
     'L0_attn_f1_b': (0.0, 0.607),
     'L0_attn_f2_b': (0.0, 0.283)}
    factors = {'L0_attn_q_w': 8.0,
     'L0_attn_k_w': 8.0,
     'L0_attn_v_w': 8.0,
     'L0_attn_o_w': 5.412,
     'L0_ffn_b1': 59.262,
     'L0_ffn_b2': 38.787}
    for name, (base, spread) in spreads.items():
        noise = np.random.default_rng([zlib.crc32(name.encode()), seed]).standard_normal(out[name].shape)
        drawn = base * np.exp(spread * noise) if base else spread * noise
        out[name] = jnp.asarray(drawn.astype(out[name].dtype))
    for name, factor in factors.items():
        out[name] = (out[name] * factor).astype(out[name].dtype)
    return out
```

```python
from contextlib import ExitStack

import numpy as np

import concourse.bass as bass
from concourse import mybir

F32 = mybir.dt.float32
F32R = mybir.dt.float32r
BF16 = mybir.dt.bfloat16
I32 = mybir.dt.int32
U32 = mybir.dt.uint32
ALU = mybir.AluOpType
ACT = mybir.ActivationFunctionType
AX_X = mybir.AxisListType.X

P = 128
LN_EPS = 1e-5
ATTN_EPS = 1e-6
DVE_ROUND = 69
POOL_ROUND = 7


def adaln_moe_program(nc, x, c, wmod, wqk, qk_b, ln1_w, ln1_b, v_w, v_b, o_w, o_b, ln2_w, ln2_b,
                      f1, f1_b, f2, f2_b, gate, w1, b1, w2, b2, out):
    B, N, D = x.shape
    KD = D // P
    H = f1.shape[-1]
    MH = H // P
    E = w1.shape[0]
    T = B * N
    TT = 2
    NT = B * TT
    GB = TT * P
    GW = NT * P
    NG = N // GB
    NF = wqk.shape[-1] // 2
    DV = D + 2
    META = D
    ROW = D + 8
    TR = 2 * P
    CAP = T + TR
    assert B == 2 and KD == 2 and MH == 8 and E == 8 and 2 * NF == P and NG >= 4

    slots = nc.dram_tensor("slots", (E * CAP, ROW), F32, kind="Internal").ap()

    with ExitStack() as ctx:
        def sb(name, shape, dt=F32):
            return ctx.enter_context(nc.sbuf_tensor(name, shape, dt))

        at = {}

        def sb_marked(name, shape, dt=F32):
            t = sb(name, shape, dt)
            at[name] = nc.sbuf_base - int(np.prod(shape[1:])) * 4
            return t

        def sb_over(name, shape, under, off=0):
            return nc.alloc_sbuf_tensor_at(name, shape, F32, offset=at[under] + off)

        def bank(name):
            return ctx.enter_context(nc.psum_tensor(name, [P, 512], F32))

        def sem(name):
            return ctx.enter_context(nc.semaphore(name))

        wqk_hi, wqk_lo = (sb(f"wqk_{s}", [P, KD, 2 * NF], F32R) for s in ("hi", "lo"))
        wvo_hi, wvo_lo = (sb(f"wvo_{s}", [P, KD, D], F32R) for s in ("hi", "lo"))
        up_hi = [sb(f"up_hi{s}", [P, KD, H], F32R) for s in (0, 1)]
        up_lo = [sb_marked(f"up_lo{s}", [P, KD, H], F32R) for s in (0, 1)]
        down_hi = [sb(f"down_hi{s}", [P, MH, D], F32R) for s in (0, 1)]
        down_lo = [sb_marked(f"down_lo{s}", [P, MH, D], F32R) for s in (0, 1)]
        FFN = 1
        raw_up = sb("raw_up", [P, KD, H])
        raw_down = sb("raw_down", [P, MH, D])
        gate_sb = sb("gate_sb", [P, KD, E])

        mod = sb("mod", [P, B, 6, D])
        SA, CA, GA, SB_, CB, GATE_B = range(6)
        b2_all = mod[:, :, 0:4, :]
        ob_bc = sb("ob_bc", [P, D])
        f2b_bc = sb("f2b_bc", [P, D])
        bvo_bc = sb("bvo_bc", [P, D])
        gb_bc = sb("gb_bc", [P, 2, D])

        vec = sb("vec", [P, 16])
        LN1W, LN1B, LN2W, LN2B, VB = (slice(KD * n, KD * n + KD) for n in range(5))
        qkb = sb("qkb", [P, 2])
        f1b = sb("f1b", [P, MH])
        b1_all = sb("b1_all", [P, E, MH])
        b1_cur = sb("b1_cur", [P, MH])
        b2_cur = sb("b2_cur", [P, D])

        ones = sb("ones", [P, P])
        ident = sb("ident", [P, P])
        causal = sb("causal", [P, 3 * P])
        below = sb("below", [P, P], BF16)
        ones_bf = sb("ones_bf", [P, P], BF16)
        expert_id = sb("expert_id", [P, E])
        slot_base = sb("slot_base", [P, E])
        neg_half = sb("neg_half", [P, NT])

        xa = sb("xa", [P, NT, D])
        hob = sb("hob", [P, NT, D])
        xn1 = sb("xn1", [P, NT, D])
        xt1_hi, xt1_lo = (sb(f"xt1_{s}", [P, KD, GW], F32R) for s in ("hi", "lo"))
        xt2_hi = sb_marked("xt2_hi", [P, KD, GW], F32R)
        xt2_lo = sb("xt2_lo", [P, KD, GW], F32R)
        h3t = raw_up[:, 0, :].rearrange("p (k n) -> p k n", k=KD)
        probs = raw_up[:, 1, 0:2 * 384].rearrange("p (b n) -> p b n", b=B)
        elu = sb("elu", [P, GW])
        qk = sb("qk", [P, GW])
        kz = sb("kz", [P, GW])
        kt = sb("kt", [P, NT, P])
        val = sb("val", [P, NT, DV])
        state = sb("state", [P, B, DV])
        h2 = sb("h2", [P, NT, D])
        xn2 = sb("xn2", [P, NT, D])
        res = sb("res", [P, NT, D])
        x2 = sb("x2", [P, NT, D])
        h3 = sb("h3", [P, NT, ROW])
        act_hi = sb_marked("act_hi", [P, MH, GW], F32R)
        act_lo = sb_marked("act_lo", [P, MH, GW], F32R)
        RING = 4
        gelu_ring = raw_down[:, :, :].rearrange("p (r m) d -> p r (m d)", r=RING)
        stats = sb("stats", [P, NT, 6])
        mv = [sb(f"mv{n}", [P, NT, 2]) for n in range(4)]
        neg_mean = [None] + [sb(f"neg_mean{n}", [P, NT]) for n in (1, 2)]
        shift = [None] + [sb(f"shift{n}", [P, NT]) for n in (1, 2)]
        ve = [sb(f"ve{n}", [P, NT]) for n in range(4)]
        rstd = [sb(f"rstd{n}", [P, NT]) for n in range(4)]
        rden = sb("rden", [P, NT])
        logits = sb("logits", [P, NT, E])
        top = sb("top", [P, NT, 8])
        top_at = sb("top_at", [P, NT, 8], U32)
        gap = sb("gap", [P, NT])
        e2 = sb("e2", [P, NT])
        e2p1 = sb("e2p1", [P, NT])
        chosen = sb("chosen", [P, 2, NT, E])
        picked = sb("picked", [P, NT, E], BF16)
        totals = sb("totals", [P, NT, E])
        place = sb("place", [P, NT, E])
        place2 = sb("place2", [P, 2, NT, E])
        pos = sb("pos", [P, 2 * NT])
        pos_u = sb("pos_u", [P, 2 * NT], U32)
        next_slot = sb("next_slot", [P, E])
        token = sb("token", [P, NT])
        cnt_f = sb("cnt_f", [P, 3, E])
        cnt_i = sb("cnt_i", [P, 3, E], I32)
        table = sb("table", [P, 3, E], I32)

        rows = hob[:, :, :].rearrange("p t d -> p (t d)")[:, 0:2 * ROW].rearrange("p (t r) -> p t r", t=2)
        pad_rows = sb("pad_rows", [P, 2, ROW])
        skip_u = sb("skip_u", [P, 1], U32)
        meta = sb("meta", [P, 2, 8])
        cur_e = sb("cur_e", [P, 1])
        is_e = sb("is_e", [P, 2, 2])
        w_two = sb("w_two", [P, 2, 2])
        w_row = sb("w_row", [P, 2])
        tok_u = sb("tok_u", [P, 2], U32)
        g_row = xn2[:, 0:2, :]
        y = xn1[:, 0:2, :]
        r_ring = h2[:, :, :].rearrange("p t d -> p (t d)").rearrange("p (r n) -> p r n", n=TR)
        r_hi = act_hi[:, :, 0:TR]
        r_lo = act_lo[:, :, 0:TR]
        rt_hi = xt1_hi[:, :, 0:TR]
        rt_lo = xt1_lo[:, :, 0:TR]

        wmod_raw = sb_over("wmod_raw", [P, KD, 6 * D], "act_lo")
        first_up = sb_over("first_up", [P, KD, H], "up_lo0")
        first_down = sb_over("first_down", [P, MH, D], "down_lo0")
        v_raw = x2[:, 0:2, :]
        o_raw = x2[:, 2:4, :]
        wqk_raw = res[:, 0, :].rearrange("p (k n) -> p k n", k=KD)
        wvo_raw = hob[:, 0:2, :]
        rep = sb_over("rep", [P, 8, P], "xt2_hi")
        cvec = sb("cvec", [P, KD, B])
        csig = sb("csig", [P, KD, B])

        TP = [bank("tp0"), bank("tp1")]
        AT = [bank("at0"), bank("at1"), bank("at2")]
        FF = [bank("ff0"), bank("ff1")]
        YP = bank("yp")
        down_bank = [FF[0], FF[1], YP, AT[0]]
        carry_bank = [TP[1], YP]
        up_bank = [FF[0], FF[1], AT[0], AT[1]]
        y_bank = [YP, AT[2]]

        s = {}

        def S(name):
            if name not in s:
                s[name] = sem(name)
            return s[name]

        for name in """ld_mod ld_vec ld_attn ld_ffn ld_first ld_rows consts mod_w mod_c silu_e silu_rep mod_mm mod_ready
                prep_vec wvo_mm wvo_raw_ready wprep ffn_bias ffn_bias_mm bias_ready first_hi first_set pool_step dve_step
                x_loaded xr_loaded x2_stored scattered
                t1_done t2_done t3_done qk_done v_done kt_done s_done av_done kv_done ff1_done ff2_done
                gate_done rank_done t1_hi t2_hi t3_copied elu_exp gate_exp gelu_done kt_copied
                t1_lo t2_lo ve_ready rstd_ready xa_normed h_ready hob_ready xn1_ready elu_min qk_ready
                v_ready act_split gap_ready picked_ready pos_ready weights_ready masked h2_ready state_ready xn2_ready
                ff2_read x2_ready h3_ready res_ready phase1_over
                table_ready padded rows_loaded up_loaded down_loaded up_hi_ready up_ready down_hi_ready down_ready rt_done l1_done l2_done relu_done rt_hi_done
                r_split rt_lo_done meta_read y_ready summed b2_loaded gb_ready pads_ready act_step
                passed ve1_ready ve2_ready ve3_ready rs1_ready rs2_ready rs3_ready shift1_ready shift2_ready""".split():
            S(name)

        NORM_A, NORM_1, NORM_2, NORM_B = range(4)
        VE = ["ve_ready", "ve1_ready", "ve2_ready", "ve3_ready"]
        RS = ["rstd_ready", "rs1_ready", "rs2_ready", "rs3_ready"]
        SHIFTED = [None, "shift1_ready", "shift2_ready"]
        NORMED = [None, "xn1_ready", "xn2_ready"]

        def alone(eng):
            eng.sem_inc(s["passed"], 1)

        def group_of(src, b, g):
            return src.rearrange("b (g t p) d -> b g p t d", t=TT, p=P)[b, g]

        def bc(ap, shape):
            return ap.broadcast_to(shape)

        def flat(ap):
            return ap

        block = ctx.enter_context(nc.Block())

        @block.sync
        def _(sp):
            sp.dma_start(cvec[:], c).then_inc(s["ld_mod"], 16)
            sp.dma_start(wmod_raw[:], wmod.rearrange("(k p) n -> p k n", p=P)).then_inc(s["ld_mod"], 16)
            for b in range(B):
                sp.dma_start(xa[:, TT * b:TT * b + TT, :], group_of(x, b, 0)).then_inc(s["x_loaded"], 16)
            for k, v in ((LN1W, ln1_w), (LN1B, ln1_b), (LN2W, ln2_w), (LN2B, ln2_b), (VB, v_b)):
                sp.dma_start(vec[:, k], v).then_inc(s["ld_vec"], 16)
            sp.dma_start(wqk_raw, wqk.rearrange("(k p) n -> p k n", p=P)).then_inc(s["ld_attn"], 16)
            sp.dma_start(v_raw, v_w.rearrange("(k p) n -> p k n", p=P)).then_inc(s["ld_attn"], 16)
            sp.dma_start(o_raw, o_w.rearrange("(k p) n -> p k n", p=P)).then_inc(s["ld_attn"], 16)
            sp.dma_start(qkb[:, 0:1], qk_b).then_inc(s["ld_attn"], 16)
            sp.dma_start(ob_bc[:], o_b.partition_broadcast(P)).then_inc(s["ld_attn"], 16)
            sp.dma_start(raw_up[:], f1.rearrange("(k p) n -> p k n", p=P)).then_inc(s["ld_ffn"], 16)
            sp.dma_start(f1b[:], f1_b).then_inc(s["ld_ffn"], 16)
            sp.dma_start(raw_down[:], f2.rearrange("(m p) n -> p m n", p=P)).then_inc(s["ld_ffn"], 16)
            sp.dma_start(f2b_bc[:], f2_b.partition_broadcast(P)).then_inc(s["ld_ffn"], 16)
            sp.dma_start(gate_sb[:], gate.rearrange("(k p) n -> p k n", p=P)).then_inc(s["ld_ffn"], 16)
            sp.dma_start(b1_all[:], b1).then_inc(s["ld_ffn"], 16)
            sp.dma_start(first_up[:], w1[0].rearrange("(k p) n -> p k n", p=P)).then_inc(s["ld_first"], 16)
            sp.dma_start(first_down[:], w2[0].rearrange("(m p) n -> p m n", p=P)).then_inc(s["ld_first"], 16)

            def load_x(n):
                sp.wait_ge(s["xn1_ready"], n)
                sp.wait_ge(s["hob_ready"], n)
                for b in range(B):
                    sp.dma_start(xa[:, TT * b:TT * b + TT, :], group_of(x, b, n)).then_inc(s["x_loaded"], 16)

            def load_residual(a):
                sp.wait_ge(s["x2_ready"], a)
                for b in range(B):
                    sp.dma_start(res[:, TT * b:TT * b + TT, :], group_of(x, b, a)).then_inc(s["xr_loaded"], 16)

            def store_x2(f):
                sp.wait_ge(s["x2_ready"], f + 1)
                for b in range(B):
                    sp.dma_start(group_of(out, b, f), x2[:, TT * b:TT * b + TT, :]).then_inc(s["x2_stored"], 16)

            load_x(1)
            sp.wait_ge(s["wprep"], 4)
            load_residual(0)
            load_x(2)
            store_x2(0)
            load_residual(1)
            with sp.Fori(2, NG - 1) as i:
                load_x(i + 1)
                store_x2(i - 1)
                load_residual(i)
            store_x2(NG - 2)
            load_residual(NG - 1)
            store_x2(NG - 1)

            sp.wait_ge(s["table_ready"], 1)
            sp.wait_ge(s["pads_ready"], 3)
            for e in range(E):
                n = sp.value_load(table[0:1, 0, e:e + 1], min_val=0, max_val=T)
                sp.dma_start(slots[bass.ds(n + e * CAP, TR), :].rearrange("(s p) r -> p s r", p=P),
                             pad_rows[:]).then_inc(s["padded"], 16)
            sp.wait_ge(s["phase1_over"], 5)
            for e in range(E):
                sp.dma_start(b2_all[:, e // 4, e % 4, :], b2[e].partition_broadcast(P)).then_inc(s["b2_loaded"], 16)
            sp.wait_ge(s["padded"], 16 * E)
            sp.wait_ge(s["scattered"], 16 * 2 * NT * NG)
            sp.wait_ge(s["x2_stored"], 16 * B * NG)
            with sp.Fori(0, E) as e:
                tiles = sp.value_load(table[0:1, 1, bass.ds(e, 1)], min_val=1, max_val=T // TR)
                first = sp.value_load(table[0:1, 2, bass.ds(e, 1)], min_val=1, max_val=2 * T // TR + E)
                with sp.Fori(0, tiles) as i:
                    sp.wait_ge(s["rt_done"], first + i)
                    sp.wait_ge(s["meta_read"], first + i)
                    sp.dma_start(rows, slots[bass.ds(e * CAP + i * TR, TR), :].rearrange("(s p) r -> p s r", p=P)) \
                        .then_inc(s["rows_loaded"], 16)
            tiles = sp.value_load(table[0:1, 1, E - 1:E], min_val=1, max_val=T // TR)
            first = sp.value_load(table[0:1, 2, E - 1:E], min_val=1, max_val=2 * T // TR + E)
            sp.wait_ge(s["rt_done"], first + tiles)
            sp.wait_ge(s["meta_read"], first + tiles)
            sp.dma_start(rows, slots[0:TR, :].rearrange("(s p) r -> p s r", p=P)).then_inc(s["rows_loaded"], 16)
            sp.wait_ge(s["summed"], (first + tiles) * 32)
            sp.wait_ge(s["rows_loaded"], (first + tiles) * 16 + 16)
            alone(sp)

        @block.tensor
        def _(pe):
            def product(dst, lhs, rhs, chunks):
                last = None
                for k in range(chunks):
                    lh, ll = lhs(k)
                    rh, rl = rhs(k)
                    pe.matmul(dst, lh, rh, start=(k == 0), stop=False)
                    pe.matmul(dst, lh, rl, start=False, stop=False)
                    last = pe.matmul(dst, ll, rh, start=False, stop=(k == chunks - 1))
                return last

            for name, per_tile in (("rt_done", 1), ("l1_done", MH), ("l2_done", 2)):
                pe.sem_inc(s[name], per_tile)
            pe.wait_ge(s["ld_mod"], 32)
            pe.wait_ge(s["silu_rep"], KD * B)
            where = [TP[0], TP[1], AT[0], AT[1], AT[2], FF[0]]
            for n in range(3):
                for b in range(B):
                    for k in range(KD):
                        last = pe.matmul(where[2 * n + b][:], rep[:, B * k + b, :], wmod_raw[:, k, 512 * n:512 * n + 512],
                                         start=(k == 0), stop=(k == KD - 1))
                    last.then_inc(s["mod_mm"], 1)
            pe.wait_ge(s["ld_attn"], 16 * 5)
            for k in range(KD):
                for n in range(KD):
                    last = pe.matmul(FF[1][:, D * k:D * k + D], v_raw[:, n, P * k:P * k + P], o_raw[:, n, :],
                                     start=(n == 0), stop=(n == KD - 1))
            last.then_inc(s["wvo_mm"], 1)
            pe.wait_ge(s["ld_vec"], 16 * 5)
            for k in range(KD):
                last = pe.matmul(YP[:, D:D + 1], wqk_raw[:, k, :], vec[:, LN1B.start + k:LN1B.start + k + 1],
                                 start=(k == 0), stop=(k == KD - 1))
            pe.wait_ge(s["wvo_raw_ready"], 1)
            pe.wait_ge(s["prep_vec"], 2 * KD)
            for k in range(KD):
                pe.matmul(YP[:, 0:D], rep[:, 4 + k, :], wvo_raw[:, k, :], start=(k == 0), stop=False)
            for k in range(KD):
                last = pe.matmul(YP[:, 0:D], rep[:, 6 + k, :], o_raw[:, k, :], start=False, stop=(k == KD - 1))
            last.then_inc(s["wvo_mm"], 1)
            pe.wait_ge(s["ld_ffn"], 16 * 6)
            pe.wait_ge(s["mod_ready"], 6)
            for m in range(MH):
                for k in range(KD):
                    last = pe.matmul(FF[0][:, m:m + 1], raw_up[:, k, P * m:P * m + P],
                                     vec[:, LN2B.start + k:LN2B.start + k + 1], start=(k == 0), stop=(k == KD - 1))
            last.then_inc(s["ffn_bias_mm"], 1)

            def transpose_group(src, banks, done):
                for k in range(KD):
                    for t in range(NT):
                        last = pe.transpose(banks[k][:, P * t:P * t + P], src[:, t, P * k:P * k + P], ident[:])
                    last.then_inc(s[done], 1)

            def t1(a):
                pe.wait_ge(s["xn1_ready"], a + 1)
                pe.wait_ge(s["h2_ready"], a)
                pe.wait_ge(s["state_ready"], a * B)
                transpose_group(xn1, TP, "t1_done")

            def t2(f):
                pe.wait_ge(s["xn2_ready"], f + 1)
                pe.wait_ge(s["h2_ready"], f + 1)
                transpose_group(xn2, [AT[1], AT[2]], "t2_done")

            def t3(g, A):
                pe.wait_ge(s["h3_ready"], g + 1)
                if A:
                    pe.wait_ge(s["t1_lo"], (g + 3) * KD)
                else:
                    pe.wait_ge(s["h2_ready"], NG)
                    pe.wait_ge(s["state_ready"], NG * B)
                transpose_group(h3, TP, "t3_done")

            def queries_keys(a):
                pe.wait_ge(s["t1_hi"], a * KD + KD)
                pe.wait_ge(s["t1_lo"], a * KD + KD)
                product(AT[0][:], lambda k: (wqk_hi[:, k, :], wqk_lo[:, k, :]),
                        lambda k: (xt1_hi[:, k, :], xt1_lo[:, k, :]), KD).then_inc(s["qk_done"], 1)

            def route(g):
                pe.wait_ge(s["t3_copied"], g * KD + KD)
                pe.wait_ge(s["x2_ready"], g + 1)
                for t in range(NT):
                    for k in range(KD):
                        last = pe.matmul(YP[:, E * t:E * t + E], h3t[:, k, P * t:P * t + P], gate_sb[:, k, :],
                                         start=(k == 0), stop=(k == KD - 1))
                last.then_inc(s["gate_done"], 1)

            def values(a):
                for j in range(2):
                    for t in (2 * j, 2 * j + 1):
                        tok = slice(P * t, P * t + P)
                        last = product(AT[1 + j][:, D * (t % 2):D * (t % 2) + D],
                                       lambda k: (xt1_hi[:, k, tok], xt1_lo[:, k, tok]),
                                       lambda k: (wvo_hi[:, k, :], wvo_lo[:, k, :]), KD)
                    last.then_inc(s["v_done"], 1)

            def ffn_up(f, chunks):
                for m in chunks:
                    if m < 2:
                        pe.wait_ge(s["x2_ready"], f)
                    else:
                        pe.wait_ge(s["gelu_done"], f * MH + m - 1)
                    hid = slice(P * m, P * m + P)
                    product(FF[m % 2][:], lambda k: (up_hi[FFN][:, k, hid], up_lo[FFN][:, k, hid]),
                            lambda k: (xt2_hi[:, k, :], xt2_lo[:, k, :]), KD).then_inc(s["ff1_done"], 1)

            def ffn_down(f, tiles):
                for t in tiles:
                    if t < 2:
                        pe.wait_ge(s["gelu_done"], f * MH + MH - 1 + t)
                    tok = slice(P * t, P * t + P)
                    for m in range(MH):
                        if t == 0:
                            pe.wait_ge(s["act_split"], f * MH + m + 1)
                        first, last = m == 0, m == MH - 1
                        dst = down_bank[t][:, 0:D]
                        pe.matmul(dst, act_hi[:, m, tok], down_hi[FFN][:, m, :], start=first, stop=False)
                        pe.matmul(dst, act_hi[:, m, tok], down_lo[FFN][:, m, :], start=False, stop=False)
                        done = pe.matmul(dst, act_lo[:, m, tok], down_hi[FFN][:, m, :], start=False, stop=last)
                    done.then_inc(s["ff2_done"], 1)

            def keys_back(a):
                pe.wait_ge(s["qk_ready"], a + 1)
                for t in range(NT):
                    last = pe.transpose(AT[0][:, P * t:P * t + P], kz[:, P * t:P * t + P], ident[:])
                last.then_inc(s["kt_done"], 1)

            def scores(a):
                for b in range(B):
                    pe.wait_ge(s["v_ready"], a * B + b + 1)
                    q0 = GB * b
                    pe.matmul(AT[1 + b][:, 0:GB], kz[:, q0:q0 + P], qk[:, q0:q0 + GB], start=True, stop=True)
                    pe.matmul(AT[1 + b][:, GB:GB + P], kz[:, q0 + P:q0 + GB], qk[:, q0 + P:q0 + GB],
                              start=True, stop=True).then_inc(s["s_done"], 1)

            def ranks(g):
                pe.wait_ge(s["picked_ready"], g + 1)
                flat_picked = picked[:, :, :].rearrange("p t e -> p (t e)")
                pe.matmul(YP[:, 2 * NT * E:3 * NT * E], below[:], flat_picked, start=True, stop=True)
                pe.matmul(YP[:, 3 * NT * E:4 * NT * E], ones_bf[:], flat_picked, start=True, stop=True) \
                    .then_inc(s["rank_done"], 1)

            def attend(a):
                pe.wait_ge(s["kt_copied"], a + 1)
                for b, t, dst in ((0, 0, AT[0]), (0, 1, AT[1]), (1, 0, AT[2]), (1, 1, TP[0])):
                    pe.wait_ge(s["masked"], a * B + b + 1)
                    q0 = GB * b + P * t
                    pe.matmul(dst[:, 0:DV], probs[:, b, P * t:P * t + P], val[:, TT * b, :], start=True, stop=False)
                    if t:
                        pe.matmul(dst[:, 0:DV], probs[:, b, 2 * P:3 * P], val[:, TT * b + 1, :], start=False, stop=False)
                    pe.matmul(dst[:, 0:DV], qk[:, q0:q0 + P], state[:, b, :], start=False, stop=True) \
                        .then_inc(s["av_done"], 1)

            def carry(a, b):
                for t in range(TT):
                    last = pe.matmul(carry_bank[b][:, 0:DV], kt[:, TT * b + t, :], val[:, TT * b + t, :],
                                     start=(t == 0), stop=(t == TT - 1))
                last.then_inc(s["kv_done"], 1)

            def iteration(i, A, F, G):
                if A:
                    t1(i)
                if F:
                    t2(i - 1)
                if A:
                    if G:
                        pe.wait_ge(s["x2_ready"], i - 1)
                    queries_keys(i)
                if F:
                    pe.wait_ge(s["t2_hi"], (i - 1) * KD + KD)
                    pe.wait_ge(s["t2_lo"], (i - 1) * KD + KD)
                if A:
                    values(i)
                if F:
                    ffn_up(i - 1, range(0, 2))
                if A:
                    keys_back(i)
                    scores(i)
                if F:
                    ffn_up(i - 1, range(2, 5))
                if G:
                    t3(i - 2, A)
                if F:
                    ffn_up(i - 1, range(5, 6))
                if G:
                    route(i - 2)
                if A:
                    attend(i)
                if F:
                    ffn_up(i - 1, range(6, 7))
                if G:
                    ranks(i - 2)
                if F:
                    ffn_up(i - 1, range(7, 8))
                if A:
                    carry(i, 0)
                if F:
                    ffn_down(i - 1, (0,))
                if A:
                    if G:
                        pe.wait_ge(s["pos_ready"], i - 1)
                    carry(i, 1)
                if F:
                    ffn_down(i - 1, (1,))
                    if A:
                        pe.wait_ge(s["state_ready"], i * B + B)
                        pe.wait_ge(s["h2_ready"], i + 1)
                    elif G:
                        pe.wait_ge(s["pos_ready"], i - 1)
                    ffn_down(i - 1, (2, 3))

            pe.wait_ge(s["state_ready"], 0)
            pe.wait_ge(s["consts"], 1)
            pe.wait_ge(s["wprep"], 8)
            pe.wait_ge(s["mod_ready"], 6)
            iteration(0, True, False, False)
            pe.wait_ge(s["bias_ready"], 8)
            iteration(1, True, True, False)
            with pe.Fori(2, NG) as i:
                iteration(i, True, True, True)
            iteration(NG, False, True, True)
            iteration(NG + 1, False, False, True)
            pe.drain().then_inc(s["phase1_over"], 1)

            def rows_back(g):
                pe.wait_ge(s["rows_loaded"], g * 16 + 16)
                pe.wait_ge(s["rt_lo_done"], g)
                for k in range(KD):
                    for t in range(2):
                        last = pe.transpose(TP[0][:, TR * k + P * t:TR * k + P * t + P], rows[:, t, P * k:P * k + P], ident[:])
                last.then_inc(s["rt_done"], 1)

            def expert_up(g, w):
                pe.wait_ge(s["rt_hi_done"], g + 1)
                pe.wait_ge(s["rt_lo_done"], g + 1)
                for m in range(MH):
                    pe.wait_ge(s["relu_done"], g * MH + max(0, m - 3))
                    hid = slice(P * m, P * m + P)
                    product(up_bank[m % 4][:, 0:TR], lambda k: (up_hi[w][:, k, hid], up_lo[w][:, k, hid]),
                            lambda k: (rt_hi[:, k, :], rt_lo[:, k, :]), KD).then_inc(s["l1_done"], 1)

            def expert_down(g, w):
                pe.wait_ge(s["y_ready"], g * 2)
                for t in range(2):
                    for m in range(MH):
                        if t == 0:
                            pe.wait_ge(s["r_split"], g * MH + m + 1)
                        dst = y_bank[t][:, 0:D]
                        row = slice(P * t, P * t + P)
                        pe.matmul(dst, r_hi[:, m, row], down_hi[w][:, m, :], start=(m == 0), stop=False)
                        pe.matmul(dst, r_hi[:, m, row], down_lo[w][:, m, :], start=False, stop=False)
                        last = pe.matmul(dst, r_lo[:, m, row], down_hi[w][:, m, :], start=False, stop=(m == MH - 1))
                    last.then_inc(s["l2_done"], 1)

            pe.wait_ge(s["table_ready"], 1)
            pe.wait_ge(s["phase1_over"], 5)
            rows_back(1)
            with pe.Fori(0, E // 2) as pair:
                for w in (0, 1):
                    tiles = pe.value_load(table[0:1, 1, bass.ds(pair * 2 + w, 1)], min_val=1, max_val=T // TR)
                    first = pe.value_load(table[0:1, 2, bass.ds(pair * 2 + w, 1)], min_val=1, max_val=2 * T // TR + E)
                    pe.wait_ge(s["up_ready"], pair * 2 + w + 1)
                    pe.wait_ge(s["down_ready"], pair * 2 + w + 1)
                    alone(pe)
                    with pe.Fori(0, tiles) as i:
                        g = first + i
                        expert_up(g, w)
                        rows_back(g + 1)
                        last = expert_down(g, w)

        @block.scalar
        def _(act):
            steps = [0]

            def step(ins):
                steps[0] += 1
                ins.then_inc(s["act_step"], 1)
                act.wait_ge(s["act_step"], steps[0])

            for name, per_tile in (("rt_hi_done", 1), ("relu_done", MH)):
                act.sem_inc(s[name], per_tile)
            act.wait_ge(s["ld_mod"], 32)
            act.activation(csig[:], cvec[:], ACT.Exp, scale=-1.0).then_inc(s["silu_e"], 1)
            act.wait_ge(s["ld_vec"], 16 * 5)
            act.wait_ge(s["ld_ffn"], 16 * 6)
            for k in range(KD):
                act.activation(up_hi[FFN][:, k, :], raw_up[:, k, :], ACT.Identity,
                               scale=vec[:, LN2W.start + k:LN2W.start + k + 1]).then_inc(s["ffn_bias"], 1)
            for n in range(2):
                act.activation(down_hi[FFN][:, 4 * n:4 * n + 4, :], raw_down[:, 4 * n:4 * n + 4, :], ACT.Copy) \
                    .then_inc(s["ffn_bias"], 1)

            def head(hi, banks, done, sem_out, base):
                for k in range(KD):
                    act.wait_ge(s[done], base + k + 1)
                    act.activation(hi[:, k, :], banks[k][:], ACT.Copy).then_inc(s[sem_out], 1)

            def gelu(f, chunks):
                for m in chunks:
                    act.wait_ge(s["ff1_done"], f * MH + m + 1)
                    act.wait_ge(s["act_split"], f * MH + max(0, m - RING + 1))
                    act.activation(gelu_ring[:, m % RING, :], FF[m % 2][:], ACT.Gelu, bias=f1b[:, m:m + 1])
                    act.activation(act_hi[:, m, :], FF[m % 2][:], ACT.Gelu, bias=f1b[:, m:m + 1]) \
                        .then_inc(s["gelu_done"], 1)

            def normed(kind, n, src, dst, done):
                act.wait_ge(s[SHIFTED[kind]], n + 1)
                for t in range(NT):
                    last = act.activation(dst[:, t, :], src[:, t, :], ACT.Identity, bias=shift[kind][:, t:t + 1],
                                          scale=rstd[kind][:, t:t + 1])
                last.then_inc(s[done], 1)

            def norm_h(n):
                act.wait_ge(s["t1_done"], n * KD)
                normed(1, n, xa, xn1, "xn1_ready")

            def norm_2(a):
                act.wait_ge(s["t2_done"], a * KD)
                normed(2, a, h2, xn2, "xn2_ready")

            def iteration(i, A, F, G, NEXT):
                if A:
                    act.wait_ge(s["v_done"], i * 2)
                    head(xt1_hi, TP, "t1_done", "t1_hi", i * KD)
                if F:
                    act.wait_ge(s["ff1_done"], (i - 1) * MH)
                    head(xt2_hi, [AT[1], AT[2]], "t2_done", "t2_hi", (i - 1) * KD)
                if A:
                    act.wait_ge(s["elu_min"], i + 1)
                    act.activation(elu[:], elu[:], ACT.Exp).then_inc(s["elu_exp"], 1)
                if F:
                    act.wait_ge(s["ff2_done"], (i - 1) * NT)
                    gelu(i - 1, range(0, 2))
                if A:
                    act.wait_ge(s["kt_done"], i + 1)
                    act.wait_ge(s["kv_done"], i * B)
                    act.activation(kt[:], AT[0][:].rearrange("p (t n) -> p t n", t=NT), ACT.Copy) \
                        .then_inc(s["kt_copied"], 1)
                if F:
                    gelu(i - 1, range(2, 5))
                if G:
                    head(h3t, TP, "t3_done", "t3_copied", (i - 2) * KD)
                if F:
                    gelu(i - 1, range(5, 7))
                if NEXT:
                    norm_h(i + 1)
                if F:
                    gelu(i - 1, range(7, 8))
                if A:
                    norm_2(i)
                if G:
                    act.wait_ge(s["gap_ready"], i - 1)
                    act.activation(e2[:], gap[:], ACT.Exp).then_inc(s["gate_exp"], 1)

            norm_h(0)
            act.wait_ge(s["bias_ready"], 8)
            act.wait_ge(s["wprep"], 8)
            iteration(0, True, False, False, True)
            iteration(1, True, True, False, True)
            with act.Fori(2, NG - 1) as i:
                iteration(i, True, True, True, True)
            iteration(NG - 1, True, True, True, False)
            iteration(NG, False, True, True, False)
            act.wait_ge(s["ld_first"], 32)
            act.activation(up_hi[0][:], first_up[:], ACT.Copy).then_inc(s["first_hi"], 1)
            act.activation(down_hi[0][:], first_down[:], ACT.Copy).then_inc(s["first_hi"], 1)
            iteration(NG + 1, False, False, True, False)
            act.drain().then_inc(s["phase1_over"], 1)

            act.wait_ge(s["table_ready"], 1)
            act.wait_ge(s["phase1_over"], 5)

            def rows_head(g):
                act.wait_ge(s["rt_done"], g + 1)
                act.activation(rt_hi, TP[0][:].rearrange("p (k n) -> p k n", k=KD), ACT.Copy) \
                    .then_inc(s["rt_hi_done"], 1)

            rows_head(1)
            with act.Fori(0, E // 2) as pair:
                for w in (0, 1):
                    e = pair * 2 + w
                    tiles = act.value_load(table[0:1, 1, bass.ds(e, 1)], min_val=1, max_val=T // TR)
                    first = act.value_load(table[0:1, 2, bass.ds(e, 1)], min_val=1, max_val=2 * T // TR + E)
                    act.wait_ge(s["up_loaded"], e * 16 + 16)
                    act.activation(up_hi[1 - w][:], raw_up[:], ACT.Copy).then_inc(s["up_hi_ready"], 1)
                    act.wait_ge(s["relu_done"], first * MH)
                    act.activation(b1_cur[:], b1_all[:, bass.ds(e, 1), :].rearrange("p e m -> p (e m)"), ACT.Copy) \
                        .then_inc(s["act_step"], 1)
                    act.wait_ge(s["act_step"], e + 1)
                    with act.Fori(0, tiles) as i:
                        g = first + i
                        act.wait_ge(s["l2_done"], g * 2)
                        for m in range(MH):
                            act.wait_ge(s["l1_done"], g * MH + m + 1)
                            act.wait_ge(s["r_split"], g * MH + max(0, m - RING + 1))
                            act.activation(r_ring[:, m % RING, :], up_bank[m % 4][:, 0:TR], ACT.Relu,
                                           bias=b1_cur[:, m:m + 1])
                            act.activation(r_hi[:, m, :], up_bank[m % 4][:, 0:TR], ACT.Relu, bias=b1_cur[:, m:m + 1]) \
                                .then_inc(s["relu_done"], 1)
                        rows_head(g + 1)

        @block.vector
        def _(dve):
            steps = [0]
            base = [0]

            def step(ins):
                steps[0] += 1
                ins.then_inc(s["dve_step"], 1)

            def settle():
                dve.wait_ge(s["dve_step"], base[0] + steps[0])

            V = nc.vector
            for name, per_tile in (("meta_read", 1), ("r_split", MH), ("rt_lo_done", 1), ("y_ready", 2), ("up_ready", 1)):
                dve.sem_inc(s[name], per_tile)
            V.memset(ones[:], 1.0).then_inc(s["mod_c"], 1)
            step(V.memset(state[:], 0.0))
            step(V.memset(kz[:], 0.0))
            step(V.memset(val[:, :, D:DV], 1.0))
            step(V.memset(neg_half[:], -0.5))
            step(V.memset(ones_bf[:], 1.0))
            step(V.memset(h3[:, :, META:ROW], 0.0))
            settle()
            step(V.memset(h3[:, TT:NT, META + 5:META + 6], 1.0))
            dve.wait_ge(s["silu_e"], 1)
            step(V.tensor_scalar(csig[:], csig[:], 1.0, None, ALU.add))
            settle()
            step(V.reciprocal(csig[:], csig[:]))
            settle()
            step(V.tensor_tensor(csig[:], csig[:], cvec[:], ALU.mult))
            settle()
            dve.wait_ge(s["mod_c"], 1)
            for k in range(KD):
                for b in range(B):
                    V.tensor_scalar(rep[:, B * k + b, :], ones[:], csig[:, k, b:b + 1], None, ALU.mult) \
                        .then_inc(s["silu_rep"], 1)
            dve.wait_ge(s["ld_vec"], 16 * 5)
            for n, src in enumerate((LN1B, VB)):
                for k in range(KD):
                    V.tensor_scalar(rep[:, 4 + 2 * n + k, :], ones[:], vec[:, src.start + k:src.start + k + 1], None,
                                    ALU.mult).then_inc(s["prep_vec"], 1)

            def norm_stats(kind, src):
                for t in range(NT):
                    step(V.bn_stats(stats[:, t, :], src[:, t, 0:D]))
                settle()
                alone(dve)
                for t in range(NT):
                    step(V.bn_aggr(mv[kind][:, t, :], stats[:, t, :]))
                settle()
                if kind in (NORM_1, NORM_2):
                    V.tensor_scalar(neg_mean[kind][:], mv[kind][:, :, 0], -1.0, None, ALU.mult).then_inc(s[VE[kind]], 1)
                V.tensor_scalar(ve[kind][:], mv[kind][:, :, 1], LN_EPS, None, ALU.add).then_inc(s[VE[kind]], 1)

            def stats_x(n):
                dve.wait_ge(s["x_loaded"], n * 32 + 32)
                norm_stats(NORM_A, xa)

            def norm_x(n):
                dve.wait_ge(s["rstd_ready"], n + 1)
                for t in range(NT):
                    last = V.tensor_scalar(xa[:, t, :], xa[:, t, :], mv[NORM_A][:, t, 0:1], rstd[NORM_A][:, t:t + 1],
                                           ALU.subtract, ALU.mult)
                last.then_inc(s["xa_normed"], 1)

            def stats_h(n):
                dve.wait_ge(s["h_ready"], n + 1)
                dve.wait_ge(s["shift1_ready"], n)
                norm_stats(NORM_1, xa)

            def stats_2(a):
                dve.wait_ge(s["h2_ready"], a + 1)
                dve.wait_ge(s["shift2_ready"], a)
                norm_stats(NORM_2, h2)

            def stats_x2(g):
                dve.wait_ge(s["x2_ready"], g + 1)
                norm_stats(NORM_B, x2)

            def norm_x2(g):
                dve.wait_ge(s["t3_done"], g * KD)
                dve.wait_ge(s["scattered"], g * (32 * NT))
                for t in range(NT):
                    step(V.scalar_tensor_tensor(h3[:, t, 0:D], x2[:, t, :], mv[NORM_B][:, t, 0:1],
                                                mod[:, t // TT, CB, :], ALU.subtract, ALU.mult))
                dve.wait_ge(s["rs3_ready"], g + 1)
                settle()
                for t in range(NT):
                    last = V.scalar_tensor_tensor(h3[:, t, 0:D], h3[:, t, 0:D], rstd[NORM_B][:, t:t + 1],
                                                  mod[:, t // TT, SB_, :], ALU.mult, ALU.add)
                last.then_inc(s["h3_ready"], 1)

            stats_x(0)
            norm_x(0)
            where = [TP[0], TP[1], AT[0], AT[1], AT[2], FF[0]]
            for n in range(3):
                for b in range(B):
                    dve.wait_ge(s["mod_mm"], 2 * n + b + 1)
                    bk = where[2 * n + b]
                    plain, other = ((0, 1), (1, 0), (0, 1))[n]
                    step(V.tensor_copy(mod[:, b, 2 * n + plain, :], bk[:, D * plain:D * plain + D]))
                    if n != 1:
                        pass
                    settle()
                    src = bk[:, D * other:D * other + D]
                    dst = mod[:, b, 2 * n + other, :]
                    if n == 0:
                        V.tensor_scalar(dst, src, 1.0, None, ALU.add).then_inc(s["mod_ready"], 1)
                    else:
                        step(V.tensor_scalar(b2_cur[:], src, 0.0, 2.0, ALU.is_ge, ALU.mult))
                        settle()
                        step(V.tensor_scalar(b2_cur[:], b2_cur[:], 1.0, None, ALU.subtract))
                        settle()
                        step(V.tensor_tensor(dst, src, b2_cur[:], ALU.mult))
                        if n == 2:
                            step(V.tensor_scalar(mod[:, b, CB, :], mod[:, b, CB, :], 1.0, None, ALU.add))
                        settle()
                        V.scalar_tensor_tensor(dst, dst, 0.25, b2_cur[:], ALU.max, ALU.mult) \
                            .then_inc(s["mod_ready"], 1)
                        dve.wait_ge(s["mod_ready"], 2 * n + b + 1)
            stats_h(0)
            dve.wait_ge(s["ld_attn"], 16 * 5)
            dve.wait_ge(s["ld_vec"], 16 * 5)
            for k in range(KD):
                step(V.tensor_scalar(wqk_raw[:, k, :], wqk_raw[:, k, :], 1.0, None, ALU.mult)
                     if False else V.tensor_scalar(elu[:, P * k:P * k + P], wqk_raw[:, k, :],
                                                   vec[:, LN1W.start + k:LN1W.start + k + 1], None, ALU.mult))
            settle()
            ewqk = elu[:, 0:KD * P].rearrange("p (k n) -> p k n", k=KD)
            V.tensor_copy(wqk_hi[:], ewqk).then_inc(s["wprep"], 1)
            dve.wait_ge(s["wprep"], 1)
            V.tensor_tensor(wqk_lo[:], ewqk, wqk_hi[:].bitcast(F32), ALU.subtract).then_inc(s["wprep"], 1)
            dve.wait_ge(s["wvo_mm"], 1)
            V.tensor_copy(wvo_raw, FF[1][:].rearrange("p (k n) -> p k n", k=KD)).then_inc(s["wvo_raw_ready"], 1)
            for k in range(KD):
                step(V.tensor_scalar(h2[:, k, :], FF[1][:, D * k:D * k + D],
                                     vec[:, LN1W.start + k:LN1W.start + k + 1], None, ALU.mult))
            settle()
            V.tensor_copy(wvo_hi[:], h2[:, 0:2, :]).then_inc(s["wprep"], 1)
            dve.wait_ge(s["wprep"], 3)
            dve.wait_ge(s["wvo_mm"], 2)
            V.tensor_tensor(wvo_lo[:], h2[:, 0:2, :], wvo_hi[:].bitcast(F32), ALU.subtract).then_inc(s["wprep"], 1)
            V.tensor_copy(bvo_bc[:], YP[:, 0:D]).then_inc(s["wprep"], 1)
            step(V.tensor_tensor(qkb[:, 0:1], qkb[:, 0:1], YP[:, D:D + 1], ALU.add))
            settle()
            V.tensor_scalar(qkb[:, 1:2], qkb[:, 0:1], 1.0, None, ALU.add).then_inc(s["wprep"], 1)
            V.tensor_copy(gb_bc[:, 0, :], mod[:, 0, GATE_B, :]).then_inc(s["wprep"], 1)
            V.tensor_tensor(gb_bc[:, 1, :], mod[:, 1, GATE_B, :], mod[:, 0, GATE_B, :], ALU.subtract) \
                .then_inc(s["wprep"], 1)
            dve.wait_ge(s["wprep"], 8)
            for k in range(KD):
                dve.wait_ge(s["ffn_bias"], k + 1)
                V.scalar_tensor_tensor(up_lo[FFN][:, k, :], raw_up[:, k, :], vec[:, LN2W.start + k:LN2W.start + k + 1],
                                       up_hi[FFN][:, k, :].bitcast(F32), ALU.mult, ALU.subtract) \
                    .then_inc(s["bias_ready"], 1)
            for n in range(4):
                dve.wait_ge(s["ffn_bias"], 3 + n // 2)
                V.tensor_tensor(down_lo[FFN][:, 2 * n:2 * n + 2, :], raw_down[:, 2 * n:2 * n + 2, :],
                                down_hi[FFN][:, 2 * n:2 * n + 2, :].bitcast(F32), ALU.subtract) \
                    .then_inc(s["bias_ready"], 1)
            dve.wait_ge(s["ffn_bias_mm"], 1)
            V.tensor_tensor(f1b[:], f1b[:], FF[0][:, 0:MH], ALU.add).then_inc(s["bias_ready"], 1)
            dve.wait_ge(s["consts"], 1)
            V.tensor_copy(next_slot[:], slot_base[:]).then_inc(s["bias_ready"], 1)
            dve.wait_ge(s["bias_ready"], 8)

            def rest(hi, lo, banks, hi_done, lo_done, n):
                for k in range(KD):
                    dve.wait_ge(s[hi_done], n * KD + k + 1)
                    V.tensor_tensor(lo[:, k, :], banks[k][:], hi[:, k, :].bitcast(F32), ALU.subtract) \
                        .then_inc(s[lo_done], 1)

            def elu_min(a):
                dve.wait_ge(s["qk_done"], a + 1)
                V.tensor_scalar(elu[:], AT[0][:], qkb[:, 0:1], 0.0, ALU.add, ALU.min).then_inc(s["elu_min"], 1)

            def elu_max(a):
                dve.wait_ge(s["elu_exp"], a + 1)
                dve.wait_ge(s["av_done"], a * NT)
                step(V.scalar_tensor_tensor(qk[:], AT[0][:], qkb[:, 1:2], elu[:], ALU.add, ALU.max))
                settle()
                V.tensor_copy(kz[0:NF, :], qk[NF:P, :]).then_inc(s["qk_ready"], 1)

            def values_out(a):
                dve.wait_ge(s["kv_done"], a * B)
                for b in range(B):
                    dve.wait_ge(s["v_done"], a * B + b + 1)
                    V.tensor_tensor(val[:, TT * b:TT * b + TT, 0:D], AT[1 + b][:].rearrange("p (t n) -> p t n", t=TT),
                                    bvo_bc[:, None, :].broadcast_to([P, TT, D]), ALU.add).then_inc(s["v_ready"], 1)

            def split_act(f, chunks):
                for m in chunks:
                    dve.wait_ge(s["gelu_done"], f * MH + m + 1)
                    V.tensor_tensor(act_lo[:, m, :], gelu_ring[:, m % RING, :], act_hi[:, m, :].bitcast(F32),
                                    ALU.subtract).then_inc(s["act_split"], 1)

            def best_two(g):
                dve.wait_ge(s["gate_done"], g + 1)
                step(V.tensor_copy(logits[:], YP[:, 0:NT * E].rearrange("p (t e) -> p t e", t=NT)))
                settle()
                alone(dve)
                for t in range(NT):
                    step(V.max(top[:, t, :], logits[:, t, :]))
                settle()
                V.tensor_tensor(gap[:], top[:, :, 1], top[:, :, 0], ALU.subtract).then_inc(s["gap_ready"], 1)
                for t in range(NT):
                    step(V.max_index(top_at[:, t, :], top[:, t, :], logits[:, t, :]))
                settle()
                step(V.tensor_copy(h3[:, :, META:META + 2], top_at[:, :, 0:2]))
                step(V.tensor_copy(h3[:, :, META + 4], token[:]))
                settle()
                step(V.tensor_scalar(token[:], token[:], float(GB), None, ALU.add))
                for c_ in range(2):
                    step(V.tensor_tensor(chosen[:, c_, :, :], expert_id[:, None, :].broadcast_to([P, NT, E]),
                                         h3[:, :, META + c_:META + c_ + 1].broadcast_to([P, NT, E]), ALU.is_equal))
                settle()
                V.tensor_tensor(picked[:], chosen[:, 0], chosen[:, 1], ALU.add).then_inc(s["picked_ready"], 1)

            def gate_weights(g):
                dve.wait_ge(s["gate_exp"], g + 1)
                step(V.tensor_scalar(e2p1[:], e2[:], 1.0, None, ALU.add))
                settle()
                step(V.reciprocal(e2p1[:], e2p1[:]))
                settle()
                V.tensor_copy(h3[:, :, META + 2], e2p1[:]).then_inc(s["weights_ready"], 1)
                V.tensor_tensor(h3[:, :, META + 3], e2p1[:], e2[:], ALU.mult).then_inc(s["weights_ready"], 1)

            def slots_of(g):
                dve.wait_ge(s["rank_done"], g + 1)
                step(V.tensor_tensor(place[:], YP[:, 2 * NT * E:3 * NT * E].rearrange("p (t e) -> p t e", t=NT),
                                     next_slot[:, None, :].broadcast_to([P, NT, E]), ALU.add))
                step(V.tensor_copy(totals[:], YP[:, 3 * NT * E:4 * NT * E].rearrange("p (t e) -> p t e", t=NT)))
                settle()
                for t in range(NT):
                    if t < NT - 1:
                        step(V.tensor_tensor(place[:, t + 1:NT, :], place[:, t + 1:NT, :],
                                             totals[:, t:t + 1, :].broadcast_to([P, NT - 1 - t, E]), ALU.add))
                    step(V.tensor_tensor(next_slot[:], next_slot[:], totals[:, t, :], ALU.add))
                    settle()
                step(V.tensor_tensor(place2[:], chosen[:], place[:, None, :, :].broadcast_to([P, 2, NT, E]), ALU.mult))
                settle()
                step(V.tensor_reduce(pos[:], place2[:].rearrange("p c t e -> p (c t) e"), AX_X, ALU.add))
                settle()
                V.tensor_copy(pos_u[:], pos[:]).then_inc(s["pos_ready"], 1)

            def mask(a):
                for b in range(B):
                    dve.wait_ge(s["s_done"], a * B + b + 1)
                    V.tensor_tensor(probs[:, b, :], AT[1 + b][:, 0:3 * P], causal[:], ALU.mult).then_inc(s["masked"], 1)

            def attended(a):
                dve.wait_ge(s["hob_ready"], a + 1)
                dve.wait_ge(s["res_ready"], a)
                for t, bk in enumerate((AT[0], AT[1], AT[2], TP[0])):
                    dve.wait_ge(s["av_done"], a * NT + t + 1)
                    step(V.tensor_scalar(rden[:, t:t + 1], bk[:, D:D + 1], ATTN_EPS, None, ALU.add))
                settle()
                step(V.reciprocal(rden[:], rden[:]))
                settle()
                for t, bk in enumerate((AT[0], AT[1], AT[2], TP[0])):
                    last = V.scalar_tensor_tensor(h2[:, t, :], bk[:, 0:D], rden[:, t:t + 1], hob[:, t, :],
                                                  ALU.mult, ALU.add)
                last.then_inc(s["h2_ready"], 1)

            def carry_state(a, b):
                dve.wait_ge(s["kv_done"], a * B + b + 1)
                V.tensor_tensor(state[:, b, :], state[:, b, :], carry_bank[b][:, 0:DV], ALU.add).then_inc(s["state_ready"], 1)

            def ffn_out(f):
                dve.wait_ge(s["x2_stored"], f * 32)
                dve.wait_ge(s["res_ready"], f + 1)
                for t in range(NT):
                    dve.wait_ge(s["ff2_done"], f * NT + t + 1)
                    V.tensor_tensor(x2[:, t, :], down_bank[t][:, 0:D], mod[:, t // TT, GA, :], ALU.mult) \
                        .then_inc(s["ff2_read"], 1)
                dve.wait_ge(s["ff2_read"], f * NT + NT)
                V.tensor_tensor(x2[:], x2[:], res[:], ALU.add).then_inc(s["x2_ready"], 1)

            def iteration(i, A, F, G, NEXT):
                if A:
                    rest(xt1_hi, xt1_lo, TP, "t1_hi", "t1_lo", i)
                if F:
                    rest(xt2_hi, xt2_lo, [AT[1], AT[2]], "t2_hi", "t2_lo", i - 1)
                if A:
                    elu_min(i)
                if G:
                    stats_x2(i - 2)
                if A:
                    elu_max(i)
                    values_out(i)
                if G:
                    norm_x2(i - 2)
                if F:
                    split_act(i - 1, range(0, 2))
                if A:
                    mask(i)
                if NEXT:
                    stats_x(i + 1)
                if F:
                    split_act(i - 1, range(2, 3))
                if NEXT:
                    norm_x(i + 1)
                if F:
                    split_act(i - 1, range(3, 5))
                if G:
                    best_two(i - 2)
                if F:
                    split_act(i - 1, range(5, 6))
                if NEXT:
                    stats_h(i + 1)
                if G:
                    slots_of(i - 2)
                if A:
                    attended(i)
                if F:
                    split_act(i - 1, range(6, 8))
                if F and not A:
                    dve.wait_ge(s["first_hi"], 1)
                    V.tensor_tensor(up_lo[0][:], first_up[:], up_hi[0][:].bitcast(F32), ALU.subtract) \
                        .then_inc(s["first_set"], 1)
                    dve.wait_ge(s["first_hi"], 2)
                    V.tensor_tensor(down_lo[0][:], first_down[:], down_hi[0][:].bitcast(F32), ALU.subtract) \
                        .then_inc(s["first_set"], 1)
                if A:
                    carry_state(i, 0)
                    stats_2(i)
                    carry_state(i, 1)
                if G:
                    gate_weights(i - 2)
                if F:
                    ffn_out(i - 1)

            iteration(0, True, False, False, True)
            iteration(1, True, True, False, True)
            start = steps[0]
            with dve.Fori(2, NG - 1) as i:
                base[0] = (i - 2) * DVE_ROUND
                iteration(i, True, True, True, True)
            assert steps[0] - start == DVE_ROUND, steps[0] - start
            base[0] = (NG - 4) * DVE_ROUND
            iteration(NG - 1, True, True, True, False)
            iteration(NG, False, True, True, False)
            iteration(NG + 1, False, False, True, False)
            step(V.tensor_tensor(cnt_f[:, 0, :], next_slot[:], slot_base[:], ALU.subtract))
            settle()
            step(V.tensor_scalar(cnt_f[:, 1, :], cnt_f[:, 0, :], float(TR - 1), None, ALU.add))
            settle()
            step(V.tensor_copy(cnt_i[:, 0:2, :], cnt_f[:, 0:2, :]))
            settle()
            step(V.tensor_single_scalar(cnt_i[:, 2, :], cnt_i[:, 1, :], TR.bit_length() - 1, ALU.logical_shift_right))
            settle()
            step(V.tensor_copy(cnt_f[:, 1, :], cnt_i[:, 2, :]))
            settle()
            step(V.tensor_scalar(cnt_f[:, 1, :], cnt_f[:, 1, :], 1.0, None, ALU.max))
            step(V.memset(cnt_f[:, 2, 0:1], 1.0))
            settle()
            for e in range(1, E):
                step(V.tensor_tensor(cnt_f[:, 2, e:e + 1], cnt_f[:, 2, e - 1:e], cnt_f[:, 1, e - 1:e], ALU.add))
                settle()
            V.tensor_copy(table[:], cnt_f[:]).then_inc(s["table_ready"], 1)
            step(V.memset(cur_e[:], -1.0))
            settle()
            dve.drain().then_inc(s["phase1_over"], 1)

            dve.wait_ge(s["table_ready"], 1)
            dve.wait_ge(s["phase1_over"], 5)
            dve.wait_ge(s["b2_loaded"], 16 * E)

            def rows_rest(g):
                dve.wait_ge(s["rt_hi_done"], g + 1)
                V.tensor_tensor(rt_lo, TP[0][:].rearrange("p (k n) -> p k n", k=KD), rt_hi.bitcast(F32),
                                ALU.subtract).then_inc(s["rt_lo_done"], 1)

            def take_meta(g):
                dve.wait_ge(s["rows_loaded"], g * 16 + 16)
                V.tensor_copy(meta[:], rows[:, :, META:ROW]).then_inc(s["meta_read"], 1)

            take_meta(1)
            rows_rest(1)
            done_before = steps[0]
            HEAD, TILE = 2, 8
            with dve.Fori(0, E // 2) as pair:
                for w in (0, 1):
                    e = pair * 2 + w
                    tiles = dve.value_load(table[0:1, 1, bass.ds(e, 1)], min_val=1, max_val=T // TR)
                    first = dve.value_load(table[0:1, 2, bass.ds(e, 1)], min_val=1, max_val=2 * T // TR + E)
                    dve.wait_ge(s["up_hi_ready"], e + 1)
                    V.tensor_tensor(up_lo[1 - w][:], raw_up[:], up_hi[1 - w][:].bitcast(F32), ALU.subtract) \
                        .then_inc(s["up_ready"], 1)
                    base[0] = (NG - 4) * DVE_ROUND + e * HEAD + (first - 1) * TILE
                    before = steps[0]
                    dve.wait_ge(s["y_ready"], first * 2)
                    step(V.tensor_copy(b2_cur[:], mod[:, bass.ds(e // 4, 1), bass.ds(e % 4, 1), :]
                                       .rearrange("p b j d -> p (b j d)")))
                    step(V.tensor_scalar(cur_e[:], cur_e[:], 1.0, None, ALU.add))
                    settle()
                    alone(dve)
                    assert steps[0] - before == HEAD
                    with dve.Fori(0, tiles) as i:
                        g = first + i
                        base[0] = (NG - 4) * DVE_ROUND + e * HEAD + (g - 1) * TILE
                        before = steps[0]
                        for m in range(MH):
                            dve.wait_ge(s["relu_done"], g * MH + m + 1)
                            V.tensor_tensor(r_lo[:, m, :], r_ring[:, m % RING, :], r_hi[:, m, :].bitcast(F32),
                                            ALU.subtract).then_inc(s["r_split"], 1)
                        dve.wait_ge(s["summed"], g * 32)
                        dve.wait_ge(s["meta_read"], g + 1)
                        step(V.tensor_scalar(is_e[:], meta[:, :, 0:2], cur_e[:, 0:1], None, ALU.is_equal))
                        settle()
                        step(V.tensor_tensor(w_two[:], is_e[:], meta[:, :, 2:4], ALU.mult))
                        settle()
                        step(V.tensor_reduce(w_row[:], w_two[:], AX_X, ALU.add))
                        step(V.tensor_copy(tok_u[:], meta[:, :, 4]))
                        for t in range(2):
                            step(V.scalar_tensor_tensor(g_row[:, t, :], gb_bc[:, 1, :], meta[:, t, 5:6],
                                                        gb_bc[:, 0, :], ALU.mult, ALU.add))
                        rows_rest(g + 1)
                        settle()
                        take_meta(g + 1)
                        for t in range(2):
                            dve.wait_ge(s["l2_done"], g * 2 + t + 1)
                            step(V.tensor_tensor(y[:, t, :], y_bank[t][:, 0:D], b2_cur[:], ALU.add))
                            settle()
                            V.scalar_tensor_tensor(y[:, t, :], y[:, t, :], w_row[:, t:t + 1], g_row[:, t, :],
                                                   ALU.mult, ALU.mult).then_inc(s["y_ready"], 1)
                        assert steps[0] - before == TILE, steps[0] - before
                        steps[0] = before
                    steps[0] = done_before

        @block.gpsimd
        def _(pool):
            G_ = nc.gpsimd
            steps = [0]
            base = [0]

            def step(ins):
                steps[0] += 1
                ins.then_inc(s["pool_step"], 1)

            def settle():
                pool.wait_ge(s["pool_step"], base[0] + steps[0])

            pool.sem_inc(s["rows_loaded"], 16)
            for t in (ident,):
                step(G_.memset(t[:], 0.0))
            step(G_.memset(causal[:], 1.0))
            step(G_.memset(below[:], 1.0))
            step(G_.memset(pad_rows[:], 0.0))
            settle()
            step(G_.affine_select(out=ident[:], in_=ident[:], compare_op=ALU.not_equal, fill=1.0, base=0,
                                  pattern=[[-1, P]], channel_multiplier=1))
            for o in (0, 2):
                step(G_.affine_select(out=causal[:, P * o:P * o + P], in_=causal[:, P * o:P * o + P],
                                      compare_op=ALU.is_ge, fill=0.0, base=0, pattern=[[1, P]], channel_multiplier=-1))
            step(G_.affine_select(out=below[:], in_=below[:], compare_op=ALU.is_gt, fill=0.0, base=0,
                                  pattern=[[1, P]], channel_multiplier=-1))
            step(G_.iota(expert_id[:], pattern=[[1, E]], base=0, channel_multiplier=0,
                         allow_small_or_imprecise_dtypes=True))
            step(G_.iota(slot_base[:], pattern=[[CAP, E]], base=0, channel_multiplier=0,
                         allow_small_or_imprecise_dtypes=True))
            step(G_.iota(token[:].rearrange("p (b t) -> p b t", b=B), pattern=[[N, B], [P, TT]], base=0,
                         channel_multiplier=1, allow_small_or_imprecise_dtypes=True))
            for t in range(2):
                G_.memset(pad_rows[:, t, META + 4:META + 5], float(T)).then_inc(s["pads_ready"], 1)
            step(G_.iota(skip_u[:], pattern=[[0, 1]], base=T, channel_multiplier=0))
            settle()
            G_.memset(e2[:], 0.0).then_inc(s["pads_ready"], 1)
            pool.drain().then_inc(s["consts"], 1)

            def power(kind, n):
                if kind in (NORM_1, NORM_2):
                    pool.wait_ge(s[NORMED[kind]], n)
                    pool.wait_ge(s[VE[kind]], n * 2 + 2)
                    step(G_.tensor_tensor(rstd[kind][:], ve[kind][:], neg_half[:], ALU.pow))
                    settle()
                    G_.tensor_tensor(shift[kind][:], neg_mean[kind][:], rstd[kind][:], ALU.mult) \
                        .then_inc(s[SHIFTED[kind]], 1)
                else:
                    pool.wait_ge(s[VE[kind]], n + 1)
                    G_.tensor_tensor(rstd[kind][:], ve[kind][:], neg_half[:], ALU.pow).then_inc(s[RS[kind]], 1)

            def modulate(dst, one_plus, shift, done):
                for b in range(B):
                    part = dst[:, TT * b:TT * b + TT, 0:D]
                    step(G_.tensor_tensor(part, part, mod[:, b, one_plus:one_plus + 1, :].broadcast_to([P, TT, D]), ALU.mult))
                settle()
                for b in range(B):
                    part = dst[:, TT * b:TT * b + TT, 0:D]
                    last = G_.tensor_tensor(part, part, mod[:, b, shift:shift + 1, :].broadcast_to([P, TT, D]), ALU.add)
                last.then_inc(s[done], 1)

            def h_of(n):
                pool.wait_ge(s["xa_normed"], n + 1)
                modulate(xa, CA, SA, "h_ready")

            def h_plus_ob(n):
                pool.wait_ge(s["h2_ready"], n)
                pool.wait_ge(s["h_ready"], n + 1)
                G_.tensor_tensor(hob[:], xa[:], ob_bc[:, None, :].broadcast_to([P, NT, D]), ALU.add) \
                    .then_inc(s["hob_ready"], 1)

            def scatter(g):
                pool.wait_ge(s["pos_ready"], g + 1)
                pool.wait_ge(s["weights_ready"], g * 2 + 2)
                alone(pool)
                for t in range(NT):
                    for c_ in range(2):
                        G_.indirect_dma_start(slots, bass.IndirectOffsetOnAxis(ap=pos_u[:, c_ * NT + t:c_ * NT + t + 1], axis=0),
                                              h3[:, t, :], None).then_inc(s["scattered"], 16)

            def residual(a):
                pool.wait_ge(s["xn2_ready"], a + 1)
                step(G_.tensor_tensor(h2[:], h2[:], f2b_bc[:, None, :].broadcast_to([P, NT, D]), ALU.add))
                settle()
                for b in range(B):
                    part = h2[:, TT * b:TT * b + TT, :]
                    step(G_.tensor_tensor(part, part, mod[:, b, GA:GA + 1, :].broadcast_to([P, TT, D]), ALU.mult))
                settle()
                pool.wait_ge(s["xr_loaded"], a * 32 + 32)
                G_.tensor_tensor(res[:], res[:], h2[:], ALU.add).then_inc(s["res_ready"], 1)

            def load_up(e):
                G_.dma_start(raw_up[:], w1[e].rearrange("(k p) n -> p k n", p=P)).then_inc(s["up_loaded"], 16)

            def load_down(e):
                G_.dma_start(raw_down[:], w2[e].rearrange("(m p) n -> p m n", p=P)).then_inc(s["down_loaded"], 16)

            def iteration(i, A, F, G, NEXT):
                if F:
                    residual(i - 1)
                if G:
                    power(NORM_B, i - 2)
                if NEXT:
                    power(NORM_A, i + 1)
                    h_of(i + 1)
                    power(NORM_1, i + 1)
                if A:
                    power(NORM_2, i)
                if NEXT:
                    h_plus_ob(i + 1)
                if G and not F:
                    pool.wait_ge(s["gate_done"], NG)
                    load_up(1)
                if G:
                    scatter(i - 2)

            pool.wait_ge(s["dve_step"], 7)
            power(0, 0)
            pool.wait_ge(s["mod_ready"], 2)
            h_of(0)
            power(1, 0)
            pool.wait_ge(s["wvo_mm"], 2)
            pool.wait_ge(s["ld_attn"], 16 * 5)
            h_plus_ob(0)
            pool.wait_ge(s["mod_ready"], 6)
            pool.wait_ge(s["ld_ffn"], 16 * 6)
            pool.wait_ge(s["wprep"], 8)

            iteration(0, True, False, False, True)
            iteration(1, True, True, False, True)
            start = steps[0]
            with pool.Fori(2, NG - 1) as i:
                base[0] = (i - 2) * POOL_ROUND
                iteration(i, True, True, True, True)
            assert steps[0] - start == POOL_ROUND, steps[0] - start
            base[0] = (NG - 4) * POOL_ROUND
            iteration(NG - 1, True, True, True, False)

            iteration(NG, False, True, True, False)
            pool.wait_ge(s["act_split"], NG * MH)
            load_down(1)
            iteration(NG + 1, False, False, True, False)
            pool.drain().then_inc(s["phase1_over"], 2)

            pool.wait_ge(s["phase1_over"], 5)
            pool.wait_ge(s["table_ready"], 1)

            pool.wait_ge(s["x2_stored"], 16 * B * NG)
            for t in range(2):
                G_.indirect_dma_start(out.rearrange("b n d -> (b n) d"),
                                      bass.IndirectOffsetOnAxis(ap=skip_u[:, 0:1], axis=0),
                                      pad_rows[:, t, 0:D], None, bounds_check=T - 1, oob_is_err=False,
                                      compute_op=ALU.add).then_inc(s["summed"], 16)
            pool.wait_ge(s["first_set"], 2)
            G_.memset(e2[:], 0.0).then_inc(s["down_ready"], 1)
            with pool.Fori(0, E // 2) as pair:
                for w in (0, 1):
                    e = pair * 2 + w
                    tiles = pool.value_load(table[0:1, 1, bass.ds(e, 1)], min_val=1, max_val=T // TR)
                    first = pool.value_load(table[0:1, 2, bass.ds(e, 1)], min_val=1, max_val=2 * T // TR + E)
                    pool.wait_ge(s["down_loaded"], e * 16 + 16)
                    pool.wait_ge(s["l2_done"], first * 2)
                    alone(pool)
                    o = 1 - w
                    G_.tensor_copy(down_hi[o][:], raw_down[:]).then_inc(s["down_hi_ready"], 1)
                    pool.wait_ge(s["up_ready"], e + 2)
                    alone(pool)
                    load_up((e + 2) % E)
                    pool.wait_ge(s["down_hi_ready"], e + 1)
                    G_.tensor_tensor(down_lo[o][:], raw_down[:], down_hi[o][:].bitcast(F32), ALU.subtract) \
                        .then_inc(s["down_ready"], 1)
                    pool.wait_ge(s["down_ready"], e + 2)
                    alone(pool)
                    load_down((e + 2) % E)
                    pool.wait_ge(s["summed"], first * 32)
                    alone(pool)
                    with pool.Fori(0, tiles) as i:
                        for t in range(2):
                            pool.wait_ge(s["y_ready"], (first + i) * 2 + t + 1)
                            alone(pool)
                            G_.indirect_dma_start(out.rearrange("b n d -> (b n) d"),
                                                  bass.IndirectOffsetOnAxis(ap=tok_u[:, t:t + 1], axis=0),
                                                  y[:, t, :], None, bounds_check=T - 1, oob_is_err=False,
                                                  compute_op=ALU.add).then_inc(s["summed"], 16)
            pool.wait_ge(s["up_loaded"], 16 * (E + 1))
            pool.wait_ge(s["down_loaded"], 16 * (E + 1))


OUT_SHAPE = (2, 2048, 256)


def kernel(**inputs):
    import concourse.bacc as bacc
    from concourse.bass_utils import run_bass_kernel_spmd

    def given(name):
        return np.asarray(inputs["L0_" + name])

    def columns(v, n=P):
        return v.reshape(-1, n).T

    layout = {
        "x": given("attn_x"),
        "c": given("c").reshape(2, 2, P).transpose(2, 1, 0),
        "wmod": given("wmod"),
        "wqk": np.concatenate([given("attn_q_w"), given("attn_k_w")], 0).T,
        "qk_b": columns(np.concatenate([given("attn_q_b"), given("attn_k_b")], 0)),
        "ln1_w": columns(given("attn_ln1_w")),
        "ln1_b": columns(given("attn_ln1_b")),
        "v_w": given("attn_v_w"),
        "v_b": columns(given("attn_v_b")),
        "o_w": given("attn_o_w").T,
        "o_b": given("attn_o_b"),
        "ln2_w": columns(given("attn_ln2_w")),
        "ln2_b": columns(given("attn_ln2_b")),
        "f1": given("attn_f1_w").T,
        "f1_b": columns(given("attn_f1_b")),
        "f2": given("attn_f2_w").T,
        "f2_b": given("attn_f2_b"),
        "gate": given("ffn_gate_w").T,
        "w1": given("ffn_w1").transpose(0, 2, 1),
        "b1": given("ffn_b1").reshape(8, 8, P).transpose(2, 0, 1),
        "w2": given("ffn_w2").transpose(0, 2, 1),
        "b2": given("ffn_b2"),
    }
    nc = bacc.Bacc("TRN2", target_bir_lowering=False, num_devices=1)
    arrays, args = {}, []
    for name, a in layout.items():
        a = np.ascontiguousarray(a)
        arrays["in_" + name] = a
        args.append(nc.dram_tensor("in_" + name, a.shape, mybir.dt.from_np(a.dtype), kind="ExternalInput").ap())
    out = nc.dram_tensor("out_0", OUT_SHAPE, F32, kind="ExternalOutput").ap()
    adaln_moe_program(nc, *args, out)
    r = run_bass_kernel_spmd(nc, [arrays], core_ids=[0])
    return r.results[0]["out_0"]
```

```python
from contextlib import ExitStack

import numpy as np

import concourse.bass as bass
from concourse import mybir

F32 = mybir.dt.float32
F32R = mybir.dt.float32r
BF16 = mybir.dt.bfloat16
I32 = mybir.dt.int32
U32 = mybir.dt.uint32
ALU = mybir.AluOpType
ACT = mybir.ActivationFunctionType
AX_X = mybir.AxisListType.X

P = 128
LN_EPS = 1e-5
ATTN_EPS = 1e-6
DVE_ROUND = 67
POOL_ROUND = 9


def adaln_moe_program(nc, x, c, wmod, wqk, qk_b, ln1_w, ln1_b, v_w, v_b, o_w, o_b, ln2_w, ln2_b,
                      f1, f1_b, f2, f2_b, gate, w1, b1, w2, b2, out):
    B, N, D = x.shape
    KD = D // P
    H = f1.shape[-1]
    MH = H // P
    E = w1.shape[0]
    T = B * N
    TT = 2
    NT = B * TT
    GB = TT * P
    GW = NT * P
    NG = N // GB
    NF = wqk.shape[-1] // 2
    DV = D + 2
    META = D
    ROW = D + 8
    TR = 2 * P
    CAP = T + TR
    assert B == 2 and KD == 2 and MH == 8 and E == 8 and 2 * NF == P and NG >= 4

    slots = nc.dram_tensor("slots", (E * CAP, ROW), F32, kind="Internal").ap()

    with ExitStack() as ctx:
        def sb(name, shape, dt=F32):
            return ctx.enter_context(nc.sbuf_tensor(name, shape, dt))

        at = {}

        def sb_marked(name, shape, dt=F32):
            t = sb(name, shape, dt)
            at[name] = nc.sbuf_base - int(np.prod(shape[1:])) * 4
            return t

        def sb_over(name, shape, under, off=0):
            return nc.alloc_sbuf_tensor_at(name, shape, F32, offset=at[under] + off)

        def bank(name):
            return ctx.enter_context(nc.psum_tensor(name, [P, 512], F32))

        def sem(name):
            return ctx.enter_context(nc.semaphore(name))

        wqk_hi, wqk_lo = (sb(f"wqk_{s}", [P, KD, 2 * NF], F32R) for s in ("hi", "lo"))
        wvo_hi, wvo_lo = (sb(f"wvo_{s}", [P, KD, D], F32R) for s in ("hi", "lo"))
        up_hi = [sb(f"up_hi{s}", [P, KD, H], F32R) for s in (0, 1)]
        up_lo = [sb_marked(f"up_lo{s}", [P, KD, H], F32R) for s in (0, 1)]
        down_hi = [sb(f"down_hi{s}", [P, MH, D], F32R) for s in (0, 1)]
        down_lo = [sb_marked(f"down_lo{s}", [P, MH, D], F32R) for s in (0, 1)]
        FFN = 1
        raw_up = sb("raw_up", [P, KD, H])
        raw_down = sb("raw_down", [P, MH, D])
        gate_sb = sb("gate_sb", [P, KD, E])

        mod = sb("mod", [P, B, 6, D])
        SA, CA, GA, SB_, CB, GATE_B = range(6)
        b2_all = mod[:, :, 0:4, :]
        ob_bc = sb("ob_bc", [P, D])
        f2b_bc = sb("f2b_bc", [P, D])
        bvo_bc = sb("bvo_bc", [P, D])
        gb_bc = sb("gb_bc", [P, 2, D])

        vec = sb("vec", [P, 16])
        LN1W, LN1B, LN2W, LN2B, VB = (slice(KD * n, KD * n + KD) for n in range(5))
        qkb = sb("qkb", [P, 2])
        f1b = sb("f1b", [P, MH])
        b1_all = sb("b1_all", [P, E, MH])
        b1_cur = sb("b1_cur", [P, MH])
        b2_cur = sb("b2_cur", [P, D])

        ones = sb("ones", [P, P])
        ident = sb("ident", [P, P])
        causal = sb("causal", [P, 3 * P])
        below = sb("below", [P, P], BF16)
        ones_bf = sb("ones_bf", [P, P], BF16)
        expert_id = sb("expert_id", [P, E])
        slot_base = sb("slot_base", [P, E])
        neg_half = sb("neg_half", [P, NT])

        xa = sb("xa", [P, NT, D])
        hob = sb("hob", [P, NT, D])
        xn1 = sb("xn1", [P, NT, D])
        xt1_hi, xt1_lo = (sb(f"xt1_{s}", [P, KD, GW], F32R) for s in ("hi", "lo"))
        xt2_hi = sb_marked("xt2_hi", [P, KD, GW], F32R)
        xt2_lo = sb("xt2_lo", [P, KD, GW], F32R)
        h3t = raw_up[:, 0, :].rearrange("p (k n) -> p k n", k=KD)
        probs = raw_up[:, 1, 0:2 * 384].rearrange("p (b n) -> p b n", b=B)
        elu = sb("elu", [P, GW])
        qk = sb("qk", [P, GW])
        kz = sb("kz", [P, GW])
        kt = sb("kt", [P, NT, P])
        val = sb("val", [P, NT, DV])
        state = sb("state", [P, B, DV])
        h2 = sb("h2", [P, NT, D])
        xn2 = sb("xn2", [P, NT, D])
        res = sb("res", [P, NT, D])
        x2 = sb("x2", [P, NT, D])
        h3 = sb("h3", [P, NT, ROW])
        act_hi = sb_marked("act_hi", [P, MH, GW], F32R)
        act_lo = sb_marked("act_lo", [P, MH, GW], F32R)
        RING = 4
        gelu_ring = raw_down[:, :, :].rearrange("p (r m) d -> p r (m d)", r=RING)
        stats = sb("stats", [P, NT, 6])
        mv = [sb(f"mv{n}", [P, NT, 2]) for n in range(4)]
        neg_mean = [sb(f"neg_mean{n}", [P, NT]) for n in range(4)]
        shift = [sb(f"shift{n}", [P, NT]) for n in range(4)]
        ve = [sb(f"ve{n}", [P, NT]) for n in range(4)]
        rstd = [sb(f"rstd{n}", [P, NT]) for n in range(4)]
        rden = sb("rden", [P, NT])
        logits = sb("logits", [P, NT, E])
        top = sb("top", [P, NT, 8])
        top_at = sb("top_at", [P, NT, 8], U32)
        gap = sb("gap", [P, NT])
        e2 = sb("e2", [P, NT])
        e2p1 = sb("e2p1", [P, NT])
        chosen = sb("chosen", [P, 2, NT, E])
        picked = sb("picked", [P, NT, E], BF16)
        totals = sb("totals", [P, NT, E])
        place = sb("place", [P, NT, E])
        place2 = sb("place2", [P, 2, NT, E])
        pos = sb("pos", [P, 2 * NT])
        pos_u = sb("pos_u", [P, 2 * NT], U32)
        next_slot = sb("next_slot", [P, E])
        token = sb("token", [P, NT])
        cnt_f = sb("cnt_f", [P, 3, E])
        cnt_i = sb("cnt_i", [P, 3, E], I32)
        table = sb("table", [P, 3, E], I32)

        rows = hob[:, :, :].rearrange("p t d -> p (t d)")[:, 0:2 * ROW].rearrange("p (t r) -> p t r", t=2)
        pad_rows = sb("pad_rows", [P, 2, ROW])
        skip_u = sb("skip_u", [P, 1], U32)
        meta = sb("meta", [P, 2, 8])
        cur_e = sb("cur_e", [P, 1])
        is_e = sb("is_e", [P, 2, 2])
        w_two = sb("w_two", [P, 2, 2])
        w_row = sb("w_row", [P, 2])
        tok_u = sb("tok_u", [P, 2], U32)
        g_row = xn2[:, 0:2, :]
        y = xn1[:, 0:2, :]
        r_ring = h2[:, :, :].rearrange("p t d -> p (t d)").rearrange("p (r n) -> p r n", n=TR)
        r_hi = act_hi[:, :, 0:TR]
        r_lo = act_lo[:, :, 0:TR]
        rt_hi = xt1_hi[:, :, 0:TR]
        rt_lo = xt1_lo[:, :, 0:TR]

        wmod_raw = sb_over("wmod_raw", [P, KD, 6 * D], "act_lo")
        first_up = sb_over("first_up", [P, KD, H], "up_lo0")
        first_down = sb_over("first_down", [P, MH, D], "down_lo0")
        v_raw = x2[:, 0:2, :]
        o_raw = x2[:, 2:4, :]
        wqk_raw = res[:, 0, :].rearrange("p (k n) -> p k n", k=KD)
        wvo_raw = hob[:, 0:2, :]
        rep = sb_over("rep", [P, 8, P], "xt2_hi")
        cvec = sb("cvec", [P, KD, B])
        csig = sb("csig", [P, KD, B])

        TP = [bank("tp0"), bank("tp1")]
        AT = [bank("at0"), bank("at1"), bank("at2")]
        FF = [bank("ff0"), bank("ff1")]
        YP = bank("yp")
        mod_bank = [TP[0], TP[1], FF[0], FF[1], FF[0], FF[1]]
        F1B = slice(D + 8, D + 8 + MH)
        down_bank = [FF[0], FF[1], AT[0], YP]
        carry_bank = [TP[1], YP]
        up_bank = [FF[0], FF[1], AT[0], AT[1]]
        y_bank = [YP, AT[2]]

        s = {}

        def S(name):
            if name not in s:
                s[name] = sem(name)
            return s[name]

        for name in """ld_c ld_mod ld_mod_rest ld_vec ld_attn ld_ffn ld_first ld_rows consts mod_w mod_c silu_e silu_rep mod_mm mod_copied mod_ready
                prep_vec wvo_mm wvo_raw_ready wprep ffn_bias ffn_bias_mm bias_ready first_hi first_set pool_step dve_step
                x_loaded xr_loaded x2_stored scattered
                t1_done t2_done t3_done qk_done v_done kt_done s_done av_done kv_done ff1_done ff2_done
                gate_done rank_done t1_hi t2_hi t3_copied elu_exp gate_exp gelu_done kt_copied
                t1_lo t2_lo xa_normed h_ready hob_ready xn1_ready elu_min qk_ready
                v_ready act_split gap_ready picked_ready pos_ready weights_ready masked h2_ready state_ready xn2_ready
                ff2_read x2_ready h3_ready res_ready phase1_over
                table_ready padded rows_loaded up_loaded down_loaded up_hi_ready up_ready down_hi_ready down_ready rt_done l1_done l2_done relu_done rt_hi_done
                r_split rt_lo_done meta_read y_ready summed b2_loaded gb_ready pads_ready act_step
                passed ve_a_ready ve_1_ready ve_2_ready ve_b_ready shift_a_ready shift_1_ready shift_2_ready shift_b_ready h3_normed""".split():
            S(name)

        NORM_A, NORM_1, NORM_2, NORM_B = range(4)
        VE = ["ve_a_ready", "ve_1_ready", "ve_2_ready", "ve_b_ready"]
        SHIFTED = ["shift_a_ready", "shift_1_ready", "shift_2_ready", "shift_b_ready"]
        NORMED = ["xa_normed", "xn1_ready", "xn2_ready", "h3_normed"]

        def alone(eng):
            eng.sem_inc(s["passed"], 1)

        def group_of(src, b, g):
            return src.rearrange("b (g t p) d -> b g p t d", t=TT, p=P)[b, g]

        def bc(ap, shape):
            return ap.broadcast_to(shape)

        def flat(ap):
            return ap

        def pad(eng, e):
            n = eng.value_load(table[0:1, 0, e:e + 1], min_val=0, max_val=T)
            eng.dma_start(slots[bass.ds(n + e * CAP, TR), :].rearrange("(s p) r -> p s r", p=P),
                          pad_rows[:]).then_inc(s["padded"], 16)

        block = ctx.enter_context(nc.Block())

        @block.sync
        def _(sp):
            wmod_in = wmod.rearrange("(k p) n -> p k n", p=P)
            sp.dma_start(cvec[:], c).then_inc(s["ld_c"], 16)
            sp.dma_start(wmod_raw[:, :, 0:2 * D], wmod_in[:, :, 0:2 * D]).then_inc(s["ld_mod"], 16)
            for b in range(B):
                sp.dma_start(xa[:, TT * b:TT * b + TT, :], group_of(x, b, 0)).then_inc(s["x_loaded"], 16)
            for k, v in ((LN1W, ln1_w), (LN1B, ln1_b), (LN2W, ln2_w), (LN2B, ln2_b), (VB, v_b)):
                sp.dma_start(vec[:, k], v).then_inc(s["ld_vec"], 16)
            sp.dma_start(wqk_raw, wqk.rearrange("(k p) n -> p k n", p=P)).then_inc(s["ld_attn"], 16)
            sp.dma_start(v_raw, v_w.rearrange("(k p) n -> p k n", p=P)).then_inc(s["ld_attn"], 16)
            sp.dma_start(o_raw, o_w.rearrange("(k p) n -> p k n", p=P)).then_inc(s["ld_attn"], 16)
            sp.dma_start(qkb[:, 0:1], qk_b).then_inc(s["ld_attn"], 16)
            sp.dma_start(ob_bc[:], o_b.partition_broadcast(P)).then_inc(s["ld_attn"], 16)
            sp.dma_start(wmod_raw[:, :, 2 * D:6 * D], wmod_in[:, :, 2 * D:6 * D]).then_inc(s["ld_mod_rest"], 16)
            sp.dma_start(raw_up[:], f1.rearrange("(k p) n -> p k n", p=P)).then_inc(s["ld_ffn"], 16)
            sp.dma_start(f1b[:], f1_b).then_inc(s["ld_ffn"], 16)
            sp.dma_start(raw_down[:], f2.rearrange("(m p) n -> p m n", p=P)).then_inc(s["ld_ffn"], 16)
            sp.dma_start(f2b_bc[:], f2_b.partition_broadcast(P)).then_inc(s["ld_ffn"], 16)
            sp.dma_start(gate_sb[:], gate.rearrange("(k p) n -> p k n", p=P)).then_inc(s["ld_ffn"], 16)
            sp.dma_start(b1_all[:], b1).then_inc(s["ld_ffn"], 16)
            sp.dma_start(first_up[:], w1[0].rearrange("(k p) n -> p k n", p=P)).then_inc(s["ld_first"], 16)
            sp.dma_start(first_down[:], w2[0].rearrange("(m p) n -> p m n", p=P)).then_inc(s["ld_first"], 16)

            def load_x(n):
                sp.wait_ge(s["xn1_ready"], n * B)
                sp.wait_ge(s["hob_ready"], n)
                for b in range(B):
                    sp.dma_start(xa[:, TT * b:TT * b + TT, :], group_of(x, b, n)).then_inc(s["x_loaded"], 16)

            def load_residual(a):
                sp.wait_ge(s["x2_ready"], a * B)
                for b in range(B):
                    sp.dma_start(res[:, TT * b:TT * b + TT, :], group_of(x, b, a)).then_inc(s["xr_loaded"], 16)

            def store_x2(f):
                sp.wait_ge(s["x2_ready"], f * B + B)
                for b in range(B):
                    sp.dma_start(group_of(out, b, f), x2[:, TT * b:TT * b + TT, :]).then_inc(s["x2_stored"], 16)

            load_x(1)
            sp.wait_ge(s["wprep"], 4)
            load_residual(0)
            load_x(2)
            store_x2(0)
            load_residual(1)
            with sp.Fori(2, NG - 1) as i:
                load_x(i + 1)
                store_x2(i - 1)
                load_residual(i)
            store_x2(NG - 2)
            load_residual(NG - 1)
            store_x2(NG - 1)

            sp.wait_ge(s["h3_ready"], NG)
            sp.wait_ge(s["res_ready"], NG)
            for e in range(E):
                sp.dma_start(b2_all[:, e // 4, e % 4, :], b2[e].partition_broadcast(P)).then_inc(s["b2_loaded"], 16)

            sp.wait_ge(s["table_ready"], 1)
            sp.wait_ge(s["pads_ready"], 3)
            for e in range(E // 2):
                pad(sp, e)
            sp.wait_ge(s["padded"], 16 * E)
            sp.wait_ge(s["scattered"], 16 * 2 * NT * NG)
            sp.wait_ge(s["x2_stored"], 16 * B * NG)
            with sp.Fori(0, E) as e:
                tiles = sp.value_load(table[0:1, 1, bass.ds(e, 1)], min_val=1, max_val=T // TR)
                first = sp.value_load(table[0:1, 2, bass.ds(e, 1)], min_val=1, max_val=2 * T // TR + E)
                with sp.Fori(0, tiles) as i:
                    sp.wait_ge(s["rt_done"], first + i)
                    sp.wait_ge(s["meta_read"], first + i)
                    sp.dma_start(rows, slots[bass.ds(e * CAP + i * TR, TR), :].rearrange("(s p) r -> p s r", p=P)) \
                        .then_inc(s["rows_loaded"], 16)
            tiles = sp.value_load(table[0:1, 1, E - 1:E], min_val=1, max_val=T // TR)
            first = sp.value_load(table[0:1, 2, E - 1:E], min_val=1, max_val=2 * T // TR + E)
            sp.wait_ge(s["rt_done"], first + tiles)
            sp.wait_ge(s["meta_read"], first + tiles)
            sp.dma_start(rows, slots[0:TR, :].rearrange("(s p) r -> p s r", p=P)).then_inc(s["rows_loaded"], 16)
            sp.wait_ge(s["summed"], (first + tiles) * 32)
            sp.wait_ge(s["rows_loaded"], (first + tiles) * 16 + 16)
            alone(sp)

        @block.tensor
        def _(pe):
            def product(dst, lhs, rhs, chunks):
                last = None
                for k in range(chunks):
                    lh, ll = lhs(k)
                    rh, rl = rhs(k)
                    pe.matmul(dst, lh, rh, start=(k == 0), stop=False)
                    pe.matmul(dst, lh, rl, start=False, stop=False)
                    last = pe.matmul(dst, ll, rh, start=False, stop=(k == chunks - 1))
                return last

            for name, per_tile in (("rt_done", 1), ("l1_done", MH), ("l2_done", 2)):
                pe.sem_inc(s[name], per_tile)
            pe.wait_ge(s["ld_mod"], 16)
            pe.wait_ge(s["silu_rep"], KD * B)

            def mod_products(n, b):
                for k in range(KD):
                    last = pe.matmul(mod_bank[2 * n + b][:], rep[:, B * k + b, :], wmod_raw[:, k, 512 * n:512 * n + 512],
                                     start=(k == 0), stop=(k == KD - 1))
                last.then_inc(s["mod_mm"], 1)

            for b in range(B):
                mod_products(0, b)
            pe.wait_ge(s["ld_attn"], 16 * 5)
            for k in range(KD):
                for n in range(KD):
                    last = pe.matmul(FF[1][:, D * k:D * k + D], v_raw[:, n, P * k:P * k + P], o_raw[:, n, :],
                                     start=(n == 0), stop=(n == KD - 1))
            last.then_inc(s["wvo_mm"], 1)
            pe.wait_ge(s["ld_vec"], 16 * 5)
            for k in range(KD):
                last = pe.matmul(YP[:, D:D + 1], wqk_raw[:, k, :], vec[:, LN1B.start + k:LN1B.start + k + 1],
                                 start=(k == 0), stop=(k == KD - 1))
            pe.wait_ge(s["wvo_raw_ready"], 1)
            pe.wait_ge(s["prep_vec"], 2 * KD)
            for k in range(KD):
                pe.matmul(YP[:, 0:D], rep[:, 4 + k, :], wvo_raw[:, k, :], start=(k == 0), stop=False)
            for k in range(KD):
                last = pe.matmul(YP[:, 0:D], rep[:, 6 + k, :], o_raw[:, k, :], start=False, stop=(k == KD - 1))
            last.then_inc(s["wvo_mm"], 1)
            pe.wait_ge(s["ld_mod_rest"], 16)
            mod_products(1, 0)
            pe.wait_ge(s["wprep"], 4)
            mod_products(1, 1)

            def ffn_bias():
                pe.wait_ge(s["ld_ffn"], 16 * 6)
                for m in range(MH):
                    for k in range(KD):
                        last = pe.matmul(YP[:, F1B.start + m:F1B.start + m + 1], raw_up[:, k, P * m:P * m + P],
                                         vec[:, LN2B.start + k:LN2B.start + k + 1], start=(k == 0), stop=(k == KD - 1))
                last.then_inc(s["ffn_bias_mm"], 1)

            def transpose_group(src, banks, done):
                for k in range(KD):
                    for t in range(NT):
                        last = pe.transpose(banks[k][:, P * t:P * t + P], src[:, t, P * k:P * k + P], ident[:])
                    last.then_inc(s[done], 1)

            def t1(a, first=False):
                pe.wait_ge(s["xn1_ready"], a * B + B)
                if first:
                    pe.wait_ge(s["mod_ready"], 2)
                else:
                    pe.wait_ge(s["h2_ready"], a)
                    pe.wait_ge(s["state_ready"], a * B - 1)
                transpose_group(xn1, TP, "t1_done")

            def t2(f):
                pe.wait_ge(s["xn2_ready"], f * B + B)
                pe.wait_ge(s["h2_ready"], f + 1)
                transpose_group(xn2, [AT[1], AT[2]], "t2_done")

            def t3(g, A):
                pe.wait_ge(s["h3_ready"], g + 1)
                if A:
                    pe.wait_ge(s["t1_lo"], (g + 3) * KD)
                else:
                    pe.wait_ge(s["h2_ready"], NG)
                    pe.wait_ge(s["state_ready"], NG * B)
                transpose_group(h3, TP, "t3_done")

            def queries_keys(a):
                pe.wait_ge(s["t1_hi"], a * KD + KD)
                pe.wait_ge(s["t1_lo"], a * KD + KD)
                product(AT[0][:], lambda k: (wqk_hi[:, k, :], wqk_lo[:, k, :]),
                        lambda k: (xt1_hi[:, k, :], xt1_lo[:, k, :]), KD).then_inc(s["qk_done"], 1)

            def route(g):
                pe.wait_ge(s["t3_copied"], g * KD + KD)
                pe.wait_ge(s["x2_ready"], g * B + B)
                for t in range(NT):
                    for k in range(KD):
                        last = pe.matmul(YP[:, E * t:E * t + E], h3t[:, k, P * t:P * t + P], gate_sb[:, k, :],
                                         start=(k == 0), stop=(k == KD - 1))
                last.then_inc(s["gate_done"], 1)

            def values(a):
                for j in range(2):
                    for t in (2 * j, 2 * j + 1):
                        tok = slice(P * t, P * t + P)
                        last = product(AT[1 + j][:, D * (t % 2):D * (t % 2) + D],
                                       lambda k: (xt1_hi[:, k, tok], xt1_lo[:, k, tok]),
                                       lambda k: (wvo_hi[:, k, :], wvo_lo[:, k, :]), KD)
                    last.then_inc(s["v_done"], 1)

            def ffn_up(f, chunks, first=False):
                for m in chunks:
                    if m < 2:
                        if not first:
                            pe.wait_ge(s["ff2_read"], f * NT - NT + m + 1)
                    else:
                        pe.wait_ge(s["gelu_done"], f * MH + m - 1)
                    hid = slice(P * m, P * m + P)
                    product(FF[m % 2][:], lambda k: (up_hi[FFN][:, k, hid], up_lo[FFN][:, k, hid]),
                            lambda k: (xt2_hi[:, k, :], xt2_lo[:, k, :]), KD).then_inc(s["ff1_done"], 1)

            def ffn_down(f, tiles):
                for t in tiles:
                    if t < 2:
                        pe.wait_ge(s["gelu_done"], f * MH + MH - 1 + t)
                    tok = slice(P * t, P * t + P)
                    for m in range(MH):
                        if t == 0:
                            pe.wait_ge(s["act_split"], f * MH + m + 1)
                        first, last = m == 0, m == MH - 1
                        dst = down_bank[t][:, 0:D]
                        pe.matmul(dst, act_hi[:, m, tok], down_hi[FFN][:, m, :], start=first, stop=False)
                        pe.matmul(dst, act_hi[:, m, tok], down_lo[FFN][:, m, :], start=False, stop=False)
                        done = pe.matmul(dst, act_lo[:, m, tok], down_hi[FFN][:, m, :], start=False, stop=last)
                    done.then_inc(s["ff2_done"], 1)

            def keys_back(a):
                pe.wait_ge(s["qk_ready"], a + 1)
                for t in range(NT):
                    last = pe.transpose(AT[0][:, P * t:P * t + P], kz[:, P * t:P * t + P], ident[:])
                last.then_inc(s["kt_done"], 1)

            def scores(a):
                for b in range(B):
                    pe.wait_ge(s["v_ready"], a * B + b + 1)
                    q0 = GB * b
                    pe.matmul(AT[1 + b][:, 0:GB], kz[:, q0:q0 + P], qk[:, q0:q0 + GB], start=True, stop=True)
                    pe.matmul(AT[1 + b][:, GB:GB + P], kz[:, q0 + P:q0 + GB], qk[:, q0 + P:q0 + GB],
                              start=True, stop=True).then_inc(s["s_done"], 1)

            def ranks(g):
                pe.wait_ge(s["picked_ready"], g + 1)
                flat_picked = picked[:, :, :].rearrange("p t e -> p (t e)")
                pe.matmul(YP[:, 2 * NT * E:3 * NT * E], below[:], flat_picked, start=True, stop=True)
                pe.matmul(YP[:, 3 * NT * E:4 * NT * E], ones_bf[:], flat_picked, start=True, stop=True) \
                    .then_inc(s["rank_done"], 1)

            def attend(a):
                pe.wait_ge(s["kt_copied"], a + 1)
                for b, t, dst in ((0, 0, AT[0]), (0, 1, AT[1]), (1, 0, AT[2]), (1, 1, TP[0])):
                    pe.wait_ge(s["masked"], a * B + b + 1)
                    q0 = GB * b + P * t
                    pe.matmul(dst[:, 0:DV], probs[:, b, P * t:P * t + P], val[:, TT * b, :], start=True, stop=False)
                    if t:
                        pe.matmul(dst[:, 0:DV], probs[:, b, 2 * P:3 * P], val[:, TT * b + 1, :], start=False, stop=False)
                    pe.matmul(dst[:, 0:DV], qk[:, q0:q0 + P], state[:, b, :], start=False, stop=True) \
                        .then_inc(s["av_done"], 1)

            def carry(a, b):
                for t in range(TT):
                    last = pe.matmul(carry_bank[b][:, 0:DV], kt[:, TT * b + t, :], val[:, TT * b + t, :],
                                     start=(t == 0), stop=(t == TT - 1))
                last.then_inc(s["kv_done"], 1)

            def iteration(i, A, F, G, NEXT, first=False):
                if F:
                    pe.wait_ge(s["t2_hi"], (i - 1) * KD + KD)
                    pe.wait_ge(s["t2_lo"], (i - 1) * KD + KD)
                    if not G:
                        pe.wait_ge(s["mod_copied"], 4)
                    ffn_up(i - 1, range(0, 1), first=not G)
                if A:
                    if G:
                        pe.wait_ge(s["ff2_read"], (i - 2) * NT + 3)
                    queries_keys(i)
                    values(i)
                if F:
                    ffn_up(i - 1, range(1, 2), first=not G)
                if first:
                    ffn_bias()
                if A:
                    keys_back(i)
                    scores(i)
                if F:
                    ffn_up(i - 1, range(2, 5))
                if G:
                    t3(i - 2, A)
                if F:
                    ffn_up(i - 1, range(5, 6))
                if G:
                    route(i - 2)
                if A:
                    attend(i)
                if F:
                    ffn_up(i - 1, range(6, 7))
                if G:
                    ranks(i - 2)
                if F:
                    ffn_up(i - 1, range(7, 8))
                if A:
                    carry(i, 0)
                if F:
                    ffn_down(i - 1, (0,))
                if A:
                    if G:
                        pe.wait_ge(s["pos_ready"], i - 1)
                    carry(i, 1)
                if F:
                    ffn_down(i - 1, (1,))
                    if A:
                        pe.wait_ge(s["h2_ready"], i + 1)
                    ffn_down(i - 1, (2,))
                if first:
                    pe.wait_ge(s["mod_copied"], 2)
                    mod_products(2, 0)
                    mod_products(2, 1)
                if A:
                    t2(i)
                if F:
                    if A:
                        pe.wait_ge(s["state_ready"], i * B + B)
                    elif G:
                        pe.wait_ge(s["pos_ready"], i - 1)
                    ffn_down(i - 1, (3,))
                if NEXT:
                    t1(i + 1)

            pe.wait_ge(s["consts"], 1)
            t1(0, first=True)
            pe.wait_ge(s["wprep"], 6)
            iteration(0, True, False, False, True, first=True)
            pe.wait_ge(s["bias_ready"], 8)
            iteration(1, True, True, False, True)
            with pe.Fori(2, NG - 1) as i:
                iteration(i, True, True, True, True)
            iteration(NG - 1, True, True, True, False)
            iteration(NG, False, True, True, False)
            iteration(NG + 1, False, False, True, False)
            pe.drain().then_inc(s["phase1_over"], 1)

            def rows_back(g):
                pe.wait_ge(s["rows_loaded"], g * 16 + 16)
                pe.wait_ge(s["rt_lo_done"], g)
                for k in range(KD):
                    for t in range(2):
                        last = pe.transpose(TP[0][:, TR * k + P * t:TR * k + P * t + P], rows[:, t, P * k:P * k + P], ident[:])
                last.then_inc(s["rt_done"], 1)

            def expert_up(g, w):
                pe.wait_ge(s["rt_hi_done"], g + 1)
                pe.wait_ge(s["rt_lo_done"], g + 1)
                for m in range(MH):
                    pe.wait_ge(s["relu_done"], g * MH + max(0, m - 3))
                    hid = slice(P * m, P * m + P)
                    product(up_bank[m % 4][:, 0:TR], lambda k: (up_hi[w][:, k, hid], up_lo[w][:, k, hid]),
                            lambda k: (rt_hi[:, k, :], rt_lo[:, k, :]), KD).then_inc(s["l1_done"], 1)

            def expert_down(g, w):
                pe.wait_ge(s["y_ready"], g * 2)
                for t in range(2):
                    for m in range(MH):
                        if t == 0:
                            pe.wait_ge(s["r_split"], g * MH + m + 1)
                        dst = y_bank[t][:, 0:D]
                        row = slice(P * t, P * t + P)
                        pe.matmul(dst, r_hi[:, m, row], down_hi[w][:, m, :], start=(m == 0), stop=False)
                        pe.matmul(dst, r_hi[:, m, row], down_lo[w][:, m, :], start=False, stop=False)
                        last = pe.matmul(dst, r_lo[:, m, row], down_hi[w][:, m, :], start=False, stop=(m == MH - 1))
                    last.then_inc(s["l2_done"], 1)

            pe.wait_ge(s["table_ready"], 1)
            pe.wait_ge(s["phase1_over"], 5)
            rows_back(1)
            with pe.Fori(0, E // 2) as pair:
                for w in (0, 1):
                    tiles = pe.value_load(table[0:1, 1, bass.ds(pair * 2 + w, 1)], min_val=1, max_val=T // TR)
                    first = pe.value_load(table[0:1, 2, bass.ds(pair * 2 + w, 1)], min_val=1, max_val=2 * T // TR + E)
                    pe.wait_ge(s["up_ready"], pair * 2 + w + 1)
                    pe.wait_ge(s["down_ready"], pair * 2 + w + 1)
                    alone(pe)
                    with pe.Fori(0, tiles) as i:
                        g = first + i
                        expert_up(g, w)
                        rows_back(g + 1)
                        last = expert_down(g, w)

        @block.scalar
        def _(act):
            steps = [0]

            def step(ins):
                steps[0] += 1
                ins.then_inc(s["act_step"], 1)
                act.wait_ge(s["act_step"], steps[0])

            for name, per_tile in (("rt_hi_done", 1), ("relu_done", MH)):
                act.sem_inc(s[name], per_tile)
            act.wait_ge(s["ld_c"], 16)
            act.activation(csig[:], cvec[:], ACT.Exp, scale=-1.0).then_inc(s["silu_e"], 1)

            def normed(kind, n, src, dst):
                act.wait_ge(s[SHIFTED[kind]], n + 1)
                for t in range(NT):
                    last = act.activation(dst[:, t, 0:D], src[:, t, 0:D], ACT.Identity, bias=shift[kind][:, t:t + 1],
                                          scale=rstd[kind][:, t:t + 1])
                    if t == TT - 1:
                        last.then_inc(s[NORMED[kind]], 1)
                last.then_inc(s[NORMED[kind]], 1)

            def norm_x(n):
                normed(NORM_A, n, xa, xa)

            def norm_h(n):
                act.wait_ge(s["t1_done"], n * KD)
                normed(NORM_1, n, xa, xn1)

            def norm_2(a):
                act.wait_ge(s["t2_done"], a * KD)
                normed(NORM_2, a, h2, xn2)

            def norm_x2(g):
                act.wait_ge(s["t3_done"], g * KD)
                act.wait_ge(s["scattered"], g * (32 * NT))
                normed(NORM_B, g, x2, h3)

            norm_x(0)
            act.wait_ge(s["ld_vec"], 16 * 5)
            act.wait_ge(s["ld_ffn"], 16 * 6)
            for k in range(KD):
                act.activation(up_hi[FFN][:, k, :], raw_up[:, k, :], ACT.Identity,
                               scale=vec[:, LN2W.start + k:LN2W.start + k + 1]).then_inc(s["ffn_bias"], 1)

            def mod_copies(n):
                for b in range(B):
                    act.wait_ge(s["mod_mm"], 2 * n + b + 1)
                    act.activation(mod[:, b, 2 * n:2 * n + 2, :].rearrange("p j d -> p (j d)"), mod_bank[2 * n + b][:],
                                   ACT.Copy).then_inc(s["mod_copied"], 1)

            def down_heads():
                for n in range(2):
                    act.activation(down_hi[FFN][:, 4 * n:4 * n + 4, :], raw_down[:, 4 * n:4 * n + 4, :], ACT.Copy) \
                        .then_inc(s["ffn_bias"], 1)

            def head(hi, banks, done, sem_out, base):
                for k in range(KD):
                    act.wait_ge(s[done], base + k + 1)
                    act.activation(hi[:, k, :], banks[k][:], ACT.Copy).then_inc(s[sem_out], 1)

            def gelu(f, chunks):
                for m in chunks:
                    act.wait_ge(s["ff1_done"], f * MH + m + 1)
                    act.wait_ge(s["act_split"], f * MH + max(0, m - RING + 1))
                    act.activation(gelu_ring[:, m % RING, :], FF[m % 2][:], ACT.Gelu, bias=f1b[:, m:m + 1])
                    act.activation(act_hi[:, m, :], FF[m % 2][:], ACT.Gelu, bias=f1b[:, m:m + 1]) \
                        .then_inc(s["gelu_done"], 1)

            def iteration(i, A, F, G, NEXT, first=False):
                if A:
                    act.wait_ge(s["v_done"], i * 2)
                    head(xt1_hi, TP, "t1_done", "t1_hi", i * KD)
                if first:
                    norm_x(1)
                if A:
                    act.wait_ge(s["elu_min"], i + 1)
                    act.activation(elu[:], elu[:], ACT.Exp).then_inc(s["elu_exp"], 1)
                if first:
                    down_heads()
                if F:
                    act.wait_ge(s["ff2_done"], (i - 1) * NT)
                    gelu(i - 1, range(0, 2))
                if G:
                    norm_x2(i - 2)
                if F:
                    gelu(i - 1, range(2, 3))
                if A:
                    act.wait_ge(s["kt_done"], i + 1)
                    act.wait_ge(s["kv_done"], i * B)
                    act.activation(kt[:], AT[0][:].rearrange("p (t n) -> p t n", t=NT), ACT.Copy) \
                        .then_inc(s["kt_copied"], 1)
                if F:
                    gelu(i - 1, range(3, 5))
                if G:
                    head(h3t, TP, "t3_done", "t3_copied", (i - 2) * KD)
                if NEXT and not first:
                    norm_x(i + 1)
                if F:
                    gelu(i - 1, range(5, 8))
                if G:
                    act.wait_ge(s["gap_ready"], i - 1)
                    act.activation(e2[:], gap[:], ACT.Exp).then_inc(s["gate_exp"], 1)
                if first:
                    norm_h(1)
                if A:
                    norm_2(i)
                if first:
                    mod_copies(2)
                if NEXT and not first:
                    norm_h(i + 1)
                if A:
                    act.wait_ge(s["ff1_done"], i * MH)
                    head(xt2_hi, [AT[1], AT[2]], "t2_done", "t2_hi", i * KD)

            norm_h(0)
            mod_copies(1)
            iteration(0, True, False, False, True, first=True)
            act.wait_ge(s["bias_ready"], 8)
            iteration(1, True, True, False, True)
            with act.Fori(2, NG - 1) as i:
                iteration(i, True, True, True, True)
            iteration(NG - 1, True, True, True, False)
            iteration(NG, False, True, True, False)
            act.wait_ge(s["ld_first"], 32)
            act.activation(up_hi[0][:], first_up[:], ACT.Copy).then_inc(s["first_hi"], 1)
            act.activation(down_hi[0][:], first_down[:], ACT.Copy).then_inc(s["first_hi"], 1)
            iteration(NG + 1, False, False, True, False)
            act.drain().then_inc(s["phase1_over"], 1)

            act.wait_ge(s["table_ready"], 1)
            act.wait_ge(s["pads_ready"], 3)
            for e in range(E // 2, E):
                pad(act, e)
            act.wait_ge(s["phase1_over"], 5)

            def rows_head(g):
                act.wait_ge(s["rt_done"], g + 1)
                act.activation(rt_hi, TP[0][:].rearrange("p (k n) -> p k n", k=KD), ACT.Copy) \
                    .then_inc(s["rt_hi_done"], 1)

            rows_head(1)
            with act.Fori(0, E // 2) as pair:
                for w in (0, 1):
                    e = pair * 2 + w
                    tiles = act.value_load(table[0:1, 1, bass.ds(e, 1)], min_val=1, max_val=T // TR)
                    first = act.value_load(table[0:1, 2, bass.ds(e, 1)], min_val=1, max_val=2 * T // TR + E)
                    act.wait_ge(s["up_loaded"], e * 16 + 16)
                    act.activation(up_hi[1 - w][:], raw_up[:], ACT.Copy).then_inc(s["up_hi_ready"], 1)
                    act.wait_ge(s["relu_done"], first * MH)
                    act.activation(b1_cur[:], b1_all[:, bass.ds(e, 1), :].rearrange("p e m -> p (e m)"), ACT.Copy) \
                        .then_inc(s["act_step"], 1)
                    act.wait_ge(s["act_step"], e + 1)
                    with act.Fori(0, tiles) as i:
                        g = first + i
                        act.wait_ge(s["l2_done"], g * 2)
                        for m in range(MH):
                            act.wait_ge(s["l1_done"], g * MH + m + 1)
                            act.wait_ge(s["r_split"], g * MH + max(0, m - RING + 1))
                            act.activation(r_ring[:, m % RING, :], up_bank[m % 4][:, 0:TR], ACT.Relu,
                                           bias=b1_cur[:, m:m + 1])
                            act.activation(r_hi[:, m, :], up_bank[m % 4][:, 0:TR], ACT.Relu, bias=b1_cur[:, m:m + 1]) \
                                .then_inc(s["relu_done"], 1)
                        rows_head(g + 1)

        @block.vector
        def _(dve):
            steps = [0]
            base = [0]

            def step(ins):
                steps[0] += 1
                ins.then_inc(s["dve_step"], 1)

            def settle():
                dve.wait_ge(s["dve_step"], base[0] + steps[0])

            V = nc.vector
            for name, per_tile in (("meta_read", 1), ("r_split", MH), ("rt_lo_done", 1), ("y_ready", 2), ("up_ready", 1)):
                dve.sem_inc(s[name], per_tile)
            V.memset(ones[:], 1.0).then_inc(s["mod_c"], 1)
            step(V.memset(state[:], 0.0))
            step(V.memset(kz[:], 0.0))
            step(V.memset(val[:, :, D:DV], 1.0))
            step(V.memset(neg_half[:], -0.5))
            step(V.memset(ones_bf[:], 1.0))
            step(V.memset(h3[:, :, META:ROW], 0.0))
            settle()
            step(V.memset(h3[:, TT:NT, META + 5:META + 6], 1.0))
            dve.wait_ge(s["silu_e"], 1)
            step(V.tensor_scalar(csig[:], csig[:], 1.0, None, ALU.add))
            settle()
            step(V.reciprocal(csig[:], csig[:]))
            settle()
            step(V.tensor_tensor(csig[:], csig[:], cvec[:], ALU.mult))
            settle()
            dve.wait_ge(s["mod_c"], 1)
            for k in range(KD):
                for b in range(B):
                    V.tensor_scalar(rep[:, B * k + b, :], ones[:], csig[:, k, b:b + 1], None, ALU.mult) \
                        .then_inc(s["silu_rep"], 1)
            dve.wait_ge(s["ld_vec"], 16 * 5)
            for n, src in enumerate((LN1B, VB)):
                for k in range(KD):
                    V.tensor_scalar(rep[:, 4 + 2 * n + k, :], ones[:], vec[:, src.start + k:src.start + k + 1], None,
                                    ALU.mult).then_inc(s["prep_vec"], 1)

            def norm_stats(kind, n, src):
                for t in range(NT):
                    step(V.bn_stats(stats[:, t, :], src[:, t, 0:D]))
                settle()
                alone(dve)
                for t in range(NT):
                    step(V.bn_aggr(mv[kind][:, t, :], stats[:, t, :]))
                settle()
                dve.wait_ge(s[SHIFTED[kind]], n)
                V.tensor_scalar(neg_mean[kind][:], mv[kind][:, :, 0], -1.0, None, ALU.mult).then_inc(s[VE[kind]], 1)
                V.tensor_scalar(ve[kind][:], mv[kind][:, :, 1], LN_EPS, None, ALU.add).then_inc(s[VE[kind]], 1)

            def stats_x(n):
                dve.wait_ge(s["x_loaded"], n * 32 + 32)
                norm_stats(NORM_A, n, xa)

            def stats_h(n):
                dve.wait_ge(s["h_ready"], n + 1)
                norm_stats(NORM_1, n, xa)

            def stats_2(a):
                dve.wait_ge(s["h2_ready"], a + 1)
                norm_stats(NORM_2, a, h2)

            def stats_x2(g):
                dve.wait_ge(s["x2_ready"], g * B + B)
                norm_stats(NORM_B, g, x2)

            def modulate_x2(g):
                modulate(h3, g, "h3_normed", CB, SB_, "h3_ready")

            def modulate(rows_, n, normed, one_plus, shift_row, done):
                for b in range(B):
                    dve.wait_ge(s[normed], n * B + b + 1)
                    part = rows_[:, TT * b:TT * b + TT, 0:D]
                    step(V.tensor_tensor(part, part, mod[:, b, one_plus:one_plus + 1, :].broadcast_to([P, TT, D]), ALU.mult))
                settle()
                for b in range(B):
                    part = rows_[:, TT * b:TT * b + TT, 0:D]
                    last = V.tensor_tensor(part, part, mod[:, b, shift_row:shift_row + 1, :].broadcast_to([P, TT, D]),
                                           ALU.add)
                last.then_inc(s[done], 1)

            stats_x(0)
            for b in range(B):
                dve.wait_ge(s["mod_mm"], b + 1)
                step(V.tensor_copy(mod[:, b, SA, :], mod_bank[b][:, 0:D]))
                V.tensor_scalar(mod[:, b, CA, :], mod_bank[b][:, D:2 * D], 1.0, None, ALU.add).then_inc(s["mod_ready"], 1)

            def floor_gate(row, scratch, done):
                g = mod[:, :, row, :]
                step(V.tensor_scalar(scratch, g, 0.0, 2.0, ALU.is_ge, ALU.mult))
                settle()
                step(V.tensor_scalar(scratch, scratch, 1.0, None, ALU.subtract))
                settle()
                step(V.tensor_tensor(g, g, scratch, ALU.mult))
                settle()
                V.scalar_tensor_tensor(g, g, 0.25, scratch, ALU.max, ALU.mult).then_inc(s[done], 1)

            settle()
            dve.wait_ge(s["mod_ready"], 2)
            modulate(xa, 0, "xa_normed", CA, SA, "h_ready")
            dve.wait_ge(s["ld_attn"], 16 * 5)
            dve.wait_ge(s["ld_vec"], 16 * 5)
            for k in range(KD):
                step(V.tensor_scalar(elu[:, P * k:P * k + P], wqk_raw[:, k, :],
                                     vec[:, LN1W.start + k:LN1W.start + k + 1], None, ALU.mult))
            settle()
            ewqk = elu[:, 0:KD * P].rearrange("p (k n) -> p k n", k=KD)
            V.tensor_copy(wqk_hi[:], ewqk).then_inc(s["wprep"], 1)
            dve.wait_ge(s["wprep"], 1)
            V.tensor_tensor(wqk_lo[:], ewqk, wqk_hi[:].bitcast(F32), ALU.subtract).then_inc(s["wprep"], 1)
            dve.wait_ge(s["wvo_mm"], 1)
            V.tensor_copy(wvo_raw, FF[1][:].rearrange("p (k n) -> p k n", k=KD)).then_inc(s["wvo_raw_ready"], 1)
            for k in range(KD):
                step(V.tensor_scalar(h2[:, k, :], FF[1][:, D * k:D * k + D],
                                     vec[:, LN1W.start + k:LN1W.start + k + 1], None, ALU.mult))
            settle()
            V.tensor_copy(wvo_hi[:], h2[:, 0:2, :]).then_inc(s["wprep"], 1)
            dve.wait_ge(s["wprep"], 3)
            V.tensor_tensor(wvo_lo[:], h2[:, 0:2, :], wvo_hi[:].bitcast(F32), ALU.subtract).then_inc(s["wprep"], 1)
            dve.wait_ge(s["wprep"], 4)
            stats_h(0)
            dve.wait_ge(s["wvo_mm"], 2)
            V.tensor_copy(bvo_bc[:], YP[:, 0:D]).then_inc(s["wprep"], 1)
            step(V.tensor_tensor(qkb[:, 0:1], qkb[:, 0:1], YP[:, D:D + 1], ALU.add))
            settle()
            V.tensor_scalar(qkb[:, 1:2], qkb[:, 0:1], 1.0, None, ALU.add).then_inc(s["wprep"], 1)
            for k in range(KD):
                dve.wait_ge(s["ffn_bias"], k + 1)
                V.scalar_tensor_tensor(up_lo[FFN][:, k, :], raw_up[:, k, :], vec[:, LN2W.start + k:LN2W.start + k + 1],
                                       up_hi[FFN][:, k, :].bitcast(F32), ALU.mult, ALU.subtract) \
                    .then_inc(s["bias_ready"], 1)
            dve.wait_ge(s["consts"], 1)
            V.tensor_copy(next_slot[:], slot_base[:]).then_inc(s["bias_ready"], 1)
            dve.wait_ge(s["wprep"], 6)
            dve.wait_ge(s["bias_ready"], 3)

            def down_rests(pieces):
                for n in pieces:
                    dve.wait_ge(s["ffn_bias"], 3 + n // 2)
                    V.tensor_tensor(down_lo[FFN][:, 2 * n:2 * n + 2, :], raw_down[:, 2 * n:2 * n + 2, :],
                                    down_hi[FFN][:, 2 * n:2 * n + 2, :].bitcast(F32), ALU.subtract) \
                        .then_inc(s["bias_ready"], 1)

            def rest(hi, lo, banks, hi_done, lo_done, n):
                for k in range(KD):
                    dve.wait_ge(s[hi_done], n * KD + k + 1)
                    V.tensor_tensor(lo[:, k, :], banks[k][:], hi[:, k, :].bitcast(F32), ALU.subtract) \
                        .then_inc(s[lo_done], 1)

            def elu_min(a):
                dve.wait_ge(s["qk_done"], a + 1)
                V.tensor_scalar(elu[:], AT[0][:], qkb[:, 0:1], 0.0, ALU.add, ALU.min).then_inc(s["elu_min"], 1)

            def elu_max(a):
                dve.wait_ge(s["elu_exp"], a + 1)
                dve.wait_ge(s["av_done"], a * NT)
                step(V.scalar_tensor_tensor(qk[:], AT[0][:], qkb[:, 1:2], elu[:], ALU.add, ALU.max))
                settle()
                V.tensor_copy(kz[0:NF, :], qk[NF:P, :]).then_inc(s["qk_ready"], 1)

            def values_out(a):
                dve.wait_ge(s["kv_done"], a * B)
                for b in range(B):
                    dve.wait_ge(s["v_done"], a * B + b + 1)
                    V.tensor_tensor(val[:, TT * b:TT * b + TT, 0:D], AT[1 + b][:].rearrange("p (t n) -> p t n", t=TT),
                                    bvo_bc[:, None, :].broadcast_to([P, TT, D]), ALU.add).then_inc(s["v_ready"], 1)

            def split_act(f, chunks):
                for m in chunks:
                    dve.wait_ge(s["gelu_done"], f * MH + m + 1)
                    V.tensor_tensor(act_lo[:, m, :], gelu_ring[:, m % RING, :], act_hi[:, m, :].bitcast(F32),
                                    ALU.subtract).then_inc(s["act_split"], 1)

            def best_two(g):
                dve.wait_ge(s["gate_done"], g + 1)
                step(V.tensor_copy(logits[:], YP[:, 0:NT * E].rearrange("p (t e) -> p t e", t=NT)))
                settle()
                alone(dve)
                for t in range(NT):
                    step(V.max(top[:, t, :], logits[:, t, :]))
                settle()
                V.tensor_tensor(gap[:], top[:, :, 1], top[:, :, 0], ALU.subtract).then_inc(s["gap_ready"], 1)
                for t in range(NT):
                    step(V.max_index(top_at[:, t, :], top[:, t, :], logits[:, t, :]))
                settle()
                step(V.tensor_copy(h3[:, :, META:META + 2], top_at[:, :, 0:2]))
                step(V.tensor_copy(h3[:, :, META + 4], token[:]))
                settle()
                step(V.tensor_scalar(token[:], token[:], float(GB), None, ALU.add))
                for c_ in range(2):
                    step(V.tensor_tensor(chosen[:, c_, :, :], expert_id[:, None, :].broadcast_to([P, NT, E]),
                                         h3[:, :, META + c_:META + c_ + 1].broadcast_to([P, NT, E]), ALU.is_equal))
                settle()
                V.tensor_tensor(picked[:], chosen[:, 0], chosen[:, 1], ALU.add).then_inc(s["picked_ready"], 1)

            def gate_weights(g):
                dve.wait_ge(s["gate_exp"], g + 1)
                step(V.tensor_scalar(e2p1[:], e2[:], 1.0, None, ALU.add))
                settle()
                step(V.reciprocal(e2p1[:], e2p1[:]))
                settle()
                V.tensor_copy(h3[:, :, META + 2], e2p1[:]).then_inc(s["weights_ready"], 1)
                V.tensor_tensor(h3[:, :, META + 3], e2p1[:], e2[:], ALU.mult).then_inc(s["weights_ready"], 1)

            def slots_of(g):
                dve.wait_ge(s["rank_done"], g + 1)
                step(V.tensor_tensor(place[:], YP[:, 2 * NT * E:3 * NT * E].rearrange("p (t e) -> p t e", t=NT),
                                     next_slot[:, None, :].broadcast_to([P, NT, E]), ALU.add))
                step(V.tensor_copy(totals[:], YP[:, 3 * NT * E:4 * NT * E].rearrange("p (t e) -> p t e", t=NT)))
                settle()
                for t in range(NT):
                    if t < NT - 1:
                        step(V.tensor_tensor(place[:, t + 1:NT, :], place[:, t + 1:NT, :],
                                             totals[:, t:t + 1, :].broadcast_to([P, NT - 1 - t, E]), ALU.add))
                    step(V.tensor_tensor(next_slot[:], next_slot[:], totals[:, t, :], ALU.add))
                    settle()
                step(V.tensor_tensor(place2[:], chosen[:], place[:, None, :, :].broadcast_to([P, 2, NT, E]), ALU.mult))
                settle()
                step(V.tensor_reduce(pos[:], place2[:].rearrange("p c t e -> p (c t) e"), AX_X, ALU.add))
                settle()
                V.tensor_copy(pos_u[:], pos[:]).then_inc(s["pos_ready"], 1)

            def mask(a):
                for b in range(B):
                    dve.wait_ge(s["s_done"], a * B + b + 1)
                    V.tensor_tensor(probs[:, b, :], AT[1 + b][:, 0:3 * P], causal[:], ALU.mult).then_inc(s["masked"], 1)

            def attended(a):
                dve.wait_ge(s["hob_ready"], a + 1)
                dve.wait_ge(s["res_ready"], a)
                for t, bk in enumerate((AT[0], AT[1], AT[2], TP[0])):
                    dve.wait_ge(s["av_done"], a * NT + t + 1)
                    step(V.tensor_scalar(rden[:, t:t + 1], bk[:, D:D + 1], ATTN_EPS, None, ALU.add))
                settle()
                step(V.reciprocal(rden[:], rden[:]))
                settle()
                for t, bk in enumerate((AT[0], AT[1], AT[2], TP[0])):
                    last = V.scalar_tensor_tensor(h2[:, t, :], bk[:, 0:D], rden[:, t:t + 1], hob[:, t, :],
                                                  ALU.mult, ALU.add)
                last.then_inc(s["h2_ready"], 1)

            def carry_state(a, b):
                dve.wait_ge(s["kv_done"], a * B + b + 1)
                V.tensor_tensor(state[:, b, :], state[:, b, :], carry_bank[b][:, 0:DV], ALU.add).then_inc(s["state_ready"], 1)

            def tile_out(f, t):
                dve.wait_ge(s["ff2_done"], f * NT + t + 1)
                V.tensor_tensor(x2[:, t, :], down_bank[t][:, 0:D], mod[:, t // TT, GA, :], ALU.mult) \
                    .then_inc(s["ff2_read"], 1)

            def ffn_out(f):
                dve.wait_ge(s["x2_stored"], f * 32)
                dve.wait_ge(s["res_ready"], f + 1)
                for t in range(NT - 1):
                    tile_out(f, t)
                    if t == TT - 1:
                        add_residual(f, 0)

            def add_residual(f, b):
                dve.wait_ge(s["ff2_read"], f * NT + TT * b + TT)
                part = slice(TT * b, TT * b + TT)
                V.tensor_tensor(x2[:, part, :], x2[:, part, :], res[:, part, :], ALU.add).then_inc(s["x2_ready"], 1)

            def iteration(i, A, F, G, NEXT, first=False):
                if F:
                    rest(xt2_hi, xt2_lo, [AT[1], AT[2]], "t2_hi", "t2_lo", i - 1)
                if G:
                    tile_out(i - 2, NT - 1)
                if A:
                    rest(xt1_hi, xt1_lo, TP, "t1_hi", "t1_lo", i)
                if G:
                    add_residual(i - 2, 1)
                if first:
                    stats_x(1)
                if A:
                    elu_min(i)
                if G:
                    stats_x2(i - 2)
                if A:
                    elu_max(i)
                    values_out(i)
                if F:
                    split_act(i - 1, range(0, 2))
                if first:
                    dve.wait_ge(s["ffn_bias_mm"], 1)
                    V.tensor_tensor(f1b[:], f1b[:], YP[:, F1B], ALU.add).then_inc(s["bias_ready"], 1)
                if A:
                    mask(i)
                if F and A and not G:
                    dve.wait_ge(s["mod_copied"], 4)
                    step(V.tensor_scalar(mod[:, :, CB, :], mod[:, :, CB, :], 1.0, None, ALU.add))
                    floor_gate(GATE_B, gb_bc[:], "mod_ready")
                    dve.wait_ge(s["mod_ready"], 4)
                    step(V.tensor_copy(gb_bc[:, 0, :], mod[:, 0, GATE_B, :]))
                    step(V.tensor_tensor(gb_bc[:, 1, :], mod[:, 1, GATE_B, :], mod[:, 0, GATE_B, :], ALU.subtract))
                if G:
                    modulate_x2(i - 2)
                if first:
                    dve.wait_ge(s["mod_copied"], 2)
                    floor_gate(GA, gb_bc[:], "mod_ready")
                    stats_h(1)
                elif NEXT:
                    stats_x(i + 1)
                if F:
                    split_act(i - 1, range(2, 5))
                if G:
                    best_two(i - 2)
                if F:
                    split_act(i - 1, range(5, 6))
                if A:
                    attended(i)
                if F:
                    split_act(i - 1, range(6, 7))
                if G:
                    slots_of(i - 2)
                if F:
                    split_act(i - 1, range(7, 8))
                if A:
                    stats_2(i)
                    carry_state(i, 0)
                if G:
                    gate_weights(i - 2)
                if NEXT and not first:
                    stats_h(i + 1)
                if A:
                    carry_state(i, 1)
                if first:
                    down_rests(range(4))
                    dve.wait_ge(s["bias_ready"], 8)
                if F and not A:
                    dve.wait_ge(s["first_hi"], 1)
                    V.tensor_tensor(up_lo[0][:], first_up[:], up_hi[0][:].bitcast(F32), ALU.subtract) \
                        .then_inc(s["first_set"], 1)
                    dve.wait_ge(s["first_hi"], 2)
                    V.tensor_tensor(down_lo[0][:], first_down[:], down_hi[0][:].bitcast(F32), ALU.subtract) \
                        .then_inc(s["first_set"], 1)
                if F:
                    ffn_out(i - 1)

            iteration(0, True, False, False, True, first=True)
            iteration(1, True, True, False, True)
            start = steps[0]
            with dve.Fori(2, NG - 1) as i:
                base[0] = (i - 2) * DVE_ROUND
                iteration(i, True, True, True, True)
            assert steps[0] - start == DVE_ROUND, steps[0] - start
            base[0] = (NG - 4) * DVE_ROUND
            iteration(NG - 1, True, True, True, False)
            iteration(NG, False, True, True, False)
            iteration(NG + 1, False, False, True, False)
            step(V.tensor_tensor(cnt_f[:, 0, :], next_slot[:], slot_base[:], ALU.subtract))
            settle()
            step(V.tensor_scalar(cnt_f[:, 1, :], cnt_f[:, 0, :], float(TR - 1), None, ALU.add))
            settle()
            step(V.tensor_copy(cnt_i[:, 0:2, :], cnt_f[:, 0:2, :]))
            settle()
            step(V.tensor_single_scalar(cnt_i[:, 2, :], cnt_i[:, 1, :], TR.bit_length() - 1, ALU.logical_shift_right))
            settle()
            step(V.tensor_copy(cnt_f[:, 1, :], cnt_i[:, 2, :]))
            settle()
            step(V.tensor_scalar(cnt_f[:, 1, :], cnt_f[:, 1, :], 1.0, None, ALU.max))
            step(V.memset(cnt_f[:, 2, 0:1], 1.0))
            settle()
            for e in range(1, E):
                step(V.tensor_tensor(cnt_f[:, 2, e:e + 1], cnt_f[:, 2, e - 1:e], cnt_f[:, 1, e - 1:e], ALU.add))
                settle()
            V.tensor_copy(table[:], cnt_f[:]).then_inc(s["table_ready"], 1)
            step(V.memset(cur_e[:], -1.0))
            settle()
            dve.drain().then_inc(s["phase1_over"], 1)

            dve.wait_ge(s["table_ready"], 1)
            dve.wait_ge(s["phase1_over"], 5)
            dve.wait_ge(s["b2_loaded"], 16 * E)

            def rows_rest(g):
                dve.wait_ge(s["rt_hi_done"], g + 1)
                V.tensor_tensor(rt_lo, TP[0][:].rearrange("p (k n) -> p k n", k=KD), rt_hi.bitcast(F32),
                                ALU.subtract).then_inc(s["rt_lo_done"], 1)

            def take_meta(g):
                dve.wait_ge(s["rows_loaded"], g * 16 + 16)
                V.tensor_copy(meta[:], rows[:, :, META:ROW]).then_inc(s["meta_read"], 1)

            take_meta(1)
            rows_rest(1)
            done_before = steps[0]
            HEAD, TILE = 2, 8
            with dve.Fori(0, E // 2) as pair:
                for w in (0, 1):
                    e = pair * 2 + w
                    tiles = dve.value_load(table[0:1, 1, bass.ds(e, 1)], min_val=1, max_val=T // TR)
                    first = dve.value_load(table[0:1, 2, bass.ds(e, 1)], min_val=1, max_val=2 * T // TR + E)
                    dve.wait_ge(s["up_hi_ready"], e + 1)
                    V.tensor_tensor(up_lo[1 - w][:], raw_up[:], up_hi[1 - w][:].bitcast(F32), ALU.subtract) \
                        .then_inc(s["up_ready"], 1)
                    base[0] = (NG - 4) * DVE_ROUND + e * HEAD + (first - 1) * TILE
                    before = steps[0]
                    dve.wait_ge(s["y_ready"], first * 2)
                    step(V.tensor_copy(b2_cur[:], mod[:, bass.ds(e // 4, 1), bass.ds(e % 4, 1), :]
                                       .rearrange("p b j d -> p (b j d)")))
                    step(V.tensor_scalar(cur_e[:], cur_e[:], 1.0, None, ALU.add))
                    settle()
                    alone(dve)
                    assert steps[0] - before == HEAD
                    with dve.Fori(0, tiles) as i:
                        g = first + i
                        base[0] = (NG - 4) * DVE_ROUND + e * HEAD + (g - 1) * TILE
                        before = steps[0]
                        for m in range(MH):
                            dve.wait_ge(s["relu_done"], g * MH + m + 1)
                            V.tensor_tensor(r_lo[:, m, :], r_ring[:, m % RING, :], r_hi[:, m, :].bitcast(F32),
                                            ALU.subtract).then_inc(s["r_split"], 1)
                        dve.wait_ge(s["summed"], g * 32)
                        dve.wait_ge(s["meta_read"], g + 1)
                        step(V.tensor_scalar(is_e[:], meta[:, :, 0:2], cur_e[:, 0:1], None, ALU.is_equal))
                        settle()
                        step(V.tensor_tensor(w_two[:], is_e[:], meta[:, :, 2:4], ALU.mult))
                        settle()
                        step(V.tensor_reduce(w_row[:], w_two[:], AX_X, ALU.add))
                        step(V.tensor_copy(tok_u[:], meta[:, :, 4]))
                        for t in range(2):
                            step(V.scalar_tensor_tensor(g_row[:, t, :], gb_bc[:, 1, :], meta[:, t, 5:6],
                                                        gb_bc[:, 0, :], ALU.mult, ALU.add))
                        rows_rest(g + 1)
                        settle()
                        take_meta(g + 1)
                        for t in range(2):
                            dve.wait_ge(s["l2_done"], g * 2 + t + 1)
                            step(V.tensor_tensor(y[:, t, :], y_bank[t][:, 0:D], b2_cur[:], ALU.add))
                            settle()
                            V.scalar_tensor_tensor(y[:, t, :], y[:, t, :], w_row[:, t:t + 1], g_row[:, t, :],
                                                   ALU.mult, ALU.mult).then_inc(s["y_ready"], 1)
                        assert steps[0] - before == TILE, steps[0] - before
                        steps[0] = before
                    steps[0] = done_before

        @block.gpsimd
        def _(pool):
            G_ = nc.gpsimd
            steps = [0]
            base = [0]

            def step(ins):
                steps[0] += 1
                ins.then_inc(s["pool_step"], 1)

            def settle():
                pool.wait_ge(s["pool_step"], base[0] + steps[0])

            pool.sem_inc(s["rows_loaded"], 16)
            for t in (ident,):
                step(G_.memset(t[:], 0.0))
            step(G_.memset(causal[:], 1.0))
            step(G_.memset(below[:], 1.0))
            step(G_.memset(pad_rows[:], 0.0))
            settle()
            step(G_.affine_select(out=ident[:], in_=ident[:], compare_op=ALU.not_equal, fill=1.0, base=0,
                                  pattern=[[-1, P]], channel_multiplier=1))
            for o in (0, 2):
                step(G_.affine_select(out=causal[:, P * o:P * o + P], in_=causal[:, P * o:P * o + P],
                                      compare_op=ALU.is_ge, fill=0.0, base=0, pattern=[[1, P]], channel_multiplier=-1))
            step(G_.affine_select(out=below[:], in_=below[:], compare_op=ALU.is_gt, fill=0.0, base=0,
                                  pattern=[[1, P]], channel_multiplier=-1))
            step(G_.iota(expert_id[:], pattern=[[1, E]], base=0, channel_multiplier=0,
                         allow_small_or_imprecise_dtypes=True))
            step(G_.iota(slot_base[:], pattern=[[CAP, E]], base=0, channel_multiplier=0,
                         allow_small_or_imprecise_dtypes=True))
            step(G_.iota(token[:].rearrange("p (b t) -> p b t", b=B), pattern=[[N, B], [P, TT]], base=0,
                         channel_multiplier=1, allow_small_or_imprecise_dtypes=True))
            for t in range(2):
                G_.memset(pad_rows[:, t, META + 4:META + 5], float(T)).then_inc(s["pads_ready"], 1)
            step(G_.iota(skip_u[:], pattern=[[0, 1]], base=T, channel_multiplier=0))
            settle()
            G_.memset(e2[:], 0.0).then_inc(s["pads_ready"], 1)
            pool.drain().then_inc(s["consts"], 1)

            def power(kind, n):
                pool.wait_ge(s[NORMED[kind]], n * B)
                pool.wait_ge(s[VE[kind]], n * 2 + 2)
                step(G_.tensor_tensor(rstd[kind][:], ve[kind][:], neg_half[:], ALU.pow))
                settle()
                G_.tensor_tensor(shift[kind][:], neg_mean[kind][:], rstd[kind][:], ALU.mult) \
                    .then_inc(s[SHIFTED[kind]], 1)

            def modulate(dst, one_plus, shift, done):
                for b in range(B):
                    part = dst[:, TT * b:TT * b + TT, 0:D]
                    step(G_.tensor_tensor(part, part, mod[:, b, one_plus:one_plus + 1, :].broadcast_to([P, TT, D]), ALU.mult))
                settle()
                for b in range(B):
                    part = dst[:, TT * b:TT * b + TT, 0:D]
                    last = G_.tensor_tensor(part, part, mod[:, b, shift:shift + 1, :].broadcast_to([P, TT, D]), ALU.add)
                last.then_inc(s[done], 1)

            def h_of(n):
                pool.wait_ge(s["xa_normed"], n * B + B)
                modulate(xa, CA, SA, "h_ready")

            def h_plus_ob(n):
                pool.wait_ge(s["h2_ready"], n)
                pool.wait_ge(s["h_ready"], n + 1)
                G_.tensor_tensor(hob[:], xa[:], ob_bc[:, None, :].broadcast_to([P, NT, D]), ALU.add) \
                    .then_inc(s["hob_ready"], 1)

            def scatter(g):
                pool.wait_ge(s["pos_ready"], g + 1)
                pool.wait_ge(s["weights_ready"], g * 2 + 2)
                alone(pool)
                for t in range(NT):
                    for c_ in range(2):
                        G_.indirect_dma_start(slots, bass.IndirectOffsetOnAxis(ap=pos_u[:, c_ * NT + t:c_ * NT + t + 1], axis=0),
                                              h3[:, t, :], None).then_inc(s["scattered"], 16)

            def residual(a):
                pool.wait_ge(s["xn2_ready"], a * B + B)
                step(G_.tensor_tensor(h2[:], h2[:], f2b_bc[:, None, :].broadcast_to([P, NT, D]), ALU.add))
                settle()
                for b in range(B):
                    part = h2[:, TT * b:TT * b + TT, :]
                    step(G_.tensor_tensor(part, part, mod[:, b, GA:GA + 1, :].broadcast_to([P, TT, D]), ALU.mult))
                settle()
                pool.wait_ge(s["xr_loaded"], a * 32 + 32)
                G_.tensor_tensor(res[:], res[:], h2[:], ALU.add).then_inc(s["res_ready"], 1)

            def load_up(e):
                G_.dma_start(raw_up[:], w1[e].rearrange("(k p) n -> p k n", p=P)).then_inc(s["up_loaded"], 16)

            def load_down(e):
                G_.dma_start(raw_down[:], w2[e].rearrange("(m p) n -> p m n", p=P)).then_inc(s["down_loaded"], 16)

            def iteration(i, A, F, G, NEXT, first=False):
                if G:
                    power(NORM_B, i - 2)
                if F:
                    residual(i - 1)
                if NEXT:
                    power(NORM_A, i + 1)
                    h_of(i + 1)
                if first:
                    power(NORM_1, 1)
                if A:
                    power(NORM_2, i)
                if NEXT and not first:
                    power(NORM_1, i + 1)
                if NEXT:
                    h_plus_ob(i + 1)
                if G and not F:
                    pool.wait_ge(s["gate_done"], NG)
                    load_up(1)
                if G:
                    scatter(i - 2)

            pool.wait_ge(s["dve_step"], 7)
            power(0, 0)
            power(1, 0)
            pool.wait_ge(s["wvo_mm"], 2)
            pool.wait_ge(s["ld_attn"], 16 * 5)
            h_plus_ob(0)
            pool.wait_ge(s["ld_ffn"], 16 * 6)
            pool.wait_ge(s["wprep"], 6)

            iteration(0, True, False, False, True, first=True)
            pool.wait_ge(s["mod_ready"], 3)
            iteration(1, True, True, False, True)
            start = steps[0]
            with pool.Fori(2, NG - 1) as i:
                base[0] = (i - 2) * POOL_ROUND
                iteration(i, True, True, True, True)
            assert steps[0] - start == POOL_ROUND, steps[0] - start
            base[0] = (NG - 4) * POOL_ROUND
            iteration(NG - 1, True, True, True, False)

            iteration(NG, False, True, True, False)
            pool.wait_ge(s["act_split"], NG * MH)
            load_down(1)
            iteration(NG + 1, False, False, True, False)
            pool.drain().then_inc(s["phase1_over"], 2)

            pool.wait_ge(s["phase1_over"], 5)
            pool.wait_ge(s["table_ready"], 1)

            pool.wait_ge(s["x2_stored"], 16 * B * NG)
            for t in range(2):
                G_.indirect_dma_start(out.rearrange("b n d -> (b n) d"),
                                      bass.IndirectOffsetOnAxis(ap=skip_u[:, 0:1], axis=0),
                                      pad_rows[:, t, 0:D], None, bounds_check=T - 1, oob_is_err=False,
                                      compute_op=ALU.add).then_inc(s["summed"], 16)
            pool.wait_ge(s["first_set"], 2)
            G_.memset(e2[:], 0.0).then_inc(s["down_ready"], 1)
            with pool.Fori(0, E // 2) as pair:
                for w in (0, 1):
                    e = pair * 2 + w
                    tiles = pool.value_load(table[0:1, 1, bass.ds(e, 1)], min_val=1, max_val=T // TR)
                    first = pool.value_load(table[0:1, 2, bass.ds(e, 1)], min_val=1, max_val=2 * T // TR + E)
                    pool.wait_ge(s["down_loaded"], e * 16 + 16)
                    pool.wait_ge(s["l2_done"], first * 2)
                    alone(pool)
                    o = 1 - w
                    G_.tensor_copy(down_hi[o][:, 0:MH // 2, :], raw_down[:, 0:MH // 2, :]) \
                        .then_inc(s["down_hi_ready"], 1)
                    pool.wait_ge(s["up_ready"], e + 2)
                    alone(pool)
                    load_up((e + 2) % E)
                    G_.tensor_copy(down_hi[o][:, MH // 2:MH, :], raw_down[:, MH // 2:MH, :]) \
                        .then_inc(s["down_hi_ready"], 1)
                    pool.wait_ge(s["down_hi_ready"], e * 2 + 2)
                    G_.tensor_tensor(down_lo[o][:], raw_down[:], down_hi[o][:].bitcast(F32), ALU.subtract) \
                        .then_inc(s["down_ready"], 1)
                    pool.wait_ge(s["down_ready"], e + 2)
                    alone(pool)
                    load_down((e + 2) % E)
                    pool.wait_ge(s["summed"], first * 32)
                    alone(pool)
                    with pool.Fori(0, tiles) as i:
                        for t in range(2):
                            pool.wait_ge(s["y_ready"], (first + i) * 2 + t + 1)
                            alone(pool)
                            G_.indirect_dma_start(out.rearrange("b n d -> (b n) d"),
                                                  bass.IndirectOffsetOnAxis(ap=tok_u[:, t:t + 1], axis=0),
                                                  y[:, t, :], None, bounds_check=T - 1, oob_is_err=False,
                                                  compute_op=ALU.add).then_inc(s["summed"], 16)
            pool.wait_ge(s["up_loaded"], 16 * (E + 1))
            pool.wait_ge(s["down_loaded"], 16 * (E + 1))


OUT_SHAPE = (2, 2048, 256)


def kernel(**inputs):
    import concourse.bacc as bacc
    from concourse.bass_utils import run_bass_kernel_spmd

    def given(name):
        return np.asarray(inputs["L0_" + name])

    def columns(v, n=P):
        return v.reshape(-1, n).T

    layout = {
        "x": given("attn_x"),
        "c": given("c").reshape(2, 2, P).transpose(2, 1, 0),
        "wmod": given("wmod"),
        "wqk": np.concatenate([given("attn_q_w"), given("attn_k_w")], 0).T,
        "qk_b": columns(np.concatenate([given("attn_q_b"), given("attn_k_b")], 0)),
        "ln1_w": columns(given("attn_ln1_w")),
        "ln1_b": columns(given("attn_ln1_b")),
        "v_w": given("attn_v_w"),
        "v_b": columns(given("attn_v_b")),
        "o_w": given("attn_o_w").T,
        "o_b": given("attn_o_b"),
        "ln2_w": columns(given("attn_ln2_w")),
        "ln2_b": columns(given("attn_ln2_b")),
        "f1": given("attn_f1_w").T,
        "f1_b": columns(given("attn_f1_b")),
        "f2": given("attn_f2_w").T,
        "f2_b": given("attn_f2_b"),
        "gate": given("ffn_gate_w").T,
        "w1": given("ffn_w1").transpose(0, 2, 1),
        "b1": given("ffn_b1").reshape(8, 8, P).transpose(2, 0, 1),
        "w2": given("ffn_w2").transpose(0, 2, 1),
        "b2": given("ffn_b2"),
    }
    nc = bacc.Bacc("TRN2", target_bir_lowering=False, num_devices=1)
    arrays, args = {}, []
    for name, a in layout.items():
        a = np.ascontiguousarray(a)
        arrays["in_" + name] = a
        args.append(nc.dram_tensor("in_" + name, a.shape, mybir.dt.from_np(a.dtype), kind="ExternalInput").ap())
    out = nc.dram_tensor("out_0", OUT_SHAPE, F32, kind="ExternalOutput").ap()
    adaln_moe_program(nc, *args, out)
    r = run_bass_kernel_spmd(nc, [arrays], core_ids=[0])
    return r.results[0]["out_0"]
```

```python
from contextlib import ExitStack

import numpy as np

import concourse.bass as bass
from concourse import mybir

F32 = mybir.dt.float32
F32R = mybir.dt.float32r
BF16 = mybir.dt.bfloat16
I32 = mybir.dt.int32
U32 = mybir.dt.uint32
ALU = mybir.AluOpType
ACT = mybir.ActivationFunctionType
AX_X = mybir.AxisListType.X

P = 128
LN_EPS = 1e-5
ATTN_EPS = 1e-6
DVE_ROUND = 67
POOL_ROUND = 9


def adaln_moe_program(nc, x, c, wmod, wqk, qk_b, ln1_w, ln1_b, v_w, v_b, o_w, o_b, ln2_w, ln2_b,
                      f1, f1_b, f2, f2_b, gate, w1, b1, w2, b2, out):
    B, N, D = x.shape
    KD = D // P
    H = f1.shape[-1]
    MH = H // P
    E = w1.shape[0]
    T = B * N
    TT = 2
    NT = B * TT
    GB = TT * P
    GW = NT * P
    NG = N // GB
    NF = wqk.shape[-1] // 2
    DV = D + 2
    META = D
    ROW = D + 8
    TWO, THREE = 2, 3
    CAP = T + THREE * P
    assert B == 2 and KD == 2 and MH == 8 and E == 8 and 2 * NF == P and NG >= 4

    slots = nc.dram_tensor("slots", (E * CAP, ROW), F32, kind="Internal").ap()

    with ExitStack() as ctx:
        def sb(name, shape, dt=F32):
            return ctx.enter_context(nc.sbuf_tensor(name, shape, dt))

        at = {}

        def sb_marked(name, shape, dt=F32):
            t = sb(name, shape, dt)
            at[name] = nc.sbuf_base - int(np.prod(shape[1:])) * 4
            return t

        def sb_over(name, shape, under, off=0):
            return nc.alloc_sbuf_tensor_at(name, shape, F32, offset=at[under] + off)

        def bank(name):
            return ctx.enter_context(nc.psum_tensor(name, [P, 512], F32))

        def sem(name):
            return ctx.enter_context(nc.semaphore(name))

        wqk_hi, wqk_lo = (sb(f"wqk_{s}", [P, KD, 2 * NF], F32R) for s in ("hi", "lo"))
        wvo_hi, wvo_lo = (sb(f"wvo_{s}", [P, KD, D], F32R) for s in ("hi", "lo"))
        up_hi = [sb(f"up_hi{s}", [P, KD, H], F32R) for s in (0, 1)]
        up_lo = [sb_marked(f"up_lo{s}", [P, KD, H], F32R) for s in (0, 1)]
        down_hi = [sb(f"down_hi{s}", [P, MH, D], F32R) for s in (0, 1)]
        down_lo = [sb_marked(f"down_lo{s}", [P, MH, D], F32R) for s in (0, 1)]
        FFN = 1
        raw_up = sb("raw_up", [P, KD, H])
        raw_down = sb("raw_down", [P, MH, D])
        gate_sb = sb("gate_sb", [P, KD, E])

        mod = sb("mod", [P, B, 6, D])
        SA, CA, GA, SB_, CB, GATE_B = range(6)
        b2_all = mod[:, :, 0:4, :]
        ob_bc = sb("ob_bc", [P, D])
        f2b_bc = sb("f2b_bc", [P, D])
        bvo_bc = sb("bvo_bc", [P, D])
        gb_bc = sb("gb_bc", [P, 2, D])

        vec = sb("vec", [P, 16])
        LN1W, LN1B, LN2W, LN2B, VB = (slice(KD * n, KD * n + KD) for n in range(5))
        qkb = sb("qkb", [P, 2])
        f1b = sb("f1b", [P, MH])
        b1_all = sb("b1_all", [P, E, MH])
        b1_cur = sb("b1_cur", [P, MH])
        b2_cur = sb("b2_cur", [P, D])

        ones = sb("ones", [P, P])
        ident = sb("ident", [P, P])
        causal = sb("causal", [P, 3 * P])
        below = sb("below", [P, P], BF16)
        ones_bf = sb("ones_bf", [P, P], BF16)
        expert_id = sb("expert_id", [P, E])
        slot_base = sb("slot_base", [P, E])
        neg_half = sb("neg_half", [P, NT])

        xa = sb("xa", [P, NT, D])
        hob = sb("hob", [P, NT, D])
        xn1 = sb("xn1", [P, NT, D])
        xt1_hi, xt1_lo = (sb(f"xt1_{s}", [P, KD, GW], F32R) for s in ("hi", "lo"))
        xt2_hi = sb_marked("xt2_hi", [P, KD, GW], F32R)
        xt2_lo = sb("xt2_lo", [P, KD, GW], F32R)
        h3t = raw_up[:, 0, :].rearrange("p (k n) -> p k n", k=KD)
        probs = raw_up[:, 1, 0:2 * 384].rearrange("p (b n) -> p b n", b=B)
        elu = sb_marked("elu", [P, GW])
        qk = sb("qk", [P, GW])
        kz = sb("kz", [P, GW])
        kt = sb("kt", [P, NT, P])
        val = sb("val", [P, NT, DV])
        state = sb("state", [P, B, DV])
        h2 = sb("h2", [P, NT, D])
        xn2 = sb("xn2", [P, NT, D])
        res = sb("res", [P, NT, D])
        x2 = sb("x2", [P, NT, D])
        h3 = sb("h3", [P, NT, ROW])
        act_hi = sb_marked("act_hi", [P, MH, GW], F32R)
        act_lo = sb_marked("act_lo", [P, MH, GW], F32R)
        RING = 4
        gelu_ring = raw_down[:, :, :].rearrange("p (r m) d -> p r (m d)", r=RING)
        stats = sb("stats", [P, NT, 6])
        mv = [sb(f"mv{n}", [P, NT, 2]) for n in range(4)]
        neg_mean = [sb(f"neg_mean{n}", [P, NT]) for n in range(4)]
        shift = [sb(f"shift{n}", [P, NT]) for n in range(4)]
        ve = [sb(f"ve{n}", [P, NT]) for n in range(4)]
        rstd = [sb(f"rstd{n}", [P, NT]) for n in range(4)]
        rden = sb("rden", [P, NT])
        logits = sb("logits", [P, NT, E])
        top = sb("top", [P, NT, 8])
        top_at = sb("top_at", [P, NT, 8], U32)
        gap = sb("gap", [P, NT])
        e2 = sb("e2", [P, NT])
        e2p1 = sb("e2p1", [P, NT])
        chosen = sb("chosen", [P, 2, NT, E])
        picked = sb("picked", [P, NT, E], BF16)
        totals = sb("totals", [P, NT, E])
        place = sb("place", [P, NT, E])
        place2 = sb("place2", [P, 2, NT, E])
        pos = sb("pos", [P, 2 * NT])
        pos_u = sb("pos_u", [P, 2 * NT], U32)
        next_slot = sb("next_slot", [P, E])
        token = sb("token", [P, NT])
        COUNT, PACKED, UNITS, ALL, HALF, PAIRS, ODD = range(7)
        cnt_f = sb("cnt_f", [P, 7, E])
        cnt_i = sb("cnt_i", [P, 4, E], I32)
        table = sb("table", [P, 3, E], I32)

        rows = hob[:, :, :].rearrange("p t d -> p (t d)")[:, 0:THREE * ROW].rearrange("p (t r) -> p t r", t=THREE)
        pad_rows = sb("pad_rows", [P, TWO, ROW])
        skip_u = sb("skip_u", [P, 1], U32)
        meta = sb("meta", [P, THREE, 8])
        cur_e = sb("cur_e", [P, 1])
        is_e = sb("is_e", [P, THREE, 2])
        w_two = sb("w_two", [P, THREE, 2])
        w_row = sb("w_row", [P, THREE])
        tok_u = sb("tok_u", [P, THREE], U32)
        g_row = xn2[:, 0:THREE, :]
        y = xn1[:, 0:THREE, :]
        r_ring = sb_over("r_ring", [P, RING, THREE * P], "elu")
        r_hi = act_hi[:, :, 0:THREE * P]
        r_lo = act_lo[:, :, 0:THREE * P]
        rt_hi = xt1_hi[:, :, 0:THREE * P]
        rt_lo = xt1_lo[:, :, 0:THREE * P]

        wmod_raw = sb_over("wmod_raw", [P, KD, 6 * D], "act_lo")
        first_up = sb_over("first_up", [P, KD, H], "up_lo0")
        first_down = sb_over("first_down", [P, MH, D], "down_lo0")
        v_raw = x2[:, 0:2, :]
        o_raw = x2[:, 2:4, :]
        wqk_raw = res[:, 0, :].rearrange("p (k n) -> p k n", k=KD)
        wvo_raw = hob[:, 0:2, :]
        rep = sb_over("rep", [P, 8, P], "xt2_hi")
        cvec = sb("cvec", [P, KD, B])
        csig = sb("csig", [P, KD, B])

        TP = [bank("tp0"), bank("tp1")]
        AT = [bank("at0"), bank("at1"), bank("at2")]
        FF = [bank("ff0"), bank("ff1")]
        YP = bank("yp")
        mod_bank = [TP[0], TP[1], FF[0], FF[1], FF[0], FF[1]]
        F1B = slice(D + 8, D + 8 + MH)
        down_bank = [FF[0], FF[1], AT[0], YP]
        carry_bank = [TP[1], YP]
        up_bank = {TWO: [FF[0], FF[1], AT[0], AT[1]], THREE: [FF[0], FF[1], AT[0]]}
        y_bank = [YP, AT[2], AT[1]]

        s = {}

        def S(name):
            if name not in s:
                s[name] = sem(name)
            return s[name]

        for name in """ld_c ld_mod ld_mod_rest ld_vec ld_attn ld_ffn ld_first ld_rows consts mod_w mod_c silu_e silu_rep mod_mm mod_copied mod_ready
                prep_vec wvo_mm wvo_raw_ready wprep ffn_bias ffn_bias_mm bias_ready first_hi first_set pool_step dve_step
                x_loaded xr_loaded x2_stored scattered scattered_too
                t1_done t2_done t3_done qk_done v_done kt_done s_done av_done kv_done ff1_done ff2_done
                gate_done rank_done t1_hi t2_hi t3_copied elu_exp gate_exp gelu_done kt_copied
                t1_lo t2_lo xa_normed h_ready hob_ready xn1_ready elu_min qk_ready
                v_ready act_split gap_ready picked_ready pos_ready weights_ready masked h2_ready state_ready xn2_ready
                ff2_read x2_ready h3_ready res_ready phase1_over
                table_ready prefilled padded rows_loaded up_loaded down_loaded up_hi_ready up_ready down_hi_ready down_ready rt_done l1_done l2_done relu_done rt_hi_done
                r_split rt_lo_done meta_read y_ready summed b2_loaded gb_ready pads_ready act_step
                passed ve_a_ready ve_1_ready ve_2_ready ve_b_ready shift_a_ready shift_1_ready shift_2_ready shift_b_ready h3_normed""".split():
            S(name)

        WHOLE = slice(0, NT)
        HALVES = [(NG - 1 + b, slice(TT * b, TT * b + TT)) for b in range(B)]
        half_rows_bank = [TP, FF]
        half_bank = [AT[1], AT[2]]

        NORM_A, NORM_1, NORM_2, NORM_B = range(4)
        VE = ["ve_a_ready", "ve_1_ready", "ve_2_ready", "ve_b_ready"]
        SHIFTED = ["shift_a_ready", "shift_1_ready", "shift_2_ready", "shift_b_ready"]
        NORMED = ["xa_normed", "xn1_ready", "xn2_ready", "h3_normed"]

        def alone(eng):
            eng.sem_inc(s["passed"], 1)

        def group_of(src, b, g):
            return src.rearrange("b (g t p) d -> b g p t d", t=TT, p=P)[b, g]

        def bc(ap, shape):
            return ap.broadcast_to(shape)

        def flat(ap):
            return ap

        def pad(eng, e):
            n = eng.value_load(table[0:1, COUNT, e:e + 1], min_val=0, max_val=T)
            eng.dma_start(slots[bass.ds(n + e * CAP, P), :], pad_rows[:, 0, :]).then_inc(s["padded"], 16)

        def expert(eng, e):
            packed = eng.value_load(table[0:1, PACKED, bass.ds(e, 1)], min_val=1, max_val=T // P + 1)
            pairs, odd = packed // 2, packed % 2
            units = eng.value_load(table[0:1, UNITS, bass.ds(e, 1)], min_val=2, max_val=2 + 2 * T // P + 3 * E)
            return pairs, odd, units

        def tiles_of(eng, pairs, odd, units, tile):
            with eng.If(pairs > 0):
                with eng.Fori(0, pairs) as i:
                    tile(units + i * TWO, TWO, i)
            with eng.If(odd > 0):
                tile(units + pairs * TWO, THREE, pairs)

        block = ctx.enter_context(nc.Block())

        @block.sync
        def _(sp):
            wmod_in = wmod.rearrange("(k p) n -> p k n", p=P)
            sp.dma_start(cvec[:], c).then_inc(s["ld_c"], 16)
            sp.dma_start(wmod_raw[:, :, 0:2 * D], wmod_in[:, :, 0:2 * D]).then_inc(s["ld_mod"], 16)
            for b in range(B):
                sp.dma_start(xa[:, TT * b:TT * b + TT, :], group_of(x, b, 0)).then_inc(s["x_loaded"], 16)
            for k, v in ((LN1W, ln1_w), (LN1B, ln1_b), (LN2W, ln2_w), (LN2B, ln2_b), (VB, v_b)):
                sp.dma_start(vec[:, k], v).then_inc(s["ld_vec"], 16)
            sp.dma_start(wqk_raw, wqk.rearrange("(k p) n -> p k n", p=P)).then_inc(s["ld_attn"], 16)
            sp.dma_start(v_raw, v_w.rearrange("(k p) n -> p k n", p=P)).then_inc(s["ld_attn"], 16)
            sp.dma_start(o_raw, o_w.rearrange("(k p) n -> p k n", p=P)).then_inc(s["ld_attn"], 16)
            sp.dma_start(qkb[:, 0:1], qk_b).then_inc(s["ld_attn"], 16)
            sp.dma_start(ob_bc[:], o_b.partition_broadcast(P)).then_inc(s["ld_attn"], 16)
            sp.dma_start(wmod_raw[:, :, 2 * D:6 * D], wmod_in[:, :, 2 * D:6 * D]).then_inc(s["ld_mod_rest"], 16)
            sp.dma_start(raw_up[:], f1.rearrange("(k p) n -> p k n", p=P)).then_inc(s["ld_ffn"], 16)
            sp.dma_start(f1b[:], f1_b).then_inc(s["ld_ffn"], 16)
            sp.dma_start(raw_down[:], f2.rearrange("(m p) n -> p m n", p=P)).then_inc(s["ld_ffn"], 16)
            sp.dma_start(f2b_bc[:], f2_b.partition_broadcast(P)).then_inc(s["ld_ffn"], 16)
            sp.dma_start(gate_sb[:], gate.rearrange("(k p) n -> p k n", p=P)).then_inc(s["ld_ffn"], 16)
            sp.dma_start(b1_all[:], b1).then_inc(s["ld_ffn"], 16)
            sp.dma_start(first_up[:], w1[0].rearrange("(k p) n -> p k n", p=P)).then_inc(s["ld_first"], 16)
            sp.dma_start(first_down[:], w2[0].rearrange("(m p) n -> p m n", p=P)).then_inc(s["ld_first"], 16)

            def load_x(n):
                sp.wait_ge(s["xn1_ready"], n * B)
                sp.wait_ge(s["hob_ready"], n)
                for b in range(B):
                    sp.dma_start(xa[:, TT * b:TT * b + TT, :], group_of(x, b, n)).then_inc(s["x_loaded"], 16)

            def load_residual(a):
                sp.wait_ge(s["x2_ready"], a * B)
                for b in range(B):
                    sp.dma_start(res[:, TT * b:TT * b + TT, :], group_of(x, b, a)).then_inc(s["xr_loaded"], 16)

            def store_x2(f):
                sp.wait_ge(s["x2_ready"], f * B + B)
                for b in range(B):
                    sp.dma_start(group_of(out, b, f), x2[:, TT * b:TT * b + TT, :]).then_inc(s["x2_stored"], 16)

            load_x(1)
            sp.wait_ge(s["wprep"], 4)
            load_residual(0)
            sp.wait_ge(s["pads_ready"], 3)
            for e in range(E):
                sp.dma_start(slots[e * CAP:e * CAP + TWO * P, :].rearrange("(s p) r -> p s r", p=P), pad_rows[:]) \
                    .then_inc(s["prefilled"], 16)
            load_x(2)
            store_x2(0)
            load_residual(1)
            with sp.Fori(2, NG - 1) as i:
                load_x(i + 1)
                store_x2(i - 1)
                load_residual(i)
            store_x2(NG - 2)
            load_residual(NG - 1)
            store_x2(NG - 1)

            sp.wait_ge(s["h3_ready"], NG + 1)
            sp.wait_ge(s["res_ready"], NG)
            for e in range(E):
                sp.dma_start(b2_all[:, e // 4, e % 4, :], b2[e].partition_broadcast(P)).then_inc(s["b2_loaded"], 16)

            sp.wait_ge(s["table_ready"], 1)
            sp.wait_ge(s["pads_ready"], 3)
            for e in range(E // 2):
                pad(sp, e)
            sp.wait_ge(s["padded"], 16 * E)
            sp.wait_ge(s["scattered"], 32 * NT * NG - 32 * TT)
            sp.wait_ge(s["scattered_too"], 32 * TT)
            sp.wait_ge(s["x2_stored"], 16 * B * NG)
            def load_rows(e, u, width, i):
                sp.wait_ge(s["rt_done"], u)
                alone(sp)
                sp.wait_ge(s["meta_read"], u)
                alone(sp)
                for t in range(width):
                    if t == TWO:
                        sp.wait_ge(s["rows_loaded"], u * 16 + TWO * 16)
                        alone(sp)
                    sp.dma_start(rows[:, t, :], slots[bass.ds(e * CAP + i * (TWO * P) + t * P, P), :]) \
                        .then_inc(s["rows_loaded"], 16)

            with sp.Fori(0, E) as e:
                pairs, odd, units = expert(sp, e)
                tiles_of(sp, pairs, odd, units, lambda u, width, i: load_rows(e, u, width, i))
            pairs, odd, units = expert(sp, E - 1)
            end = units + pairs * TWO + odd * THREE
            load_rows(0, end, TWO, 0)
            sp.wait_ge(s["summed"], end * 16)
            alone(sp)
            sp.wait_ge(s["rows_loaded"], end * 16 + 32)
            alone(sp)

        @block.tensor
        def _(pe):
            def product(dst, lhs, rhs, chunks):
                last = None
                for k in range(chunks):
                    lh, ll = lhs(k)
                    rh, rl = rhs(k)
                    pe.matmul(dst, lh, rh, start=(k == 0), stop=False)
                    pe.matmul(dst, lh, rl, start=False, stop=False)
                    last = pe.matmul(dst, ll, rh, start=False, stop=(k == chunks - 1))
                return last

            for name, per_tile in (("rt_done", TWO), ("l1_done", TWO * MH), ("l2_done", TWO)):
                pe.sem_inc(s[name], per_tile)
            pe.wait_ge(s["ld_mod"], 16)
            pe.wait_ge(s["silu_rep"], KD * B)

            def mod_products(n, b):
                for k in range(KD):
                    last = pe.matmul(mod_bank[2 * n + b][:], rep[:, B * k + b, :], wmod_raw[:, k, 512 * n:512 * n + 512],
                                     start=(k == 0), stop=(k == KD - 1))
                last.then_inc(s["mod_mm"], 1)

            for b in range(B):
                mod_products(0, b)
            pe.wait_ge(s["ld_attn"], 16 * 5)
            for k in range(KD):
                for n in range(KD):
                    last = pe.matmul(FF[1][:, D * k:D * k + D], v_raw[:, n, P * k:P * k + P], o_raw[:, n, :],
                                     start=(n == 0), stop=(n == KD - 1))
            last.then_inc(s["wvo_mm"], 1)
            pe.wait_ge(s["ld_vec"], 16 * 5)
            for k in range(KD):
                last = pe.matmul(YP[:, D:D + 1], wqk_raw[:, k, :], vec[:, LN1B.start + k:LN1B.start + k + 1],
                                 start=(k == 0), stop=(k == KD - 1))
            pe.wait_ge(s["wvo_raw_ready"], 1)
            pe.wait_ge(s["prep_vec"], 2 * KD)
            for k in range(KD):
                pe.matmul(YP[:, 0:D], rep[:, 4 + k, :], wvo_raw[:, k, :], start=(k == 0), stop=False)
            for k in range(KD):
                last = pe.matmul(YP[:, 0:D], rep[:, 6 + k, :], o_raw[:, k, :], start=False, stop=(k == KD - 1))
            last.then_inc(s["wvo_mm"], 1)
            pe.wait_ge(s["ld_mod_rest"], 16)
            mod_products(1, 0)
            pe.wait_ge(s["wprep"], 4)
            mod_products(1, 1)

            def ffn_bias():
                pe.wait_ge(s["ld_ffn"], 16 * 6)
                for m in range(MH):
                    for k in range(KD):
                        last = pe.matmul(YP[:, F1B.start + m:F1B.start + m + 1], raw_up[:, k, P * m:P * m + P],
                                         vec[:, LN2B.start + k:LN2B.start + k + 1], start=(k == 0), stop=(k == KD - 1))
                last.then_inc(s["ffn_bias_mm"], 1)

            def transpose_group(src, banks, done, tiles=WHOLE):
                for k in range(KD):
                    for t in range(tiles.start, tiles.stop):
                        last = pe.transpose(banks[k][:, P * t:P * t + P], src[:, t, P * k:P * k + P], ident[:])
                    last.then_inc(s[done], 1)

            def t1(a, first=False):
                pe.wait_ge(s["xn1_ready"], a * B + B)
                if first:
                    pe.wait_ge(s["mod_ready"], 2)
                else:
                    pe.wait_ge(s["h2_ready"], a)
                    pe.wait_ge(s["state_ready"], a * B - 1)
                transpose_group(xn1, TP, "t1_done")

            def t2(f):
                pe.wait_ge(s["xn2_ready"], f * B + B)
                pe.wait_ge(s["h2_ready"], f + 1)
                transpose_group(xn2, [AT[1], AT[2]], "t2_done")

            def t3(g, A):
                pe.wait_ge(s["h3_ready"], g + 1)
                if A:
                    pe.wait_ge(s["t1_lo"], (g + 3) * KD)
                else:
                    pe.wait_ge(s["h2_ready"], NG)
                    pe.wait_ge(s["state_ready"], NG * B)
                transpose_group(h3, TP, "t3_done")

            def last_t3(b):
                g, tiles = HALVES[b]
                pe.wait_ge(s["h3_ready"], g + 1)
                if b == 0:
                    pe.wait_ge(s["t3_copied"], g * KD)
                else:
                    pe.wait_ge(s["ff2_read"], NG * NT)
                transpose_group(h3, half_rows_bank[b], "t3_done", tiles)

            def queries_keys(a):
                pe.wait_ge(s["t1_hi"], a * KD + KD)
                pe.wait_ge(s["t1_lo"], a * KD + KD)
                product(AT[0][:], lambda k: (wqk_hi[:, k, :], wqk_lo[:, k, :]),
                        lambda k: (xt1_hi[:, k, :], xt1_lo[:, k, :]), KD).then_inc(s["qk_done"], 1)

            def logits_of(g, bank_, tiles):
                pe.wait_ge(s["t3_copied"], g * KD + KD)
                for t in range(tiles.start, tiles.stop):
                    for k in range(KD):
                        last = pe.matmul(bank_[:, E * t:E * t + E], h3t[:, k, P * t:P * t + P], gate_sb[:, k, :],
                                         start=(k == 0), stop=(k == KD - 1))
                last.then_inc(s["gate_done"], 1)

            def route(g):
                pe.wait_ge(s["x2_ready"], g * B + B)
                logits_of(g, YP, WHOLE)

            def values(a):
                for j in range(2):
                    for t in (2 * j, 2 * j + 1):
                        tok = slice(P * t, P * t + P)
                        last = product(AT[1 + j][:, D * (t % 2):D * (t % 2) + D],
                                       lambda k: (xt1_hi[:, k, tok], xt1_lo[:, k, tok]),
                                       lambda k: (wvo_hi[:, k, :], wvo_lo[:, k, :]), KD)
                    last.then_inc(s["v_done"], 1)

            def ffn_up(f, chunks, first=False):
                for m in chunks:
                    if m < 2:
                        if not first:
                            pe.wait_ge(s["ff2_read"], f * NT - NT + m + 1)
                    else:
                        pe.wait_ge(s["gelu_done"], f * MH + m - 1)
                    hid = slice(P * m, P * m + P)
                    product(FF[m % 2][:], lambda k: (up_hi[FFN][:, k, hid], up_lo[FFN][:, k, hid]),
                            lambda k: (xt2_hi[:, k, :], xt2_lo[:, k, :]), KD).then_inc(s["ff1_done"], 1)

            def ffn_down(f, tiles):
                for t in tiles:
                    if t < 2:
                        pe.wait_ge(s["gelu_done"], f * MH + MH - 1 + t)
                    tok = slice(P * t, P * t + P)
                    for m in range(MH):
                        if t == 0:
                            pe.wait_ge(s["act_split"], f * MH + m + 1)
                        first, last = m == 0, m == MH - 1
                        dst = down_bank[t][:, 0:D]
                        pe.matmul(dst, act_hi[:, m, tok], down_hi[FFN][:, m, :], start=first, stop=False)
                        pe.matmul(dst, act_hi[:, m, tok], down_lo[FFN][:, m, :], start=False, stop=False)
                        done = pe.matmul(dst, act_lo[:, m, tok], down_hi[FFN][:, m, :], start=False, stop=last)
                    done.then_inc(s["ff2_done"], 1)

            def keys_back(a):
                pe.wait_ge(s["qk_ready"], a + 1)
                for t in range(NT):
                    last = pe.transpose(AT[0][:, P * t:P * t + P], kz[:, P * t:P * t + P], ident[:])
                last.then_inc(s["kt_done"], 1)

            def scores(a):
                for b in range(B):
                    pe.wait_ge(s["v_ready"], a * B + b + 1)
                    q0 = GB * b
                    pe.matmul(AT[1 + b][:, 0:GB], kz[:, q0:q0 + P], qk[:, q0:q0 + GB], start=True, stop=True)
                    pe.matmul(AT[1 + b][:, GB:GB + P], kz[:, q0 + P:q0 + GB], qk[:, q0 + P:q0 + GB],
                              start=True, stop=True).then_inc(s["s_done"], 1)

            def ranks(g, bank_=YP, tiles=WHOLE):
                pe.wait_ge(s["picked_ready"], g + 1)
                width = (tiles.stop - tiles.start) * E
                flat_picked = picked[:, tiles, :].rearrange("p t e -> p (t e)")
                pe.matmul(bank_[:, 2 * NT * E:2 * NT * E + width], below[:], flat_picked, start=True, stop=True)
                pe.matmul(bank_[:, 3 * NT * E:3 * NT * E + width], ones_bf[:], flat_picked, start=True, stop=True) \
                    .then_inc(s["rank_done"], 1)

            def attend(a):
                pe.wait_ge(s["kt_copied"], a + 1)
                for b, t, dst in ((0, 0, AT[0]), (0, 1, AT[1]), (1, 0, AT[2]), (1, 1, TP[0])):
                    pe.wait_ge(s["masked"], a * B + b + 1)
                    q0 = GB * b + P * t
                    pe.matmul(dst[:, 0:DV], probs[:, b, P * t:P * t + P], val[:, TT * b, :], start=True, stop=False)
                    if t:
                        pe.matmul(dst[:, 0:DV], probs[:, b, 2 * P:3 * P], val[:, TT * b + 1, :], start=False, stop=False)
                    pe.matmul(dst[:, 0:DV], qk[:, q0:q0 + P], state[:, b, :], start=False, stop=True) \
                        .then_inc(s["av_done"], 1)

            def carry(a, b):
                for t in range(TT):
                    last = pe.matmul(carry_bank[b][:, 0:DV], kt[:, TT * b + t, :], val[:, TT * b + t, :],
                                     start=(t == 0), stop=(t == TT - 1))
                last.then_inc(s["kv_done"], 1)

            def iteration(i, A, F, G, NEXT, first=False):
                if F:
                    pe.wait_ge(s["t2_hi"], (i - 1) * KD + KD)
                    pe.wait_ge(s["t2_lo"], (i - 1) * KD + KD)
                    if not G:
                        pe.wait_ge(s["mod_copied"], 4)
                    ffn_up(i - 1, range(0, 1), first=not G)
                if A:
                    if G:
                        pe.wait_ge(s["ff2_read"], (i - 2) * NT + 3)
                    queries_keys(i)
                    values(i)
                if F:
                    ffn_up(i - 1, range(1, 2), first=not G)
                if first:
                    ffn_bias()
                if A:
                    keys_back(i)
                    scores(i)
                if F:
                    ffn_up(i - 1, range(2, 5))
                if G:
                    t3(i - 2, A)
                if F:
                    ffn_up(i - 1, range(5, 6))
                if G:
                    route(i - 2)
                if A:
                    attend(i)
                if F:
                    ffn_up(i - 1, range(6, 7))
                if G:
                    ranks(i - 2)
                if F:
                    ffn_up(i - 1, range(7, 8))
                if A:
                    carry(i, 0)
                if F:
                    ffn_down(i - 1, (0,))
                if A:
                    if G:
                        pe.wait_ge(s["pos_ready"], i - 1)
                    carry(i, 1)
                if F:
                    ffn_down(i - 1, (1,))
                    if A:
                        pe.wait_ge(s["h2_ready"], i + 1)
                    ffn_down(i - 1, (2,))
                if first:
                    pe.wait_ge(s["mod_copied"], 2)
                    mod_products(2, 0)
                    mod_products(2, 1)
                if A:
                    t2(i)
                if F:
                    if A:
                        pe.wait_ge(s["state_ready"], i * B + B)
                    elif G:
                        pe.wait_ge(s["pos_ready"], i - 1)
                    ffn_down(i - 1, (3,))
                if NEXT:
                    t1(i + 1)

            pe.wait_ge(s["consts"], 1)
            t1(0, first=True)
            pe.wait_ge(s["wprep"], 6)
            iteration(0, True, False, False, True, first=True)
            pe.wait_ge(s["bias_ready"], 8)
            iteration(1, True, True, False, True)
            with pe.Fori(2, NG - 1) as i:
                iteration(i, True, True, True, True)
            iteration(NG - 1, True, True, True, False)
            iteration(NG, False, True, True, False)
            last_t3(0)
            logits_of(HALVES[0][0], half_bank[0], HALVES[0][1])
            ranks(HALVES[0][0], half_bank[0], HALVES[0][1])
            last_t3(1)
            logits_of(HALVES[1][0], half_bank[1], HALVES[1][1])
            ranks(HALVES[1][0], half_bank[1], HALVES[1][1])
            pe.drain().then_inc(s["phase1_over"], 1)

            def rows_back(u):
                pe.wait_ge(s["rows_loaded"], u * 16 + TWO * 16)
                pe.wait_ge(s["rt_lo_done"], u)
                for k in range(KD):
                    for t in range(TWO):
                        last = pe.transpose(TP[0][:, P * (TWO * k + t):P * (TWO * k + t) + P],
                                            rows[:, t, P * k:P * k + P], ident[:])
                last.then_inc(s["rt_done"], TWO)

            def third_back(u):
                pe.wait_ge(s["rows_loaded"], u * 16 + THREE * 16)
                pe.wait_ge(s["rt_lo_done"], u)
                for k in range(KD):
                    last = pe.transpose(TP[1][:, P * k:P * k + P], rows[:, TWO, P * k:P * k + P], ident[:])
                last.then_inc(s["rt_done"], 1)

            def expert_up(u, width, w):
                pe.wait_ge(s["rt_hi_done"], u + width)
                pe.wait_ge(s["rt_lo_done"], u + width)
                banks = up_bank[width]
                for m in range(MH):
                    pe.wait_ge(s["relu_done"], u * MH + width * max(0, m - len(banks) + 1))
                    if m == len(up_bank[THREE]):
                        pe.wait_ge(s["y_ready"], u)
                    hid = slice(P * m, P * m + P)
                    product(banks[m % len(banks)][:, 0:P * width], lambda k: (up_hi[w][:, k, hid], up_lo[w][:, k, hid]),
                            lambda k: (rt_hi[:, k, 0:P * width], rt_lo[:, k, 0:P * width]), KD) \
                        .then_inc(s["l1_done"], width)

            def expert_down(u, width, w):
                pe.wait_ge(s["y_ready"], u)
                for t in range(width):
                    for m in range(MH):
                        if t == 0:
                            pe.wait_ge(s["r_split"], u * MH + width * (m + 1))
                        dst = y_bank[t][:, 0:D]
                        row = slice(P * t, P * t + P)
                        pe.matmul(dst, r_hi[:, m, row], down_hi[w][:, m, :], start=(m == 0), stop=False)
                        pe.matmul(dst, r_hi[:, m, row], down_lo[w][:, m, :], start=False, stop=False)
                        last = pe.matmul(dst, r_lo[:, m, row], down_hi[w][:, m, :], start=False, stop=(m == MH - 1))
                    last.then_inc(s["l2_done"], 1)

            def expert_tile(u, width, w):
                if width == THREE:
                    third_back(u)
                expert_up(u, width, w)
                rows_back(u + width)
                expert_down(u, width, w)

            pe.wait_ge(s["table_ready"], 1)
            pe.wait_ge(s["phase1_over"], 5)
            rows_back(TWO)
            with pe.Fori(0, E // 2) as pair:
                for w in (0, 1):
                    pairs, odd, units = expert(pe, pair * 2 + w)
                    pe.wait_ge(s["up_ready"], pair * 2 + w + 1)
                    pe.wait_ge(s["down_ready"], pair * 2 + w + 1)
                    alone(pe)
                    tiles_of(pe, pairs, odd, units, lambda u, width, i: expert_tile(u, width, w))

        @block.scalar
        def _(act):
            steps = [0]

            def step(ins):
                steps[0] += 1
                ins.then_inc(s["act_step"], 1)
                act.wait_ge(s["act_step"], steps[0])

            for name, per_tile in (("rt_hi_done", TWO), ("relu_done", TWO * MH)):
                act.sem_inc(s[name], per_tile)
            act.wait_ge(s["ld_c"], 16)
            act.activation(csig[:], cvec[:], ACT.Exp, scale=-1.0).then_inc(s["silu_e"], 1)

            def normed(kind, n, src, dst):
                act.wait_ge(s[SHIFTED[kind]], n + 1)
                for t in range(NT):
                    last = act.activation(dst[:, t, 0:D], src[:, t, 0:D], ACT.Identity, bias=shift[kind][:, t:t + 1],
                                          scale=rstd[kind][:, t:t + 1])
                    if t == TT - 1:
                        last.then_inc(s[NORMED[kind]], 1)
                last.then_inc(s[NORMED[kind]], 1)

            def norm_x(n):
                normed(NORM_A, n, xa, xa)

            def norm_h(n):
                act.wait_ge(s["t1_done"], n * KD)
                normed(NORM_1, n, xa, xn1)

            def norm_2(a):
                act.wait_ge(s["t2_done"], a * KD)
                normed(NORM_2, a, h2, xn2)

            def last_norm(b):
                g, tiles = HALVES[b]
                act.wait_ge(s["t3_done"], (NG - 1) * KD)
                if b == 0:
                    act.wait_ge(s["scattered"], (NG - 2) * (32 * NT) + 32 * TT)
                else:
                    act.wait_ge(s["scattered_too"], 32 * TT)
                act.wait_ge(s["shift_b_ready"], g + 1)
                for t in range(tiles.start, tiles.stop):
                    last = act.activation(h3[:, t, 0:D], x2[:, t, 0:D], ACT.Identity, bias=shift[NORM_B][:, t:t + 1],
                                          scale=rstd[NORM_B][:, t:t + 1])
                last.then_inc(s["h3_normed"], 1)

            def last_rows(b):
                g, tiles = HALVES[b]
                cols = slice(P * tiles.start, P * tiles.stop)
                for k in range(KD):
                    act.wait_ge(s["t3_done"], g * KD + k + 1)
                    act.activation(h3t[:, k, cols], half_rows_bank[b][k][:, cols], ACT.Copy).then_inc(s["t3_copied"], 1)

            def last_exp(b):
                g, tiles = HALVES[b]
                act.wait_ge(s["gap_ready"], g + 1)
                act.activation(e2[:, tiles], gap[:, tiles], ACT.Exp).then_inc(s["gate_exp"], 1)

            def norm_x2(g):
                act.wait_ge(s["t3_done"], g * KD)
                act.wait_ge(s["scattered"], g * (32 * NT))
                normed(NORM_B, g, x2, h3)

            norm_x(0)
            act.wait_ge(s["ld_vec"], 16 * 5)
            act.wait_ge(s["ld_ffn"], 16 * 6)
            for k in range(KD):
                act.activation(up_hi[FFN][:, k, :], raw_up[:, k, :], ACT.Identity,
                               scale=vec[:, LN2W.start + k:LN2W.start + k + 1]).then_inc(s["ffn_bias"], 1)

            def mod_copies(n):
                for b in range(B):
                    act.wait_ge(s["mod_mm"], 2 * n + b + 1)
                    act.activation(mod[:, b, 2 * n:2 * n + 2, :].rearrange("p j d -> p (j d)"), mod_bank[2 * n + b][:],
                                   ACT.Copy).then_inc(s["mod_copied"], 1)

            def down_heads():
                for n in range(2):
                    act.activation(down_hi[FFN][:, 4 * n:4 * n + 4, :], raw_down[:, 4 * n:4 * n + 4, :], ACT.Copy) \
                        .then_inc(s["ffn_bias"], 1)

            def head(hi, banks, done, sem_out, base):
                for k in range(KD):
                    act.wait_ge(s[done], base + k + 1)
                    act.activation(hi[:, k, :], banks[k][:], ACT.Copy).then_inc(s[sem_out], 1)

            def gelu(f, chunks):
                for m in chunks:
                    act.wait_ge(s["ff1_done"], f * MH + m + 1)
                    act.wait_ge(s["act_split"], f * MH + max(0, m - RING + 1))
                    act.activation(gelu_ring[:, m % RING, :], FF[m % 2][:], ACT.Gelu, bias=f1b[:, m:m + 1])
                    act.activation(act_hi[:, m, :], FF[m % 2][:], ACT.Gelu, bias=f1b[:, m:m + 1]) \
                        .then_inc(s["gelu_done"], 1)

            def iteration(i, A, F, G, NEXT, first=False):
                if A:
                    act.wait_ge(s["v_done"], i * 2)
                    head(xt1_hi, TP, "t1_done", "t1_hi", i * KD)
                if first:
                    norm_x(1)
                if A:
                    act.wait_ge(s["elu_min"], i + 1)
                    act.activation(elu[:], elu[:], ACT.Exp).then_inc(s["elu_exp"], 1)
                if first:
                    down_heads()
                if F:
                    act.wait_ge(s["ff2_done"], (i - 1) * NT)
                    gelu(i - 1, range(0, 2))
                if G:
                    norm_x2(i - 2)
                if F:
                    gelu(i - 1, range(2, 3))
                if A:
                    act.wait_ge(s["kt_done"], i + 1)
                    act.wait_ge(s["kv_done"], i * B)
                    act.activation(kt[:], AT[0][:].rearrange("p (t n) -> p t n", t=NT), ACT.Copy) \
                        .then_inc(s["kt_copied"], 1)
                if F:
                    gelu(i - 1, range(3, 5))
                if G:
                    head(h3t, TP, "t3_done", "t3_copied", (i - 2) * KD)
                if NEXT and not first:
                    norm_x(i + 1)
                if F:
                    gelu(i - 1, range(5, 8))
                if G:
                    act.wait_ge(s["gap_ready"], i - 1)
                    act.activation(e2[:], gap[:], ACT.Exp).then_inc(s["gate_exp"], 1)
                if first:
                    act.wait_ge(s["ld_first"], 32)
                    act.activation(up_hi[0][:], first_up[:], ACT.Copy).then_inc(s["first_hi"], 1)
                    act.activation(down_hi[0][:], first_down[:], ACT.Copy).then_inc(s["first_hi"], 1)
                    norm_h(1)
                if A:
                    norm_2(i)
                if first:
                    mod_copies(2)
                if NEXT and not first:
                    norm_h(i + 1)
                if A:
                    act.wait_ge(s["ff1_done"], i * MH)
                    head(xt2_hi, [AT[1], AT[2]], "t2_done", "t2_hi", i * KD)

            norm_h(0)
            mod_copies(1)
            iteration(0, True, False, False, True, first=True)
            act.wait_ge(s["bias_ready"], 8)
            iteration(1, True, True, False, True)
            with act.Fori(2, NG - 1) as i:
                iteration(i, True, True, True, True)
            iteration(NG - 1, True, True, True, False)
            iteration(NG, False, True, True, False)
            last_norm(0)
            last_rows(0)
            last_norm(1)
            last_exp(0)
            last_rows(1)
            last_exp(1)
            act.drain().then_inc(s["phase1_over"], 1)

            act.wait_ge(s["table_ready"], 1)
            act.wait_ge(s["pads_ready"], 3)
            for e in range(E // 2, E):
                pad(act, e)
            act.wait_ge(s["phase1_over"], 5)

            def rows_head(u):
                act.wait_ge(s["rt_done"], u + TWO)
                act.activation(rt_hi[:, :, 0:TWO * P], TP[0][:].rearrange("p (k n) -> p k n", k=KD), ACT.Copy) \
                    .then_inc(s["rt_hi_done"], TWO)

            def expert_tile(u, width):
                if width == THREE:
                    act.wait_ge(s["rt_done"], u + THREE)
                    act.activation(rt_hi[:, :, TWO * P:THREE * P], TP[1][:, 0:KD * P].rearrange("p (k n) -> p k n", k=KD),
                                   ACT.Copy).then_inc(s["rt_hi_done"], 1)
                act.wait_ge(s["l2_done"], u)
                banks = up_bank[width]
                for m in range(MH):
                    src = banks[m % len(banks)][:, 0:P * width]
                    act.wait_ge(s["l1_done"], u * MH + width * (m + 1))
                    act.wait_ge(s["r_split"], u * MH + width * max(0, m - RING + 1))
                    act.activation(r_ring[:, m % RING, 0:P * width], src, ACT.Relu, bias=b1_cur[:, m:m + 1])
                    act.activation(r_hi[:, m, 0:P * width], src, ACT.Relu, bias=b1_cur[:, m:m + 1]) \
                        .then_inc(s["relu_done"], width)
                rows_head(u + width)

            rows_head(TWO)
            with act.Fori(0, E // 2) as pair:
                for w in (0, 1):
                    e = pair * 2 + w
                    pairs, odd, units = expert(act, e)
                    act.wait_ge(s["up_loaded"], e * 16 + 16)
                    act.activation(up_hi[1 - w][:], raw_up[:], ACT.Copy).then_inc(s["up_hi_ready"], 1)
                    act.wait_ge(s["relu_done"], units * MH)
                    act.activation(b1_cur[:], b1_all[:, bass.ds(e, 1), :].rearrange("p e m -> p (e m)"), ACT.Copy) \
                        .then_inc(s["act_step"], 1)
                    act.wait_ge(s["act_step"], e + 1)
                    alone(act)
                    tiles_of(act, pairs, odd, units, lambda u, width, i: expert_tile(u, width))

        @block.vector
        def _(dve):
            steps = [0]
            base = [0]

            def step(ins, n=1):
                steps[0] += n
                ins.then_inc(s["dve_step"], n)

            def settle():
                dve.wait_ge(s["dve_step"], base[0] + steps[0])

            V = nc.vector
            for name, per_tile in (("meta_read", TWO), ("r_split", TWO * MH), ("rt_lo_done", TWO), ("y_ready", TWO),
                                   ("up_ready", 1)):
                dve.sem_inc(s[name], per_tile)
            V.memset(ones[:], 1.0).then_inc(s["mod_c"], 1)
            step(V.memset(state[:], 0.0))
            step(V.memset(kz[:], 0.0))
            step(V.memset(val[:, :, D:DV], 1.0))
            step(V.memset(neg_half[:], -0.5))
            step(V.memset(ones_bf[:], 1.0))
            step(V.memset(h3[:, :, META:ROW], 0.0))
            settle()
            step(V.memset(h3[:, TT:NT, META + 5:META + 6], 1.0))
            dve.wait_ge(s["silu_e"], 1)
            step(V.tensor_scalar(csig[:], csig[:], 1.0, None, ALU.add))
            settle()
            step(V.reciprocal(csig[:], csig[:]))
            settle()
            step(V.tensor_tensor(csig[:], csig[:], cvec[:], ALU.mult))
            settle()
            dve.wait_ge(s["mod_c"], 1)
            for k in range(KD):
                for b in range(B):
                    V.tensor_scalar(rep[:, B * k + b, :], ones[:], csig[:, k, b:b + 1], None, ALU.mult) \
                        .then_inc(s["silu_rep"], 1)
            dve.wait_ge(s["ld_vec"], 16 * 5)
            for n, src in enumerate((LN1B, VB)):
                for k in range(KD):
                    V.tensor_scalar(rep[:, 4 + 2 * n + k, :], ones[:], vec[:, src.start + k:src.start + k + 1], None,
                                    ALU.mult).then_inc(s["prep_vec"], 1)

            def norm_stats(kind, n, src, tiles=WHOLE):
                for t in range(tiles.start, tiles.stop):
                    step(V.bn_stats(stats[:, t, :], src[:, t, 0:D]))
                settle()
                alone(dve)
                for t in range(tiles.start, tiles.stop):
                    step(V.bn_aggr(mv[kind][:, t, :], stats[:, t, :]))
                settle()
                dve.wait_ge(s[SHIFTED[kind]], n)
                V.tensor_scalar(neg_mean[kind][:, tiles], mv[kind][:, tiles, 0], -1.0, None, ALU.mult).then_inc(s[VE[kind]], 1)
                V.tensor_scalar(ve[kind][:, tiles], mv[kind][:, tiles, 1], LN_EPS, None, ALU.add).then_inc(s[VE[kind]], 1)

            def stats_x(n):
                dve.wait_ge(s["x_loaded"], n * 32 + 32)
                norm_stats(NORM_A, n, xa)

            def stats_h(n):
                dve.wait_ge(s["h_ready"], n + 1)
                norm_stats(NORM_1, n, xa)

            def stats_2(a):
                dve.wait_ge(s["h2_ready"], a + 1)
                norm_stats(NORM_2, a, h2)

            def stats_x2(g):
                dve.wait_ge(s["x2_ready"], g * B + B)
                norm_stats(NORM_B, g, x2)

            def last_stats(b):
                g, tiles = HALVES[b]
                dve.wait_ge(s["x2_ready"], (NG - 1) * B + b + 1)
                norm_stats(NORM_B, g, x2, tiles)

            def last_modulate(b):
                dve.wait_ge(s["h3_normed"], (NG - 1) * B + b + 1)
                part = h3[:, HALVES[b][1], 0:D]
                step(V.tensor_tensor(part, part, mod[:, b, CB:CB + 1, :].broadcast_to([P, TT, D]), ALU.mult))
                settle()
                V.tensor_tensor(part, part, mod[:, b, SB_:SB_ + 1, :].broadcast_to([P, TT, D]), ALU.add) \
                    .then_inc(s["h3_ready"], 1)

            def modulate_x2(g):
                modulate(h3, g, "h3_normed", CB, SB_, "h3_ready")

            def modulate(rows_, n, normed, one_plus, shift_row, done):
                for b in range(B):
                    dve.wait_ge(s[normed], n * B + b + 1)
                    part = rows_[:, TT * b:TT * b + TT, 0:D]
                    step(V.tensor_tensor(part, part, mod[:, b, one_plus:one_plus + 1, :].broadcast_to([P, TT, D]), ALU.mult))
                settle()
                for b in range(B):
                    part = rows_[:, TT * b:TT * b + TT, 0:D]
                    last = V.tensor_tensor(part, part, mod[:, b, shift_row:shift_row + 1, :].broadcast_to([P, TT, D]),
                                           ALU.add)
                last.then_inc(s[done], 1)

            stats_x(0)
            for b in range(B):
                dve.wait_ge(s["mod_mm"], b + 1)
                step(V.tensor_copy(mod[:, b, SA, :], mod_bank[b][:, 0:D]))
                V.tensor_scalar(mod[:, b, CA, :], mod_bank[b][:, D:2 * D], 1.0, None, ALU.add).then_inc(s["mod_ready"], 1)

            def floor_gate(row, scratch, done):
                g = mod[:, :, row, :]
                step(V.tensor_scalar(scratch, g, 0.0, 2.0, ALU.is_ge, ALU.mult))
                settle()
                step(V.tensor_scalar(scratch, scratch, 1.0, None, ALU.subtract))
                settle()
                step(V.tensor_tensor(g, g, scratch, ALU.mult))
                settle()
                V.scalar_tensor_tensor(g, g, 0.25, scratch, ALU.max, ALU.mult).then_inc(s[done], 1)

            settle()
            dve.wait_ge(s["mod_ready"], 2)
            modulate(xa, 0, "xa_normed", CA, SA, "h_ready")
            dve.wait_ge(s["ld_attn"], 16 * 5)
            dve.wait_ge(s["ld_vec"], 16 * 5)
            for k in range(KD):
                step(V.tensor_scalar(elu[:, P * k:P * k + P], wqk_raw[:, k, :],
                                     vec[:, LN1W.start + k:LN1W.start + k + 1], None, ALU.mult))
            settle()
            ewqk = elu[:, 0:KD * P].rearrange("p (k n) -> p k n", k=KD)
            V.tensor_copy(wqk_hi[:], ewqk).then_inc(s["wprep"], 1)
            dve.wait_ge(s["wprep"], 1)
            V.tensor_tensor(wqk_lo[:], ewqk, wqk_hi[:].bitcast(F32), ALU.subtract).then_inc(s["wprep"], 1)
            dve.wait_ge(s["wvo_mm"], 1)
            V.tensor_copy(wvo_raw, FF[1][:].rearrange("p (k n) -> p k n", k=KD)).then_inc(s["wvo_raw_ready"], 1)
            for k in range(KD):
                step(V.tensor_scalar(h2[:, k, :], FF[1][:, D * k:D * k + D],
                                     vec[:, LN1W.start + k:LN1W.start + k + 1], None, ALU.mult))
            settle()
            V.tensor_copy(wvo_hi[:], h2[:, 0:2, :]).then_inc(s["wprep"], 1)
            dve.wait_ge(s["wprep"], 3)
            V.tensor_tensor(wvo_lo[:], h2[:, 0:2, :], wvo_hi[:].bitcast(F32), ALU.subtract).then_inc(s["wprep"], 1)
            dve.wait_ge(s["wprep"], 4)
            stats_h(0)
            dve.wait_ge(s["wvo_mm"], 2)
            V.tensor_copy(bvo_bc[:], YP[:, 0:D]).then_inc(s["wprep"], 1)
            step(V.tensor_tensor(qkb[:, 0:1], qkb[:, 0:1], YP[:, D:D + 1], ALU.add))
            settle()
            V.tensor_scalar(qkb[:, 1:2], qkb[:, 0:1], 1.0, None, ALU.add).then_inc(s["wprep"], 1)
            for k in range(KD):
                dve.wait_ge(s["ffn_bias"], k + 1)
                V.scalar_tensor_tensor(up_lo[FFN][:, k, :], raw_up[:, k, :], vec[:, LN2W.start + k:LN2W.start + k + 1],
                                       up_hi[FFN][:, k, :].bitcast(F32), ALU.mult, ALU.subtract) \
                    .then_inc(s["bias_ready"], 1)
            dve.wait_ge(s["consts"], 1)
            V.tensor_copy(next_slot[:], slot_base[:]).then_inc(s["bias_ready"], 1)
            dve.wait_ge(s["wprep"], 6)
            dve.wait_ge(s["bias_ready"], 3)

            def down_rests(pieces):
                for n in pieces:
                    dve.wait_ge(s["ffn_bias"], 3 + n // 2)
                    V.tensor_tensor(down_lo[FFN][:, 2 * n:2 * n + 2, :], raw_down[:, 2 * n:2 * n + 2, :],
                                    down_hi[FFN][:, 2 * n:2 * n + 2, :].bitcast(F32), ALU.subtract) \
                        .then_inc(s["bias_ready"], 1)

            def rest(hi, lo, banks, hi_done, lo_done, n):
                for k in range(KD):
                    dve.wait_ge(s[hi_done], n * KD + k + 1)
                    V.tensor_tensor(lo[:, k, :], banks[k][:], hi[:, k, :].bitcast(F32), ALU.subtract) \
                        .then_inc(s[lo_done], 1)

            def elu_min(a):
                dve.wait_ge(s["qk_done"], a + 1)
                V.tensor_scalar(elu[:], AT[0][:], qkb[:, 0:1], 0.0, ALU.add, ALU.min).then_inc(s["elu_min"], 1)

            def elu_max(a):
                dve.wait_ge(s["elu_exp"], a + 1)
                dve.wait_ge(s["av_done"], a * NT)
                step(V.scalar_tensor_tensor(qk[:], AT[0][:], qkb[:, 1:2], elu[:], ALU.add, ALU.max))
                settle()
                V.tensor_copy(kz[0:NF, :], qk[NF:P, :]).then_inc(s["qk_ready"], 1)

            def values_out(a):
                dve.wait_ge(s["kv_done"], a * B)
                for b in range(B):
                    dve.wait_ge(s["v_done"], a * B + b + 1)
                    V.tensor_tensor(val[:, TT * b:TT * b + TT, 0:D], AT[1 + b][:].rearrange("p (t n) -> p t n", t=TT),
                                    bvo_bc[:, None, :].broadcast_to([P, TT, D]), ALU.add).then_inc(s["v_ready"], 1)

            def split_act(f, chunks):
                for m in chunks:
                    dve.wait_ge(s["gelu_done"], f * MH + m + 1)
                    V.tensor_tensor(act_lo[:, m, :], gelu_ring[:, m % RING, :], act_hi[:, m, :].bitcast(F32),
                                    ALU.subtract).then_inc(s["act_split"], 1)

            def best_two(g, bank_=YP, tiles=WHOLE):
                n = tiles.stop - tiles.start
                numbers = range(tiles.start, tiles.stop)
                dve.wait_ge(s["gate_done"], g + 1)
                step(V.tensor_copy(logits[:, tiles, :],
                                   bank_[:, E * tiles.start:E * tiles.stop].rearrange("p (t e) -> p t e", t=n)))
                settle()
                alone(dve)
                for t in numbers:
                    step(V.max(top[:, t, :], logits[:, t, :]))
                settle()
                V.tensor_tensor(gap[:, tiles], top[:, tiles, 1], top[:, tiles, 0], ALU.subtract).then_inc(s["gap_ready"], 1)
                for t in numbers:
                    step(V.max_index(top_at[:, t, :], top[:, t, :], logits[:, t, :]))
                settle()
                step(V.tensor_copy(h3[:, tiles, META:META + 2], top_at[:, tiles, 0:2]))
                step(V.tensor_copy(h3[:, tiles, META + 4], token[:, tiles]))
                settle()
                step(V.tensor_scalar(token[:, tiles], token[:, tiles], float(GB), None, ALU.add))
                for c_ in range(2):
                    step(V.tensor_tensor(chosen[:, c_, tiles, :], expert_id[:, None, :].broadcast_to([P, n, E]),
                                         h3[:, tiles, META + c_:META + c_ + 1].broadcast_to([P, n, E]), ALU.is_equal))
                settle()
                V.tensor_tensor(picked[:, tiles, :], chosen[:, 0, tiles], chosen[:, 1, tiles], ALU.add) \
                    .then_inc(s["picked_ready"], 1)

            def gate_weights(g, tiles=WHOLE):
                dve.wait_ge(s["gate_exp"], g + 1)
                step(V.tensor_scalar(e2p1[:, tiles], e2[:, tiles], 1.0, None, ALU.add))
                settle()
                step(V.reciprocal(e2p1[:, tiles], e2p1[:, tiles]))
                settle()
                V.tensor_copy(h3[:, tiles, META + 2], e2p1[:, tiles]).then_inc(s["weights_ready"], 1)
                V.tensor_tensor(h3[:, tiles, META + 3], e2p1[:, tiles], e2[:, tiles], ALU.mult) \
                    .then_inc(s["weights_ready"], 1)

            def slots_of(g, bank_=YP, tiles=WHOLE):
                n = tiles.stop - tiles.start
                dve.wait_ge(s["rank_done"], g + 1)
                step(V.tensor_tensor(place[:, tiles, :],
                                     bank_[:, 2 * NT * E:(2 * NT + n) * E].rearrange("p (t e) -> p t e", t=n),
                                     next_slot[:, None, :].broadcast_to([P, n, E]), ALU.add))
                step(V.tensor_copy(totals[:, tiles, :],
                                   bank_[:, 3 * NT * E:(3 * NT + n) * E].rearrange("p (t e) -> p t e", t=n)))
                settle()
                for t in range(tiles.start, tiles.stop):
                    if t < tiles.stop - 1:
                        step(V.tensor_tensor(place[:, t + 1:tiles.stop, :], place[:, t + 1:tiles.stop, :],
                                             totals[:, t:t + 1, :].broadcast_to([P, tiles.stop - 1 - t, E]), ALU.add))
                    step(V.tensor_tensor(next_slot[:], next_slot[:], totals[:, t, :], ALU.add))
                    settle()
                step(V.tensor_tensor(place2[:, :, tiles], chosen[:, :, tiles],
                                     place[:, None, tiles, :].broadcast_to([P, 2, n, E]), ALU.mult))
                settle()
                pos_ct = pos[:].rearrange("p (c t) -> p c t", c=2)
                pos_u_ct = pos_u[:].rearrange("p (c t) -> p c t", c=2)
                step(V.tensor_reduce(pos_ct[:, :, tiles], place2[:, :, tiles, :], AX_X, ALU.add))
                settle()
                V.tensor_copy(pos_u_ct[:, :, tiles], pos_ct[:, :, tiles]).then_inc(s["pos_ready"], 1)

            def mask(a):
                for b in range(B):
                    dve.wait_ge(s["s_done"], a * B + b + 1)
                    V.tensor_tensor(probs[:, b, :], AT[1 + b][:, 0:3 * P], causal[:], ALU.mult).then_inc(s["masked"], 1)

            def attended(a):
                dve.wait_ge(s["hob_ready"], a + 1)
                dve.wait_ge(s["res_ready"], a)
                for t, bk in enumerate((AT[0], AT[1], AT[2], TP[0])):
                    dve.wait_ge(s["av_done"], a * NT + t + 1)
                    step(V.tensor_scalar(rden[:, t:t + 1], bk[:, D:D + 1], ATTN_EPS, None, ALU.add))
                settle()
                step(V.reciprocal(rden[:], rden[:]))
                settle()
                for t, bk in enumerate((AT[0], AT[1], AT[2], TP[0])):
                    last = V.scalar_tensor_tensor(h2[:, t, :], bk[:, 0:D], rden[:, t:t + 1], hob[:, t, :],
                                                  ALU.mult, ALU.add)
                last.then_inc(s["h2_ready"], 1)

            def carry_state(a, b):
                dve.wait_ge(s["kv_done"], a * B + b + 1)
                V.tensor_tensor(state[:, b, :], state[:, b, :], carry_bank[b][:, 0:DV], ALU.add).then_inc(s["state_ready"], 1)

            def tile_out(f, t):
                dve.wait_ge(s["ff2_done"], f * NT + t + 1)
                V.tensor_tensor(x2[:, t, :], down_bank[t][:, 0:D], mod[:, t // TT, GA, :], ALU.mult) \
                    .then_inc(s["ff2_read"], 1)

            def ffn_out(f):
                dve.wait_ge(s["x2_stored"], f * 32)
                dve.wait_ge(s["res_ready"], f + 1)
                for t in range(NT - 1):
                    tile_out(f, t)
                    if t == TT - 1:
                        add_residual(f, 0)

            def add_residual(f, b):
                dve.wait_ge(s["ff2_read"], f * NT + TT * b + TT)
                part = slice(TT * b, TT * b + TT)
                V.tensor_tensor(x2[:, part, :], x2[:, part, :], res[:, part, :], ALU.add).then_inc(s["x2_ready"], 1)

            def iteration(i, A, F, G, NEXT, first=False):
                if F:
                    rest(xt2_hi, xt2_lo, [AT[1], AT[2]], "t2_hi", "t2_lo", i - 1)
                if G:
                    tile_out(i - 2, NT - 1)
                if A:
                    rest(xt1_hi, xt1_lo, TP, "t1_hi", "t1_lo", i)
                if G:
                    add_residual(i - 2, 1)
                if first:
                    stats_x(1)
                if A:
                    elu_min(i)
                if G:
                    stats_x2(i - 2)
                if F and not A:
                    dve.wait_ge(s["first_hi"], 2)
                    V.tensor_tensor(up_lo[0][:], first_up[:], up_hi[0][:].bitcast(F32), ALU.subtract) \
                        .then_inc(s["first_set"], 1)
                if A:
                    elu_max(i)
                    values_out(i)
                if F:
                    split_act(i - 1, range(0, 2))
                if first:
                    dve.wait_ge(s["ffn_bias_mm"], 1)
                    V.tensor_tensor(f1b[:], f1b[:], YP[:, F1B], ALU.add).then_inc(s["bias_ready"], 1)
                if A:
                    mask(i)
                if F and A and not G:
                    dve.wait_ge(s["mod_copied"], 4)
                    step(V.tensor_scalar(mod[:, :, CB, :], mod[:, :, CB, :], 1.0, None, ALU.add))
                    floor_gate(GATE_B, gb_bc[:], "mod_ready")
                    dve.wait_ge(s["mod_ready"], 4)
                    step(V.tensor_copy(gb_bc[:, 0, :], mod[:, 0, GATE_B, :]))
                    step(V.tensor_tensor(gb_bc[:, 1, :], mod[:, 1, GATE_B, :], mod[:, 0, GATE_B, :], ALU.subtract))
                if G:
                    modulate_x2(i - 2)
                if F and not A:
                    V.tensor_tensor(down_lo[0][:], first_down[:], down_hi[0][:].bitcast(F32), ALU.subtract) \
                        .then_inc(s["first_set"], 1)
                if first:
                    dve.wait_ge(s["mod_copied"], 2)
                    floor_gate(GA, gb_bc[:], "mod_ready")
                    stats_h(1)
                elif NEXT:
                    stats_x(i + 1)
                if F:
                    split_act(i - 1, range(2, 5))
                if G:
                    best_two(i - 2)
                if F:
                    split_act(i - 1, range(5, 6))
                if A:
                    attended(i)
                if F:
                    split_act(i - 1, range(6, 7))
                if G:
                    slots_of(i - 2)
                if F:
                    split_act(i - 1, range(7, 8))
                if A:
                    stats_2(i)
                    carry_state(i, 0)
                if G:
                    gate_weights(i - 2)
                if NEXT and not first:
                    stats_h(i + 1)
                if A:
                    carry_state(i, 1)
                if first:
                    down_rests(range(4))
                    dve.wait_ge(s["bias_ready"], 8)
                if F and A:
                    ffn_out(i - 1)

            iteration(0, True, False, False, True, first=True)
            iteration(1, True, True, False, True)
            start = steps[0]
            with dve.Fori(2, NG - 1) as i:
                base[0] = (i - 2) * DVE_ROUND
                iteration(i, True, True, True, True)
            assert steps[0] - start == DVE_ROUND, steps[0] - start
            base[0] = (NG - 4) * DVE_ROUND
            iteration(NG - 1, True, True, True, False)
            iteration(NG, False, True, True, False)
            last = NG - 1
            dve.wait_ge(s["x2_stored"], last * 32)
            dve.wait_ge(s["res_ready"], NG)
            tile_out(last, 0)
            tile_out(last, 1)
            add_residual(last, 0)
            last_stats(0)
            tile_out(last, 2)
            last_modulate(0)
            tile_out(last, 3)
            add_residual(last, 1)
            last_stats(1)
            for b in range(B):
                best_two(HALVES[b][0], half_bank[b], HALVES[b][1])
                if b == 0:
                    last_modulate(1)
                slots_of(HALVES[b][0], half_bank[b], HALVES[b][1])
                gate_weights(*HALVES[b])
            step(V.tensor_tensor(cnt_f[:, COUNT, :], next_slot[:], slot_base[:], ALU.subtract))
            settle()
            step(V.tensor_scalar(cnt_f[:, ALL, :], cnt_f[:, COUNT, :], float(P - 1), None, ALU.add))
            settle()
            step(V.tensor_copy(cnt_i[:, 0, :], cnt_f[:, ALL, :]))
            settle()
            step(V.tensor_single_scalar(cnt_i[:, 1, :], cnt_i[:, 0, :], P.bit_length() - 1, ALU.logical_shift_right))
            settle()
            step(V.tensor_copy(cnt_f[:, ALL, :], cnt_i[:, 1, :]))
            settle()
            step(V.tensor_scalar(cnt_f[:, ALL, :], cnt_f[:, ALL, :], float(TWO), None, ALU.max))
            settle()
            step(V.tensor_copy(cnt_i[:, 2, :], cnt_f[:, ALL, :]))
            settle()
            step(V.tensor_single_scalar(cnt_i[:, 3, :], cnt_i[:, 2, :], 1, ALU.logical_shift_right))
            settle()
            step(V.tensor_copy(cnt_f[:, HALF, :], cnt_i[:, 3, :]))
            step(V.memset(cnt_f[:, UNITS, 0:1], float(TWO)))
            settle()
            step(V.tensor_scalar(cnt_f[:, PAIRS, :], cnt_f[:, HALF, :], -2.0, None, ALU.mult))
            settle()
            step(V.tensor_tensor(cnt_f[:, ODD, :], cnt_f[:, ALL, :], cnt_f[:, PAIRS, :], ALU.add))
            settle()
            step(V.tensor_tensor(cnt_f[:, PAIRS, :], cnt_f[:, HALF, :], cnt_f[:, ODD, :], ALU.subtract))
            settle()
            step(V.tensor_tensor(cnt_f[:, PACKED, :], cnt_f[:, PAIRS, :], cnt_f[:, HALF, :], ALU.add))
            for e in range(1, E):
                step(V.tensor_tensor(cnt_f[:, UNITS, e:e + 1], cnt_f[:, UNITS, e - 1:e], cnt_f[:, ALL, e - 1:e], ALU.add))
                settle()
            V.tensor_copy(table[:], cnt_f[:, 0:3, :]).then_inc(s["table_ready"], 1)
            step(V.memset(cur_e[:], -1.0))
            settle()
            dve.drain().then_inc(s["phase1_over"], 1)

            dve.wait_ge(s["table_ready"], 1)
            dve.wait_ge(s["phase1_over"], 5)
            dve.wait_ge(s["b2_loaded"], 16 * E)

            def rows_rest(u):
                dve.wait_ge(s["rt_hi_done"], u + TWO)
                V.tensor_tensor(rt_lo[:, :, 0:TWO * P], TP[0][:].rearrange("p (k n) -> p k n", k=KD),
                                rt_hi[:, :, 0:TWO * P].bitcast(F32), ALU.subtract).then_inc(s["rt_lo_done"], TWO)

            def take_meta(u):
                dve.wait_ge(s["rows_loaded"], u * 16 + TWO * 16)
                V.tensor_copy(meta[:, 0:TWO, :], rows[:, 0:TWO, META:ROW]).then_inc(s["meta_read"], TWO)

            def third_rest(u):
                dve.wait_ge(s["rt_hi_done"], u + THREE)
                V.tensor_tensor(rt_lo[:, :, TWO * P:THREE * P], TP[1][:, 0:KD * P].rearrange("p (k n) -> p k n", k=KD),
                                rt_hi[:, :, TWO * P:THREE * P].bitcast(F32), ALU.subtract).then_inc(s["rt_lo_done"], 1)

            def expert_tile(e, u, width, pairs):
                base[0] = (NG - 4) * DVE_ROUND + e * HEAD + (u - TWO) * UNIT
                before = steps[0]
                if width == THREE:
                    with dve.If(pairs > 0):
                        third_rest(u)
                    dve.wait_ge(s["rows_loaded"], u * 16 + THREE * 16)
                    V.tensor_copy(meta[:, TWO, :], rows[:, TWO, META:ROW]).then_inc(s["meta_read"], 1)
                for m in range(MH):
                    dve.wait_ge(s["relu_done"], u * MH + width * (m + 1))
                    V.tensor_tensor(r_lo[:, m, 0:P * width], r_ring[:, m % RING, 0:P * width],
                                    r_hi[:, m, 0:P * width].bitcast(F32), ALU.subtract).then_inc(s["r_split"], width)
                dve.wait_ge(s["summed"], u * 16)
                dve.wait_ge(s["meta_read"], u + width)
                step(V.tensor_scalar(is_e[:, 0:width], meta[:, 0:width, 0:2], cur_e[:, 0:1], None, ALU.is_equal), width - 1)
                settle()
                step(V.tensor_tensor(w_two[:, 0:width], is_e[:, 0:width], meta[:, 0:width, 2:4], ALU.mult), width - 1)
                settle()
                step(V.tensor_reduce(w_row[:, 0:width], w_two[:, 0:width], AX_X, ALU.add))
                step(V.tensor_copy(tok_u[:, 0:width], meta[:, 0:width, 4]))
                for t in range(width):
                    step(V.scalar_tensor_tensor(g_row[:, t, :], gb_bc[:, 1, :], meta[:, t, 5:6],
                                                gb_bc[:, 0, :], ALU.mult, ALU.add))
                rows_rest(u + width)
                settle()
                take_meta(u + width)
                for t in range(width):
                    dve.wait_ge(s["l2_done"], u + t + 1)
                    step(V.tensor_tensor(y[:, t, :], y_bank[t][:, 0:D], b2_cur[:], ALU.add))
                    settle()
                    V.scalar_tensor_tensor(y[:, t, :], y[:, t, :], w_row[:, t:t + 1], g_row[:, t, :],
                                           ALU.mult, ALU.mult).then_inc(s["y_ready"], 1)
                assert steps[0] - before == width * UNIT, steps[0] - before
                steps[0] = before

            take_meta(TWO)
            rows_rest(TWO)
            done_before = steps[0]
            HEAD, UNIT = 2, 4
            with dve.Fori(0, E // 2) as pair:
                for w in (0, 1):
                    e = pair * 2 + w
                    pairs, odd, units = expert(dve, e)
                    with dve.If(pairs < 1):
                        third_rest(units)
                    dve.wait_ge(s["up_hi_ready"], e + 1)
                    V.tensor_tensor(up_lo[1 - w][:], raw_up[:], up_hi[1 - w][:].bitcast(F32), ALU.subtract) \
                        .then_inc(s["up_ready"], 1)
                    base[0] = (NG - 4) * DVE_ROUND + e * HEAD + (units - TWO) * UNIT
                    before = steps[0]
                    dve.wait_ge(s["y_ready"], units)
                    step(V.tensor_copy(b2_cur[:], mod[:, bass.ds(e // 4, 1), bass.ds(e % 4, 1), :]
                                       .rearrange("p b j d -> p (b j d)")))
                    step(V.tensor_scalar(cur_e[:], cur_e[:], 1.0, None, ALU.add))
                    settle()
                    alone(dve)
                    assert steps[0] - before == HEAD
                    tiles_of(dve, pairs, odd, units, lambda u, width, i: expert_tile(e, u, width, pairs))
                    steps[0] = done_before

        @block.gpsimd
        def _(pool):
            G_ = nc.gpsimd
            steps = [0]
            base = [0]

            def step(ins):
                steps[0] += 1
                ins.then_inc(s["pool_step"], 1)

            def settle():
                pool.wait_ge(s["pool_step"], base[0] + steps[0])

            pool.sem_inc(s["rows_loaded"], TWO * 16)
            for t in (ident,):
                step(G_.memset(t[:], 0.0))
            step(G_.memset(causal[:], 1.0))
            step(G_.memset(below[:], 1.0))
            step(G_.memset(pad_rows[:], 0.0))
            settle()
            step(G_.affine_select(out=ident[:], in_=ident[:], compare_op=ALU.not_equal, fill=1.0, base=0,
                                  pattern=[[-1, P]], channel_multiplier=1))
            for o in (0, 2):
                step(G_.affine_select(out=causal[:, P * o:P * o + P], in_=causal[:, P * o:P * o + P],
                                      compare_op=ALU.is_ge, fill=0.0, base=0, pattern=[[1, P]], channel_multiplier=-1))
            step(G_.affine_select(out=below[:], in_=below[:], compare_op=ALU.is_gt, fill=0.0, base=0,
                                  pattern=[[1, P]], channel_multiplier=-1))
            step(G_.iota(expert_id[:], pattern=[[1, E]], base=0, channel_multiplier=0,
                         allow_small_or_imprecise_dtypes=True))
            step(G_.iota(slot_base[:], pattern=[[CAP, E]], base=0, channel_multiplier=0,
                         allow_small_or_imprecise_dtypes=True))
            step(G_.iota(token[:].rearrange("p (b t) -> p b t", b=B), pattern=[[N, B], [P, TT]], base=0,
                         channel_multiplier=1, allow_small_or_imprecise_dtypes=True))
            for t in range(TWO):
                G_.memset(pad_rows[:, t, META + 4:META + 5], float(T)).then_inc(s["pads_ready"], 1)
            step(G_.iota(skip_u[:], pattern=[[0, 1]], base=T, channel_multiplier=0))
            settle()
            G_.memset(e2[:], 0.0).then_inc(s["pads_ready"], 1)
            pool.drain().then_inc(s["consts"], 1)

            def power(kind, n):
                pool.wait_ge(s[NORMED[kind]], n * B)
                pool.wait_ge(s[VE[kind]], n * 2 + 2)
                step(G_.tensor_tensor(rstd[kind][:], ve[kind][:], neg_half[:], ALU.pow))
                settle()
                G_.tensor_tensor(shift[kind][:], neg_mean[kind][:], rstd[kind][:], ALU.mult) \
                    .then_inc(s[SHIFTED[kind]], 1)

            def modulate(dst, one_plus, shift, done):
                for b in range(B):
                    part = dst[:, TT * b:TT * b + TT, 0:D]
                    step(G_.tensor_tensor(part, part, mod[:, b, one_plus:one_plus + 1, :].broadcast_to([P, TT, D]), ALU.mult))
                settle()
                for b in range(B):
                    part = dst[:, TT * b:TT * b + TT, 0:D]
                    last = G_.tensor_tensor(part, part, mod[:, b, shift:shift + 1, :].broadcast_to([P, TT, D]), ALU.add)
                last.then_inc(s[done], 1)

            def h_of(n):
                pool.wait_ge(s["xa_normed"], n * B + B)
                modulate(xa, CA, SA, "h_ready")

            def h_plus_ob(n):
                pool.wait_ge(s["h2_ready"], n)
                pool.wait_ge(s["h_ready"], n + 1)
                G_.tensor_tensor(hob[:], xa[:], ob_bc[:, None, :].broadcast_to([P, NT, D]), ALU.add) \
                    .then_inc(s["hob_ready"], 1)

            def scatter(g, tiles=WHOLE, done="scattered"):
                pool.wait_ge(s["pos_ready"], g + 1)
                pool.wait_ge(s["weights_ready"], g * 2 + 2)
                alone(pool)
                for t in range(tiles.start, tiles.stop):
                    for c_ in range(2):
                        G_.indirect_dma_start(slots, bass.IndirectOffsetOnAxis(ap=pos_u[:, c_ * NT + t:c_ * NT + t + 1], axis=0),
                                              h3[:, t, :], None).then_inc(s[done], 16)

            def residual(a):
                pool.wait_ge(s["xn2_ready"], a * B + B)
                step(G_.tensor_tensor(h2[:], h2[:], f2b_bc[:, None, :].broadcast_to([P, NT, D]), ALU.add))
                settle()
                for b in range(B):
                    part = h2[:, TT * b:TT * b + TT, :]
                    step(G_.tensor_tensor(part, part, mod[:, b, GA:GA + 1, :].broadcast_to([P, TT, D]), ALU.mult))
                settle()
                pool.wait_ge(s["xr_loaded"], a * 32 + 32)
                G_.tensor_tensor(res[:], res[:], h2[:], ALU.add).then_inc(s["res_ready"], 1)

            def load_up(e):
                G_.dma_start(raw_up[:], w1[e].rearrange("(k p) n -> p k n", p=P)).then_inc(s["up_loaded"], 16)

            def load_down(e):
                G_.dma_start(raw_down[:], w2[e].rearrange("(m p) n -> p m n", p=P)).then_inc(s["down_loaded"], 16)

            def iteration(i, A, F, G, NEXT, first=False):
                if G:
                    power(NORM_B, i - 2)
                if F:
                    residual(i - 1)
                if NEXT:
                    power(NORM_A, i + 1)
                    h_of(i + 1)
                if first:
                    power(NORM_1, 1)
                if A:
                    power(NORM_2, i)
                if NEXT and not first:
                    power(NORM_1, i + 1)
                if NEXT:
                    h_plus_ob(i + 1)
                if G and A:
                    scatter(i - 2)

            pool.wait_ge(s["dve_step"], 7)
            power(0, 0)
            power(1, 0)
            pool.wait_ge(s["wvo_mm"], 2)
            pool.wait_ge(s["ld_attn"], 16 * 5)
            h_plus_ob(0)
            pool.wait_ge(s["ld_ffn"], 16 * 6)
            pool.wait_ge(s["wprep"], 6)

            iteration(0, True, False, False, True, first=True)
            pool.wait_ge(s["mod_ready"], 3)
            iteration(1, True, True, False, True)
            start = steps[0]
            pool.wait_ge(s["prefilled"], 16 * E)
            with pool.Fori(2, NG - 1) as i:
                base[0] = (i - 2) * POOL_ROUND
                iteration(i, True, True, True, True)
            assert steps[0] - start == POOL_ROUND, steps[0] - start
            base[0] = (NG - 4) * POOL_ROUND
            iteration(NG - 1, True, True, True, False)

            iteration(NG, False, True, True, False)

            def last_power(b):
                g, tiles = HALVES[b]
                pool.wait_ge(s["h3_normed"], (NG - 1) * B)
                pool.wait_ge(s["ve_b_ready"], g * 2 + 2)
                step(G_.tensor_tensor(rstd[NORM_B][:, tiles], ve[NORM_B][:, tiles], neg_half[:, tiles], ALU.pow))
                settle()
                G_.tensor_tensor(shift[NORM_B][:, tiles], neg_mean[NORM_B][:, tiles], rstd[NORM_B][:, tiles], ALU.mult) \
                    .then_inc(s["shift_b_ready"], 1)

            scatter(NG - 2, HALVES[0][1])
            last_power(0)
            scatter(NG - 2, HALVES[1][1], "scattered_too")
            pool.wait_ge(s["act_split"], NG * MH)
            load_down(1)
            last_power(1)
            scatter(*HALVES[0])
            pool.wait_ge(s["gate_done"], NG + 1)
            load_up(1)
            scatter(*HALVES[1])
            pool.drain().then_inc(s["phase1_over"], 2)

            pool.wait_ge(s["phase1_over"], 5)
            pool.wait_ge(s["table_ready"], 1)

            def sum_rows(u, width):
                for t in range(width):
                    pool.wait_ge(s["y_ready"], u + t + 1)
                    alone(pool)
                    G_.indirect_dma_start(out.rearrange("b n d -> (b n) d"),
                                          bass.IndirectOffsetOnAxis(ap=tok_u[:, t:t + 1], axis=0),
                                          y[:, t, :], None, bounds_check=T - 1, oob_is_err=False,
                                          compute_op=ALU.add).then_inc(s["summed"], 16)

            pool.wait_ge(s["x2_stored"], 16 * B * NG)
            for t in range(2):
                G_.indirect_dma_start(out.rearrange("b n d -> (b n) d"),
                                      bass.IndirectOffsetOnAxis(ap=skip_u[:, 0:1], axis=0),
                                      pad_rows[:, t, 0:D], None, bounds_check=T - 1, oob_is_err=False,
                                      compute_op=ALU.add).then_inc(s["summed"], 16)
            pool.wait_ge(s["first_set"], 2)
            G_.memset(e2[:], 0.0).then_inc(s["down_ready"], 1)
            with pool.Fori(0, E // 2) as pair:
                for w in (0, 1):
                    e = pair * 2 + w
                    pairs, odd, units = expert(pool, e)
                    pool.wait_ge(s["down_loaded"], e * 16 + 16)
                    pool.wait_ge(s["l2_done"], units)
                    alone(pool)
                    o = 1 - w
                    G_.tensor_copy(down_hi[o][:, 0:MH // 2, :], raw_down[:, 0:MH // 2, :]) \
                        .then_inc(s["down_hi_ready"], 1)
                    pool.wait_ge(s["up_ready"], e + 2)
                    alone(pool)
                    load_up((e + 2) % E)
                    G_.tensor_copy(down_hi[o][:, MH // 2:MH, :], raw_down[:, MH // 2:MH, :]) \
                        .then_inc(s["down_hi_ready"], 1)
                    pool.wait_ge(s["down_hi_ready"], e * 2 + 2)
                    G_.tensor_tensor(down_lo[o][:], raw_down[:], down_hi[o][:].bitcast(F32), ALU.subtract) \
                        .then_inc(s["down_ready"], 1)
                    pool.wait_ge(s["down_ready"], e + 2)
                    alone(pool)
                    load_down((e + 2) % E)
                    pool.wait_ge(s["summed"], units * 16)
                    alone(pool)
                    tiles_of(pool, pairs, odd, units, lambda u, width, i: sum_rows(u, width))
            pool.wait_ge(s["up_loaded"], 16 * (E + 1))
            pool.wait_ge(s["down_loaded"], 16 * (E + 1))


OUT_SHAPE = (2, 2048, 256)


def kernel(**inputs):
    import concourse.bacc as bacc
    from concourse.bass_utils import run_bass_kernel_spmd

    def given(name):
        return np.asarray(inputs["L0_" + name])

    def columns(v, n=P):
        return v.reshape(-1, n).T

    layout = {
        "x": given("attn_x"),
        "c": given("c").reshape(2, 2, P).transpose(2, 1, 0),
        "wmod": given("wmod"),
        "wqk": np.concatenate([given("attn_q_w"), given("attn_k_w")], 0).T,
        "qk_b": columns(np.concatenate([given("attn_q_b"), given("attn_k_b")], 0)),
        "ln1_w": columns(given("attn_ln1_w")),
        "ln1_b": columns(given("attn_ln1_b")),
        "v_w": given("attn_v_w"),
        "v_b": columns(given("attn_v_b")),
        "o_w": given("attn_o_w").T,
        "o_b": given("attn_o_b"),
        "ln2_w": columns(given("attn_ln2_w")),
        "ln2_b": columns(given("attn_ln2_b")),
        "f1": given("attn_f1_w").T,
        "f1_b": columns(given("attn_f1_b")),
        "f2": given("attn_f2_w").T,
        "f2_b": given("attn_f2_b"),
        "gate": given("ffn_gate_w").T,
        "w1": given("ffn_w1").transpose(0, 2, 1),
        "b1": given("ffn_b1").reshape(8, 8, P).transpose(2, 0, 1),
        "w2": given("ffn_w2").transpose(0, 2, 1),
        "b2": given("ffn_b2"),
    }
    nc = bacc.Bacc("TRN2", target_bir_lowering=False, num_devices=1)
    arrays, args = {}, []
    for name, a in layout.items():
        a = np.ascontiguousarray(a)
        arrays["in_" + name] = a
        args.append(nc.dram_tensor("in_" + name, a.shape, mybir.dt.from_np(a.dtype), kind="ExternalInput").ap())
    out = nc.dram_tensor("out_0", OUT_SHAPE, F32, kind="ExternalOutput").ap()
    adaln_moe_program(nc, *args, out)
    r = run_bass_kernel_spmd(nc, [arrays], core_ids=[0])
    return r.results[0]["out_0"]
```
